# Optimizing a Trainium2 kernel written in Bass

```python
import numpy as np
import jax
import jax.numpy as jnp

def _softmax(x, axis=-1):
    return jax.nn.softmax(x, axis=axis)
def _gelu(x):
    return jax.nn.gelu(x, approximate=True)
def _silu(x):
    return jax.nn.silu(x)
def _sigmoid(x):
    return jax.nn.sigmoid(x)
def _layernorm(x, axis=-1, eps=1e-5):
    m = jnp.mean(x, axis=axis, keepdims=True)
    v = jnp.var(x, axis=axis, keepdims=True)
    return (x - m) / jnp.sqrt(v + eps)
def _scatter_add(tgt, idx, src, axis=0):
    return tgt.at[idx].add(src)
def _segment_sum(src, seg, n):
    return jax.ops.segment_sum(src, seg, n)

kernel_name = 'mk_dlrm_tower_d1_rec_812b6a'

def setup_inputs(seed: int = 0):
    np.random.seed(seed)
    _w = jnp.asarray
    def _rec_inputs():
        import jax
        import jax.numpy as jnp
        _tk = jax.random.key(seed)
        ids = jnp.stack([jax.random.randint(jax.random.fold_in(_tk, 200 + f), (1024,), 0, v, jnp.int32) for f, v in enumerate([1000, 1000000, 100000, 10000])], axis=1)
        tbl_0 = 0.05 * jax.random.normal(jax.random.fold_in(_tk, 500 + 0), (1000, 4), jnp.float32)
        tbl_1 = 0.05 * jax.random.normal(jax.random.fold_in(_tk, 500 + 1), (1000000, 4), jnp.float32)
        tbl_2 = 0.05 * jax.random.normal(jax.random.fold_in(_tk, 500 + 2), (100000, 4), jnp.float32)
        tbl_3 = 0.05 * jax.random.normal(jax.random.fold_in(_tk, 500 + 3), (10000, 4), jnp.float32)
        _rk = jax.random.fold_in(_tk, 7)
        r_x = 7.22013e-05 + 1.00017 * jax.random.normal(jax.random.fold_in(_rk, 101), (1024, 2048), jnp.float32)
        W_top1 = 0.0197642 * jax.random.normal(jax.random.fold_in(_tk, 801), (2560, 512), jnp.float32)
        W_top2 = 0.0441942 * jax.random.normal(jax.random.fold_in(_tk, 802), (512, 256), jnp.float32)
        W_top3 = 0.0625 * jax.random.normal(jax.random.fold_in(_tk, 803), (256, 1), jnp.float32)
        b_top1 = jnp.zeros((512,), jnp.float32)
        b_top2 = jnp.zeros((256,), jnp.float32)
        return r_x, ids, tbl_0, tbl_1, tbl_2, tbl_3, W_top1, b_top1, W_top2, b_top2, W_top3
    r_x, ids, tbl_0, tbl_1, tbl_2, tbl_3, W_top1, b_top1, W_top2, b_top2, W_top3 = _rec_inputs()
    def _L0_rec_setup():
        import jax, jax.numpy as jnp
        import numpy as np
        B, IN, HID, D, N, OUT = (4096, 2048, 2048, 512, 4, 512)
        H = 8
        HD = D // H

        def _ln(x, g, b):
            m = x.mean(-1, keepdims=True)
            v = ((x - m) ** 2).mean(-1, keepdims=True)
            return (x - m) / jnp.sqrt(v + 1e-05) * g + b
        key = jax.random.key(seed)
        ks = jax.random.split(key, 32)

        def nrm(k, shape, scale=0.02):
            return jax.random.normal(k, shape, jnp.float32) * scale
        inp = {}
        inp['x'] = jax.random.normal(ks[0], (B, IN), jnp.float32)
        inp['strength'] = jax.random.uniform(ks[1], (B, N, N), jnp.float32)
        for t, i in (('er', 2), ('ei', 4)):
            inp[t + '_W1'] = nrm(ks[i], (HID, IN))
            inp[t + '_b1'] = jnp.zeros((HID,), jnp.float32)
            inp[t + '_g1'] = jnp.ones((HID,), jnp.float32)
            inp[t + '_be1'] = jnp.zeros((HID,), jnp.float32)
            inp[t + '_W2'] = nrm(ks[i + 1], (N * D, HID))
            inp[t + '_b2'] = jnp.zeros((N * D,), jnp.float32)
        names = ['Wq_r', 'Wq_i', 'Wk_r', 'Wk_i', 'Wv_r', 'Wv_i', 'Wo_r', 'Wo_i']
        for j, nm in enumerate(names):
            inp[nm] = nrm(ks[6 + j], (D, D))
            inp['b' + nm[1:]] = jnp.zeros((D,), jnp.float32)
        inp['int_Wr'] = jnp.tile(jnp.eye(D, dtype=jnp.float32)[None], (N, 1, 1))
        inp['int_Wi'] = jnp.zeros((N, D, D), jnp.float32)
        inp['meas_Mr'] = nrm(ks[20], (OUT, D), 1.0 / np.sqrt(D))
        inp['meas_Mi'] = nrm(ks[21], (OUT, D), 1.0 / np.sqrt(D))
        inp['post_W'] = nrm(ks[22], (OUT, OUT))
        inp['post_b'] = jnp.zeros((OUT,), jnp.float32)
        inp['post_g'] = jnp.ones((OUT,), jnp.float32)
        inp['post_be'] = jnp.zeros((OUT,), jnp.float32)
        return inp
    _L0_rec_all = _L0_rec_setup()
    _L0_rec_in = {k: v for k, v in _L0_rec_all.items() if k in ('er_W1', 'er_b1', 'er_g1', 'er_be1', 'er_W2', 'er_b2', 'ei_W1', 'ei_b1', 'ei_g1', 'ei_be1', 'ei_W2', 'ei_b2', 'Wq_r', 'bq_r', 'Wq_i', 'bq_i', 'Wk_r', 'bk_r', 'Wk_i', 'bk_i', 'Wv_r', 'bv_r', 'Wv_i', 'bv_i', 'Wo_r', 'bo_r', 'Wo_i', 'bo_i', 'int_Wr', 'int_Wi', 'meas_Mr', 'meas_Mi', 'post_W', 'post_b', 'post_g', 'post_be', )}
    del _L0_rec_all

    return {
        "r_x": r_x,
        "ids": ids,
        "tbl_0": tbl_0,
        "tbl_1": tbl_1,
        "tbl_2": tbl_2,
        "tbl_3": tbl_3,
        "W_top1": W_top1,
        "b_top1": b_top1,
        "W_top2": W_top2,
        "b_top2": b_top2,
        "W_top3": W_top3,
        "L0_rec_er_W1": _L0_rec_in["er_W1"],
        "L0_rec_er_b1": _L0_rec_in["er_b1"],
        "L0_rec_er_g1": _L0_rec_in["er_g1"],
        "L0_rec_er_be1": _L0_rec_in["er_be1"],
        "L0_rec_er_W2": _L0_rec_in["er_W2"],
        "L0_rec_er_b2": _L0_rec_in["er_b2"],
        "L0_rec_ei_W1": _L0_rec_in["ei_W1"],
        "L0_rec_ei_b1": _L0_rec_in["ei_b1"],
        "L0_rec_ei_g1": _L0_rec_in["ei_g1"],
        "L0_rec_ei_be1": _L0_rec_in["ei_be1"],
        "L0_rec_ei_W2": _L0_rec_in["ei_W2"],
        "L0_rec_ei_b2": _L0_rec_in["ei_b2"],
        "L0_rec_Wq_r": _L0_rec_in["Wq_r"],
        "L0_rec_bq_r": _L0_rec_in["bq_r"],
        "L0_rec_Wq_i": _L0_rec_in["Wq_i"],
        "L0_rec_bq_i": _L0_rec_in["bq_i"],
        "L0_rec_Wk_r": _L0_rec_in["Wk_r"],
        "L0_rec_bk_r": _L0_rec_in["bk_r"],
        "L0_rec_Wk_i": _L0_rec_in["Wk_i"],
        "L0_rec_bk_i": _L0_rec_in["bk_i"],
        "L0_rec_Wv_r": _L0_rec_in["Wv_r"],
        "L0_rec_bv_r": _L0_rec_in["bv_r"],
        "L0_rec_Wv_i": _L0_rec_in["Wv_i"],
        "L0_rec_bv_i": _L0_rec_in["bv_i"],
        "L0_rec_Wo_r": _L0_rec_in["Wo_r"],
        "L0_rec_bo_r": _L0_rec_in["bo_r"],
        "L0_rec_Wo_i": _L0_rec_in["Wo_i"],
        "L0_rec_bo_i": _L0_rec_in["bo_i"],
        "L0_rec_int_Wr": _L0_rec_in["int_Wr"],
        "L0_rec_int_Wi": _L0_rec_in["int_Wi"],
        "L0_rec_meas_Mr": _L0_rec_in["meas_Mr"],
        "L0_rec_meas_Mi": _L0_rec_in["meas_Mi"],
        "L0_rec_post_W": _L0_rec_in["post_W"],
        "L0_rec_post_b": _L0_rec_in["post_b"],
        "L0_rec_post_g": _L0_rec_in["post_g"],
        "L0_rec_post_be": _L0_rec_in["post_be"],
    }

def reference(r_x, ids, tbl_0, tbl_1, tbl_2, tbl_3, W_top1, b_top1, W_top2, b_top2, W_top3, L0_rec_er_W1, L0_rec_er_b1, L0_rec_er_g1, L0_rec_er_be1, L0_rec_er_W2, L0_rec_er_b2, L0_rec_ei_W1, L0_rec_ei_b1, L0_rec_ei_g1, L0_rec_ei_be1, L0_rec_ei_W2, L0_rec_ei_b2, L0_rec_Wq_r, L0_rec_bq_r, L0_rec_Wq_i, L0_rec_bq_i, L0_rec_Wk_r, L0_rec_bk_r, L0_rec_Wk_i, L0_rec_bk_i, L0_rec_Wv_r, L0_rec_bv_r, L0_rec_Wv_i, L0_rec_bv_i, L0_rec_Wo_r, L0_rec_bo_r, L0_rec_Wo_i, L0_rec_bo_i, L0_rec_int_Wr, L0_rec_int_Wi, L0_rec_meas_Mr, L0_rec_meas_Mi, L0_rec_post_W, L0_rec_post_b, L0_rec_post_g, L0_rec_post_be):
    import jax
    import jax.numpy as jnp
    def _L0_rec_ref(x, strength, er_W1, er_b1, er_g1, er_be1, er_W2, er_b2, ei_W1, ei_b1, ei_g1, ei_be1, ei_W2, ei_b2, Wq_r, bq_r, Wq_i, bq_i, Wk_r, bk_r, Wk_i, bk_i, Wv_r, bv_r, Wv_i, bv_i, Wo_r, bo_r, Wo_i, bo_i, int_Wr, int_Wi, meas_Mr, meas_Mi, post_W, post_b, post_g, post_be):
        import jax, jax.numpy as jnp
        import numpy as np
        B, IN, HID, D, N, OUT = (4096, 2048, 2048, 512, 4, 512)
        H = 8
        HD = D // H

        def _ln(x, g, b):
            m = x.mean(-1, keepdims=True)
            v = ((x - m) ** 2).mean(-1, keepdims=True)
            return (x - m) / jnp.sqrt(v + 1e-05) * g + b
        Bsz = x.shape[0]

        def enc(W1, b1, g, be, W2, b2):
            h = jax.nn.gelu(_ln(x @ W1.T + b1, g, be), approximate=False)
            return (h @ W2.T + b2).reshape(Bsz, N, D)
        sr = enc(er_W1, er_b1, er_g1, er_be1, er_W2, er_b2)
        si = enc(ei_W1, ei_b1, ei_g1, ei_be1, ei_W2, ei_b2)

        def heads(t):
            return t.reshape(Bsz, N, H, HD).transpose(0, 2, 1, 3)
        qr = heads(sr @ Wq_r.T + bq_r)
        qi = heads(si @ Wq_i.T + bq_i)
        kr = heads(sr @ Wk_r.T + bk_r)
        ki = heads(si @ Wk_i.T + bk_i)
        vr = heads(sr @ Wv_r.T + bv_r)
        vi = heads(si @ Wv_i.T + bv_i)
        ar = jnp.einsum('bhnd,bhmd->bhnm', qr, kr) + jnp.einsum('bhnd,bhmd->bhnm', qi, ki)
        ai = jnp.einsum('bhnd,bhmd->bhnm', qi, kr) - jnp.einsum('bhnd,bhmd->bhnm', qr, ki)
        mag = jnp.sqrt(ar ** 2 + ai ** 2 + 1e-08) * HD ** (-0.5)
        w = jax.nn.softmax(mag, axis=-1)
        out_r = jnp.einsum('bhnm,bhmd->bhnd', w, vr).transpose(0, 2, 1, 3).reshape(Bsz, N, D)
        out_i = jnp.einsum('bhnm,bhmd->bhnd', w, vi).transpose(0, 2, 1, 3).reshape(Bsz, N, D)
        attn_r = out_r @ Wo_r.T + bo_r
        attn_i = out_i @ Wo_i.T + bo_i
        R = jnp.einsum('bnd,ned->bne', attn_r, int_Wr) - jnp.einsum('bnd,ned->bne', attn_i, int_Wi)
        I = jnp.einsum('bnd,ned->bne', attn_r, int_Wi) + jnp.einsum('bnd,ned->bne', attn_i, int_Wr)
        Ri, Ii = (R[:, :, None, :], I[:, :, None, :])
        Rj, Ij = (R[:, None, :, :], I[:, None, :, :])
        phase = jnp.arctan2(Ii * Rj - Ri * Ij, Ri * Rj + Ii * Ij)
        f = jnp.cos(phase) * strength[..., None]
        sup_r = jnp.einsum('bijd,bjd->bd', f, R)
        sup_i = jnp.einsum('bijd,bjd->bd', f, I)
        norm = jnp.sqrt(jnp.sum(sup_r ** 2 + sup_i ** 2, axis=-1, keepdims=True) + 1e-08)
        sup_r = sup_r / norm
        sup_i = sup_i / norm
        mr = sup_r @ meas_Mr.T - sup_i @ meas_Mi.T
        mi = sup_r @ meas_Mi.T + sup_i @ meas_Mr.T
        amp = jnp.sqrt(mr ** 2 + mi ** 2)
        out = jax.nn.gelu(_ln(amp @ post_W.T + post_b, post_g, post_be), approximate=False)
        return out

    e = jnp.stack([tbl_0[ids[:, 0]], tbl_1[ids[:, 1]], tbl_2[ids[:, 2]], tbl_3[ids[:, 3]]], axis=1)
    z = _L0_rec_ref(r_x, e, L0_rec_er_W1, L0_rec_er_b1, L0_rec_er_g1, L0_rec_er_be1, L0_rec_er_W2, L0_rec_er_b2, L0_rec_ei_W1, L0_rec_ei_b1, L0_rec_ei_g1, L0_rec_ei_be1, L0_rec_ei_W2, L0_rec_ei_b2, L0_rec_Wq_r, L0_rec_bq_r, L0_rec_Wq_i, L0_rec_bq_i, L0_rec_Wk_r, L0_rec_bk_r, L0_rec_Wk_i, L0_rec_bk_i, L0_rec_Wv_r, L0_rec_bv_r, L0_rec_Wv_i, L0_rec_bv_i, L0_rec_Wo_r, L0_rec_bo_r, L0_rec_Wo_i, L0_rec_bo_i, L0_rec_int_Wr, L0_rec_int_Wi, L0_rec_meas_Mr, L0_rec_meas_Mi, L0_rec_post_W, L0_rec_post_b, L0_rec_post_g, L0_rec_post_be)
    z = z.reshape(z.shape[0], -1)
    h = jnp.concatenate([z, r_x], axis=1)
    h = jnp.maximum(h @ W_top1 + b_top1, 0.0)
    h = jnp.maximum(h @ W_top2 + b_top2, 0.0)
    y = h @ W_top3
    return y


_drawn_inputs = setup_inputs


def setup_inputs(seed=0):
    import zlib

    import numpy as np

    out = dict(_drawn_inputs(seed))
    spreads = {'b_top1': (0.0, 0.1),
     'b_top2': (0.0, 0.1),
     'L0_rec_er_b1': (0.0, 0.8),
     'L0_rec_er_g1': (1.0, 0.6),
     'L0_rec_er_be1': (0.0, 0.8),
     'L0_rec_er_b2': (0.0, 0.8),
     'L0_rec_ei_b1': (0.0, 0.8),
     'L0_rec_ei_g1': (1.0, 0.6),
     'L0_rec_ei_be1': (0.0, 0.8),
     'L0_rec_ei_b2': (0.0, 0.8),
     'L0_rec_bq_r': (0.0, 0.8),
     'L0_rec_bq_i': (0.0, 0.8),
     'L0_rec_bk_r': (0.0, 0.8),
     'L0_rec_bk_i': (0.0, 0.8),
     'L0_rec_bv_r': (0.0, 0.1),
     'L0_rec_bv_i': (0.0, 0.1),
     'L0_rec_bo_r': (0.0, 0.1),
     'L0_rec_bo_i': (0.0, 0.1),
     'L0_rec_int_Wi': (0.0, 0.1),
     'L0_rec_post_b': (0.0, 0.1),
     'L0_rec_post_g': (1.0, 0.2),
     'L0_rec_post_be': (0.0, 0.1)}
    factors = {'L0_rec_Wq_r': 8.0, 'L0_rec_Wq_i': 8.0, 'L0_rec_Wk_r': 8.0, 'L0_rec_Wk_i': 8.0}
    for name, (base, spread) in spreads.items():
        noise = np.random.default_rng([zlib.crc32(name.encode()), seed]).standard_normal(out[name].shape)
        drawn = base * np.exp(spread * noise) if base else spread * noise
        out[name] = jnp.asarray(drawn.astype(out[name].dtype))
    for name, factor in factors.items():
        out[name] = (out[name] * factor).astype(out[name].dtype)
    return out
```

```python
from contextlib import ExitStack

import concourse.bass as bass
from concourse import mybir

F32 = mybir.dt.float32
F32R = mybir.dt.float32r
ALU = mybir.AluOpType
ACT = mybir.ActivationFunctionType
AX_X = mybir.AxisListType.X

P = 128
B, IN, HID, D, N, H, OUT = 1024, 2048, 2048, 512, 4, 8, 512
HD = D // H
HB = 512
HALVES = B // HB
KT = IN // P
CH = B // P
DT = D // P
EPS = 1e-5
CREDIT = 2


def encoders(nc, sems, x_t, enc_w, enc_bias, ln_gb, s_dram, hx_dram):
    L1 = HID // P
    XP = 512 // P
    L2 = N * D // P
    TILES = 2 * L1 + XP + 2 * L2
    XPIECES = KT // 2
    PIECE = KT // 2 * P
    PIECES = XPIECES + 2 * TILES
    STORES = (XP + 2 * L2) // 2

    with ExitStack() as ctx:
        def sb(name, shape, dt=F32):
            return ctx.enter_context(nc.sbuf_tensor(name, shape, dt))

        def sem(name):
            return sems.enter_context(nc.semaphore(name))

        act_hi = sb("act_hi", [P, KT, HB], F32R)
        act_lo = sb("act_lo", [P, KT, HB], F32R)
        y_r_at = nc.sbuf_base
        y_r = sb("y_r", [P, KT, HB])
        hid_hi = nc.alloc_sbuf_tensor_at("hid_hi", [P, KT, HB], F32R, offset=y_r_at)
        hid_lo = sb("hid_lo", [P, KT, HB], F32R)
        y_i = sb("y_i", [P, KT, HB])
        raw = sb("raw", [P, 2, PIECE])
        w_hi = sb("w_hi", [P, 2, PIECE], F32R)
        w_lo = sb("w_lo", [P, 2, PIECE], F32R)
        total = sb("total", [P, HB])
        sq_total = sb("sq_total", [P, HB])
        mean = sb("mean", [P, HB])
        rstd = sb("rstd", [P, HB])
        ln_tmp = sb("ln_tmp", [P, 2, HB])
        stage = sb("stage", [P, 2, 2, HB])
        bias = sb("bias", [P, TILES])
        gb = sb("gb", [P, 2, 2, KT])
        over_n = sb("over_n", [P, P])
        eps = sb("eps", [P, 1])
        acc = [ctx.enter_context(nc.psum_tensor(f"acc{u}", [P, HB], F32)) for u in range(2)]
        stat = ctx.enter_context(nc.psum_tensor("stat", [P, HB], F32))

        loaded = [sem(f"loaded{u}") for u in range(2)]
        hi_done = sem("hi_done")
        lo_done = sem("lo_done")
        half_done = sem("half_done")
        tile_done = sem("tile_done")
        evacuated = sem("evacuated")
        added = sem("added")
        cleared = sem("cleared")
        stat_done = sem("stat_done")
        mean_ready = sem("mean_ready")
        centered = sem("centered")
        squared = sem("squared")
        sq_added = sem("sq_added")
        root_done = sem("root_done")
        rstd_ready = sem("rstd_ready")
        scaled = sem("scaled")
        gelu_done = sem("gelu_done")
        h_hi = sem("h_hi")
        h_lo = sem("h_lo")
        hi_staged = sem("hi_staged")
        stored = [sem(f"stored{u}") for u in range(2)]
        consts_in = sem("consts_in")
        consts_set = sem("consts_set")

        block = ctx.enter_context(nc.Block())

        R1, I1, TX, R2, I2 = (0, L1), (L1, L1), (2 * L1, XP), (2 * L1 + XP, L2), (2 * L1 + XP + L2, L2)

        @block.sync
        def _(sp):
            sp.dma_start(bias[:, :], enc_bias).then_inc(consts_in, 16)
            sp.dma_start(gb[:, :, :, :], ln_gb).then_inc(consts_in, 16)
            for u in range(2):
                sp.sem_inc(stored[u], 32)

            def load(h, piece, u, src):
                sp.wait_ge(hi_done, h * PIECES + piece + 1)
                sp.wait_ge(lo_done, h * PIECES + piece + 1)
                sp.dma_start(raw[:, u, :], src).then_inc(loaded[u], 16)

            def load_tile(h, t):
                for u in range(2):
                    load(h, XPIECES + 2 * t + u, u, enc_w[bass.ds(2 * t + u, 1)].rearrange("a p n -> p (a n)"))

            def store(h, stage_, t, u):
                first, _ = stage_
                sp.wait_ge(evacuated, h * TILES + first + t + 1 + CREDIT)
                if stage_ is TX:
                    for v in range(2):
                        sp.dma_start(hx_dram[bass.ds(h, 1), :, bass.ds(t, 1), v * 256:(v + 1) * 256]
                                     .rearrange("a p t n -> p (a t n)"),
                                     stage[:, u, 0, v * 256:(v + 1) * 256]).then_inc(stored[u], 16)
                else:
                    ri = 0 if stage_ is R2 else 1
                    for v in range(2):
                        sp.dma_start(s_dram[ri, v, bass.ds(h * 4, 4), :, bass.ds(t, 1), :]
                                     .rearrange("c p t b -> p c (t b)"),
                                     stage[:, u, v, :].rearrange("p (c b) -> p c b", c=4)).then_inc(stored[u], 16)

            with sp.Fori(0, HALVES) as h:
                with sp.Fori(0, XPIECES // 2) as q:
                    for u in range(2):
                        load(h, 2 * q + u, u, x_t[bass.ds(h, 1), bass.ds(2 * q + u, 1)].rearrange("a b p n -> p (a b n)"))
                with sp.Fori(0, L1) as i:
                    load_tile(h, 2 * i)
                    load_tile(h, 2 * i + 1)
                before = None
                for st in (TX, R2, I2):
                    first, tiles = st
                    load_tile(h, first)
                    load_tile(h, first + 1)
                    if before:
                        for u in range(2):
                            store(h, before, before[1] - 2 + u, u)
                    with sp.Fori(1, tiles // 2) as i:
                        load_tile(h, first + 2 * i)
                        load_tile(h, first + 2 * i + 1)
                        for u in range(2):
                            store(h, st, 2 * i - 2 + u, u)
                    before = st
                for u in range(2):
                    store(h, I2, L2 - 2 + u, u)
            for u in range(2):
                sp.wait_ge(stored[u], 32 * (HALVES * STORES + 1))

        @block.gpsimd
        def _(pool):
            pool.sem_inc(lo_done, CREDIT)
            pool.memset(over_n[:, :], 1.0 / HID).then_inc(consts_set, 1)
            pool.memset(eps[:, :], EPS).then_inc(consts_set, 1)

            def low(h, piece, n, u, dst, hi):
                pool.wait_ge(loaded[u], 16 * (h * (PIECES // 2) + n + 1))
                pool.wait_ge(hi_done, h * PIECES + piece + 1 + CREDIT)
                pool.tensor_tensor(dst, raw[:, u, :], hi.bitcast(F32), ALU.subtract).then_inc(lo_done, 1)

            with pool.Fori(0, HALVES) as h:
                with pool.Fori(0, XPIECES // 2) as q:
                    for u in range(2):
                        low(h, 2 * q + u, q, u,
                            act_lo[:, bass.ds(2 * (2 * q + u), 2), :].rearrange("p a b -> p (a b)"),
                            act_hi[:, bass.ds(2 * (2 * q + u), 2), :].rearrange("p a b -> p (a b)"))
                with pool.Fori(0, TILES) as t:
                    for u in range(2):
                        pool.wait_ge((half_done, tile_done)[u], h * TILES + t + CREDIT)
                        low(h, XPIECES + 2 * t + u, XPIECES // 2 + t, u, w_lo[:, u, :], w_hi[:, u, :])

        @block.scalar
        def _(act):
            act.sem_inc(hi_done, CREDIT)

            def high(h, n, u, dst):
                act.wait_ge(consts_in, 32)
                act.wait_ge(loaded[u], 16 * (h * (PIECES // 2) + n + 1))
                act.activation(dst, raw[:, u, :], ACT.Copy).then_inc(hi_done, 1)

            def high_tile(h, t):
                for u in range(2):
                    act.wait_ge((half_done, tile_done)[u], h * TILES + t + CREDIT)
                    high(h, XPIECES // 2 + t, u, w_hi[:, u, :])

            def square(h, ln, y, j, u):
                at = h * 2 * KT + ln * KT + j
                act.wait_ge(centered, at + 1)
                act.wait_ge(sq_added, at + 1)
                act.wait_ge(consts_in, 32)
                act.activation(ln_tmp[:, u, :], y[:, bass.ds(j, 1), :].rearrange("p a b -> p (a b)"),
                               ACT.Square).then_inc(squared, 1)

            def gelu(h, ln, y, hi, j, u):
                at = h * 2 * KT + ln * KT + j
                act.wait_ge(scaled, at + 1)
                act.wait_ge(h_lo, at + 1)
                act.wait_ge(consts_in, 32)
                act.activation(ln_tmp[:, u, :], y[:, bass.ds(j, 1), :].rearrange("p a b -> p (a b)"), ACT.Gelu,
                               scale=gb[:, ln, 0, bass.ds(j, 1)], bias=gb[:, ln, 1, bass.ds(j, 1)]).then_inc(gelu_done, 1)
                act.wait_ge(consts_in, 32)
                act.wait_ge(gelu_done, at + 1)
                act.activation(hi[:, bass.ds(j, 1), :].rearrange("p a b -> p (a b)"), ln_tmp[:, u, :],
                               ACT.Copy).then_inc(h_hi, 1)

            def with_norm(h, ln, first, y, hi):
                for u in range(2):
                    high_tile(h, first + u)
                with act.Fori(0, 4) as i:
                    for v in range(2):
                        high_tile(h, first + 2 + 2 * i + v)
                        for u in range(2):
                            square(h, ln, y, 4 * i + 2 * v + u, u)
                for u in range(2):
                    high_tile(h, first + 10 + u)
                act.wait_ge(stat_done, 4 * h + 2 * ln + 2)
                act.activation(rstd[:, :], stat[:, :], ACT.Sqrt, bias=eps[:, 0:1]).then_inc(root_done, 1)
                with act.Fori(0, 2) as i:
                    for v in range(2):
                        high_tile(h, first + 12 + 2 * i + v)
                        for u in range(4):
                            gelu(h, ln, y, hi, 8 * i + 4 * v + u, u % 2)

            act.wait_ge(consts_in, 32)
            act.wait_ge(consts_set, 2)
            with act.Fori(0, HALVES) as h:
                act.wait_ge(consts_in, 32)
                act.wait_ge(tile_done, h * TILES + CREDIT)
                with act.Fori(0, XPIECES // 2) as q:
                    for u in range(2):
                        high(h, q, u, act_hi[:, bass.ds(2 * (2 * q + u), 2), :].rearrange("p a b -> p (a b)"))
                with act.Fori(0, L1) as t:
                    high_tile(h, t)
                with_norm(h, 0, I1[0], y_r, hid_hi)
                with act.Fori(0, XP) as t:
                    high_tile(h, TX[0] + t)
                with_norm(h, 1, R2[0], y_i, act_hi)
                with act.Fori(0, L2) as t:
                    high_tile(h, I2[0] + t)

        @block.vector
        def _(dve):
            dve.sem_inc(evacuated, CREDIT)
            dve.sem_inc(sq_added, CREDIT)
            dve.sem_inc(h_lo, CREDIT)
            dve.sem_inc(added, 1)

            def tile2(x, j):
                return x[:, bass.ds(j, 1), :].rearrange("p a b -> p (a b)")

            def evacuate_first(h, st, t, u, ln, y):
                first, _ = st
                dve.wait_ge(cleared, 3 * h + ln + 1)
                dve.wait_ge(tile_done, h * TILES + first + t + 1 + CREDIT)
                dve.tensor_scalar(tile2(y, t), acc[u][:, :], bias[:, bass.ds(first + t, 1)], None,
                                  ALU.add).then_inc(evacuated, 1)
                dve.wait_ge(evacuated, h * TILES + first + t + 1 + CREDIT)
                dve.wait_ge(added, h * 2 * KT + ln * KT + t + 1)
                dve.tensor_tensor(total[:, :], total[:, :], tile2(y, t), ALU.add).then_inc(added, 1)

            def evacuate_second(h, st, t, half_t, u, n0):
                first, _ = st
                dve.wait_ge(tile_done, h * TILES + first + t + 1 + CREDIT)
                dve.wait_ge(stored[u], 32 * (h * STORES + n0 + half_t + 1))
                hi = stage[:, u, 0, :]
                b = bias[:, bass.ds(first + t, 1)]
                dve.tensor_scalar(hi.bitcast(F32R), acc[u][:, :], b, None, ALU.add).then_inc(hi_staged, 1)
                dve.wait_ge(hi_staged, h * 2 * L2 + (first - R2[0]) + t + 1)
                dve.scalar_tensor_tensor(out=stage[:, u, 1, :].bitcast(F32R), in0=acc[u][:, :], scalar=b, in1=hi,
                                         op0=ALU.add, op1=ALU.subtract).then_inc(evacuated, 1)

            def with_norm(h, ln, y, hi, lo, evac):
                s = 4 * h + 2 * ln
                dve.wait_ge(stat_done, s + 1)
                dve.tensor_copy(mean[:, :], stat[:, :]).then_inc(mean_ready, 1)
                dve.memset(total[:, :], 0.0)
                dve.memset(sq_total[:, :], 0.0).then_inc(cleared, 1)
                dve.wait_ge(mean_ready, 2 * h + ln + 1)
                dve.wait_ge(cleared, 3 * h + ln + 2)
                evac(0, 0)
                evac(0, 1)
                at = h * 2 * KT + ln * KT
                with dve.Fori(0, 4) as i:
                    for u in range(4):
                        j = 4 * i + u
                        dve.tensor_tensor(tile2(y, j), tile2(y, j), mean[:, :], ALU.subtract).then_inc(centered, 1)
                    for u in range(4):
                        j = 4 * i + u
                        dve.wait_ge(squared, at + j + 1)
                        dve.wait_ge(sq_added, at + j + CREDIT)
                        dve.tensor_tensor(sq_total[:, :], sq_total[:, :], ln_tmp[:, u % 2, :], ALU.add).then_inc(sq_added, 1)
                    evac(i + 1, 0)
                    evac(i + 1, 1)
                dve.wait_ge(root_done, 2 * h + ln + 1)
                dve.reciprocal(rstd[:, :], rstd[:, :]).then_inc(rstd_ready, 1)
                evac(5, 0)
                evac(5, 1)
                dve.wait_ge(consts_in, 32)
                dve.wait_ge(rstd_ready, 2 * h + ln + 1)
                with dve.Fori(0, 2) as i:
                    for u in range(8):
                        j = 8 * i + u
                        dve.tensor_tensor(tile2(y, j), tile2(y, j), rstd[:, :], ALU.mult).then_inc(scaled, 1)
                    for v in range(2):
                        for u in range(4):
                            j = 8 * i + 4 * v + u
                            dve.wait_ge(h_hi, at + j + 1)
                            dve.tensor_tensor(tile2(lo, j), ln_tmp[:, u % 2, :], tile2(hi, j).bitcast(F32),
                                              ALU.subtract).then_inc(h_lo, 1)
                        evac(i + 6, v)

            dve.wait_ge(consts_in, 32)
            with dve.Fori(0, HALVES) as h:
                dve.memset(total[:, :], 0.0).then_inc(cleared, 1)
                with dve.Fori(0, L1 // 2) as i:
                    for u in range(2):
                        evacuate_first(h, R1, 2 * i + u, u, 0, y_r)
                with_norm(h, 0, y_r, hid_hi, hid_lo, lambda i, u: evacuate_first(h, I1, 2 * i + u, u, 1, y_i))
                with dve.Fori(0, XP // 2) as i:
                    for u in range(2):
                        dve.wait_ge(tile_done, h * TILES + TX[0] + 2 * i + u + 1 + CREDIT)
                        dve.wait_ge(stored[u], 32 * (h * STORES + i + 1))
                        dve.tensor_scalar(stage[:, u, 0, :], acc[u][:, :], bias[:, bass.ds(TX[0] + 2 * i + u, 1)], None,
                                          ALU.add).then_inc(evacuated, 1)
                with_norm(h, 1, y_i, act_hi, act_lo,
                          lambda i, u: evacuate_second(h, R2, 2 * i + u, i, u, XP // 2))
                with dve.Fori(0, L2 // 2) as i:
                    for u in range(2):
                        evacuate_second(h, I2, 2 * i + u, i, u, XP // 2 + L2 // 2)

        @block.tensor
        def _(pe):
            pe.sem_inc(half_done, CREDIT)
            pe.sem_inc(tile_done, CREDIT)

            def multiply(h, t, u, hi, lo):
                pe.wait_ge(evacuated, h * TILES + t + 1)
                for q in range(2):
                    piece = h * PIECES + XPIECES + 2 * t + q
                    pe.wait_ge(hi_done, piece + 1 + CREDIT)
                    pe.wait_ge(lo_done, piece + 1 + CREDIT)
                    for k in range(KT // 2):
                        kk = q * (KT // 2) + k
                        wh, wl = w_hi[:, q, k * P:(k + 1) * P], w_lo[:, q, k * P:(k + 1) * P]
                        pe.matmul(acc[u][:, :], wh, hi[:, kk, :], start=kk == 0, stop=False)
                        pe.matmul(acc[u][:, :], wh, lo[:, kk, :], start=False, stop=False)
                        last = pe.matmul(acc[u][:, :], wl, hi[:, kk, :], start=False, stop=kk == KT - 1)
                    last.then_inc((half_done, tile_done)[q], 1)

            def statistic(src):
                return pe.matmul(stat[:, :], over_n[:, :], src[:, :], start=True, stop=True)

            def with_norm(h, ln, first, hi, lo):
                at = h * 2 * KT + ln * KT
                multiply(h, first, 0, hi, lo)
                pe.wait_ge(added, at + KT + 1)
                statistic(total).then_inc(stat_done, 1)
                multiply(h, first + 1, 1, hi, lo)
                with pe.Fori(1, 5) as i:
                    for u in range(2):
                        multiply(h, first + 2 * i + u, u, hi, lo)
                pe.wait_ge(sq_added, at + KT + CREDIT)
                statistic(sq_total).then_inc(stat_done, 1)
                with pe.Fori(5, 8) as i:
                    for u in range(2):
                        multiply(h, first + 2 * i + u, u, hi, lo)

            pe.wait_ge(consts_set, 2)
            with pe.Fori(0, HALVES) as h:
                with pe.Fori(0, L1 // 2) as i:
                    for u in range(2):
                        multiply(h, 2 * i + u, u, act_hi, act_lo)
                with_norm(h, 0, I1[0], act_hi, act_lo)
                with pe.Fori(0, XP // 2) as i:
                    for u in range(2):
                        multiply(h, TX[0] + 2 * i + u, u, act_hi, act_lo)
                pe.wait_ge(h_lo, h * 2 * KT + KT + CREDIT)
                with_norm(h, 1, R2[0], hid_hi, hid_lo)
                pe.wait_ge(consts_set, 2)
                pe.wait_ge(h_lo, h * 2 * KT + 2 * KT + CREDIT)
                with pe.Fori(0, L2 // 2) as i:
                    for u in range(2):
                        multiply(h, I2[0] + 2 * i + u, u, act_hi, act_lo)


G = 4
GB = P // G
T = N * P
HH = H // 2


def attention(nc, sems, qkv_w, qk_bias, v_bias, s_dram, o_dram):
    with ExitStack() as ctx:
        def sb(name, shape, dt=F32):
            return ctx.enter_context(nc.sbuf_tensor(name, shape, dt))

        def sem(name):
            return sems.enter_context(nc.semaphore(name))

        def ps(name, shape):
            return ctx.enter_context(nc.psum_tensor(name, shape, F32))

        wt_hi = sb("wt_hi", [P, 6, DT, D], F32R)
        wt_lo = sb("wt_lo", [P, 6, DT, D], F32R)
        s_hi = sb("s_hi", [P, 2, DT, T], F32R)
        s_lo = sb("s_lo", [P, 2, DT, T], F32R)
        q2 = sb("q2", [P, HH, 2, T])
        ks = sb("ks", [P, HH, T])
        v = sb("v", [P, G, H, 2, HD])
        pt = sb("pt", [P, G * HH, P])
        o_out = sb("o_out", [P, 2, HH, T])
        masked = sb("masked", [P, 2, 16, GB])
        vb = sb("vb", [P, 2, D])
        qkb = sb("qkb", [P, 4, DT])
        neg_b = sb("neg_b", [P, DT])
        ident = sb("ident", [P, P])
        mask = sb("mask", [P, GB])
        sc = sb("sc", [P, G, 2, 2, 2, N])
        sc_sq = sb("sc_sq", [P, G * HH, 2, N])
        mag2 = sb("mag2", [P, G * HH, N])
        mag = sb("mag", [P, G * HH * N])
        top = sb("top", [G * HH * N, GB])
        ex = sb("ex", [G * HH * N, N, GB])
        den = sb("den", [G * HH * N, GB])
        w_t = sb("w_t", [P, G * HH * N])
        tiny = sb("tiny", [P, 1])
        proj = [ps(f"proj{u}", [P, T]) for u in range(2)]
        scp = [ps(f"scp{u}", [P, T]) for u in range(2)]
        avp = [ps(f"avp{u}", [P, T]) for u in range(2)]
        tp = ps("tp", [P, T])
        R = G * HH * N
        raw = v[:, :, :, :, :].rearrange("p g h r d -> p (g h r d)").rearrange("p (u n) -> p u n", u=2)

        w_in = [sem(f"w_in{u}") for u in range(2)]
        w_hi_done = sem("w_hi_done")
        w_lo_done = sem("w_lo_done")
        small_in = sem("small_in")
        neg_set = sem("neg_set")
        s_in = sem("s_in")
        proj_done = sem("proj_done")
        even_out = sem("even_out")
        odd_out = sem("odd_out")
        score_done = sem("score_done")
        score_masked = sem("score_masked")
        score_out = sem("score_out")
        squared2 = sem("squared2")
        mag2_set = sem("mag2_set")
        mag_set = sem("mag_set")
        mag_turned = sem("mag_turned")
        top_set = sem("top_set")
        less_top = sem("less_top")
        exp_set = sem("exp_set")
        den_set = sem("den_set")
        den_inv = sem("den_inv")
        prob_set = sem("prob_set")
        prob_turned = sem("prob_turned")
        w_t_set = sem("w_t_set")
        pt_set = sem("pt_set")
        av_done = sem("av_done")
        o_set = sem("o_set")
        o_stored = [sem(f"o_stored{u}") for u in range(2)]
        set_up = sem("set_up")

        block = ctx.enter_context(nc.Block())
        QK0, V0, QK1, PER = 0, 8, 16, 24
        qk_at = (QK0, QK1)

        @block.sync
        def _(sp):
            sp.dma_start(qkb[:, :, :], qk_bias).then_inc(small_in, 16)
            sp.dma_start(vb[:, :, :], v_bias.partition_broadcast(P)).then_inc(small_in, 16)
            for u in range(2):
                sp.sem_inc(o_stored[u], 64)
            for m in range(6):
                if m >= 2:
                    sp.wait_ge(w_hi_done, m - 1)
                    sp.wait_ge(w_lo_done, m - 1)
                sp.dma_start(raw[:, m % 2, :], qkv_w[m]).then_inc(w_in[m % 2], 16)

            def load_s(c):
                for r in range(2):
                    for x, t in ((0, s_hi), (1, s_lo)):
                        sp.dma_start(t[:, r].rearrange("p d t -> p (d t)").bitcast(F32),
                                     s_dram[r, x, bass.ds(c, 1)].rearrange("c p t b -> p (c t b)")).then_inc(s_in, 16)

            def store_o(c, hh):
                sp.wait_ge(o_set, 8 * c + 4 * hh + 4 + CREDIT)
                for r in range(2):
                    for par in range(2):
                        sp.dma_start(o_dram[r, hh, bass.ds(c, 1), par * HD:(par + 1) * HD].rearrange("c p d t -> p (c d) t"),
                                     o_out[r * HD:(r + 1) * HD, hh].rearrange("p (d a) t -> p a d t", a=2)[:, par]
                                     ).then_inc(o_stored[hh], 16)

            load_s(0)
            with sp.Fori(1, CH) as c:
                sp.wait_ge(proj_done, PER * c)
                load_s(c)
                store_o(c - 1, 0)
                store_o(c - 1, 1)
            store_o(CH - 1, 0)
            store_o(CH - 1, 1)
            for u in range(2):
                sp.wait_ge(o_stored[u], 64 * (CH + 1))

        @block.gpsimd
        def _(pool):
            pool.memset(tiny[:, :], 1e-8)
            pool.memset(ident[:, :], 0.0).then_inc(set_up, 1)
            pool.wait_ge(set_up, 1)
            pool.affine_select(out=ident[:, :], in_=ident[:, :], compare_op=ALU.not_equal, fill=1.0,
                               base=0, pattern=[[-1, P]], channel_multiplier=1).then_inc(set_up, 1)
            for m in range(6):
                pool.wait_ge(w_in[m % 2], 16 * (m // 2 + 1))
                pool.wait_ge(w_hi_done, m + 1)
                pool.tensor_tensor(wt_lo[:, m].rearrange("p k n -> p (k n)"), raw[:, m % 2, :],
                                   wt_hi[:, m].rearrange("p k n -> p (k n)").bitcast(F32), ALU.subtract).then_inc(w_lo_done, 1)

            def expand(c, hh):
                pool.wait_ge(av_done, 8 * c + 4 * hh)
                pool.wait_ge(w_t_set, 2 * c + hh + 1)
                pool.tensor_tensor(pt[:, :, :].rearrange("p a (n b) -> p (a n) b", b=GB),
                                   w_t[:, :].unsqueeze(2).broadcast_to([P, R, GB]),
                                   mask[:, :].unsqueeze(1).broadcast_to([P, R, GB]), ALU.mult).then_inc(pt_set, 1)

            pool.wait_ge(set_up, 3)
            expand(0, 0)
            expand(0, 1)
            with pool.Fori(1, CH) as c:
                expand(c, 0)
                expand(c, 1)

        @block.scalar
        def _(act):
            act.sem_inc(even_out, CREDIT)
            act.sem_inc(o_set, CREDIT)
            for m in range(6):
                act.wait_ge(w_in[m % 2], 16 * (m // 2 + 1))
                act.activation(wt_hi[:, m].rearrange("p k n -> p (k n)"), raw[:, m % 2, :], ACT.Copy).then_inc(w_hi_done, 1)
            act.wait_ge(small_in, 32)
            act.activation(neg_b[:, :], qkb[:, 0, :], ACT.Copy, scale=-1.0).then_inc(neg_set, 1)
            act.wait_ge(neg_set, 1)
            act.wait_ge(set_up, 3)

            def take_even(c, hh, i):
                j, kind = i // 4, i % 4
                act.wait_ge(proj_done, PER * c + qk_at[hh] + i + 1)
                src = proj[i % 2][0:HD, :].rearrange("p (t g) -> p g t", g=G)
                b = qkb[0:HD, kind, 2 * hh + j:2 * hh + j + 1]

                def to(x):
                    return x.rearrange("p (g t) -> p g t", g=G)

                h = 2 * j
                if kind == 0:
                    act.activation(to(q2[0:HD, h, 0]), src, ACT.Identity, bias=b)
                    act.activation(to(q2[HD:P, h, 1]), src, ACT.Identity, scale=-1.0,
                                   bias=neg_b[0:HD, 2 * hh + j:2 * hh + j + 1]).then_inc(even_out, 1)
                elif kind == 1:
                    act.activation(to(q2[HD:P, h, 0]), src, ACT.Identity, bias=b)
                    act.activation(to(q2[0:HD, h, 1]), src, ACT.Identity, bias=b).then_inc(even_out, 1)
                else:
                    row = (kind - 2) * HD
                    act.activation(to(ks[row:row + HD, h]), src, ACT.Identity, bias=b).then_inc(even_out, 1)

            def qk(c, hh, n=None):
                if n is not None:
                    act.wait_ge(mag2_set, n + 1)
                    act.activation(mag[:, :], mag2[:, :, :].rearrange("p a n -> p (a n)"), ACT.Sqrt,
                                   bias=tiny[:, 0:1]).then_inc(mag_set, 1)
                for i in range(8):
                    take_even(c, hh, i)
                    if i == 1 and n is not None:
                        exponent(n)

            def exponent(n):
                act.wait_ge(less_top, n + 1)
                act.activation(ex[:, :, :], ex[:, :, :], ACT.Exp, scale=HD ** -0.5).then_inc(exp_set, 1)

            def take_o(c, hh, g):
                act.wait_ge(av_done, 8 * c + 4 * hh + g + 1)
                if g == 0:
                    act.wait_ge(o_stored[hh], 64 * (c + 1))
                act.activation(o_out[:, hh, :, g:T:G], avp[g % 2][:, :].rearrange("p (h t) -> p h t", h=HH), ACT.Copy).then_inc(o_set, 1)

            def body(c, last):
                qk(c, 1, 2 * c)
                for g in range(G):
                    take_o(c, 0, g)
                if not last:
                    qk(c + 1, 0, 2 * c + 1)
                else:
                    act.wait_ge(mag2_set, 2 * c + 2)
                    act.activation(mag[:, :], mag2[:, :, :].rearrange("p a n -> p (a n)"), ACT.Sqrt,
                                   bias=tiny[:, 0:1]).then_inc(mag_set, 1)
                    exponent(2 * c + 1)
                for g in range(G):
                    take_o(c, 1, g)

            qk(0, 0)
            with act.Fori(0, CH - 1) as c:
                body(c, False)
            body(CH - 1, True)

        @block.vector
        def _(dve):
            dve.sem_inc(odd_out, CREDIT)
            dve.sem_inc(score_out, CREDIT)
            dve.wait_ge(set_up, 2)
            dve.tensor_reduce(mask[:, :], ident[:, :].rearrange("p (m b) -> p b m", m=N), AX_X, ALU.add).then_inc(set_up, 1)
            dve.wait_ge(small_in, 32)
            dve.wait_ge(set_up, 3)

            def take_odd(c, hh, i):
                j, kind = i // 4, i % 4
                dve.wait_ge(proj_done, PER * c + qk_at[hh] + i + 1)
                src = proj[i % 2][HD:P, :].rearrange("p (t g) -> p g t", g=G)
                b = qkb[HD:P, kind, 2 * hh + j:2 * hh + j + 1]

                def to(x):
                    return x.rearrange("p (g t) -> p g t", g=G)

                h = 2 * j + 1
                if kind == 0:
                    dve.tensor_scalar(to(q2[0:HD, h, 0]), src, b, None, ALU.add)
                    dve.tensor_scalar(to(q2[HD:P, h, 1]), src, b, -1.0, ALU.add, ALU.mult).then_inc(odd_out, 1)
                elif kind == 1:
                    dve.tensor_scalar(to(q2[HD:P, h, 0]), src, b, None, ALU.add)
                    dve.tensor_scalar(to(q2[0:HD, h, 1]), src, b, None, ALU.add).then_inc(odd_out, 1)
                else:
                    row = (kind - 2) * HD
                    dve.tensor_scalar(to(ks[row:row + HD, h]), src, b, None, ALU.add).then_inc(odd_out, 1)

            def take_v(c, i):
                g, r = i // 2, i % 2
                dve.wait_ge(proj_done, PER * c + V0 + i + 1)
                dve.tensor_tensor(v[:, g, :, r, :], proj[i % 2][:, :].rearrange("p (h d) -> p h d", h=H),
                                  vb[:, r].rearrange("p (h d) -> p h d", h=H), ALU.add).then_inc(odd_out, 1)

            def take_scores(c, hh, i):
                n = 16 * c + 8 * hh + i
                dve.wait_ge(score_done, n + 1)
                dve.tensor_tensor(masked[:, i % 2], scp[i % 2][:, :].rearrange("p (a b) -> p a b", b=GB),
                                  mask[:, :].unsqueeze(1).broadcast_to([P, 16, GB]), ALU.mult).then_inc(score_masked, 1)
                dve.wait_ge(score_masked, n + 1)
                dve.tensor_reduce(sc[:, i // 2, i % 2].rearrange("p h x n -> p (h x n)"), masked[:, i % 2],
                                  AX_X, ALU.add).then_inc(score_out, 1)

            def magnitudes(n):
                dve.wait_ge(score_out, 8 * n + 8 + CREDIT)
                s = sc[:, :, :, :, :, :].rearrange("p g a h x n -> p (g a h) x n")
                dve.tensor_tensor(sc_sq[:, :, :, :], s, s, ALU.mult).then_inc(squared2, 1)
                dve.wait_ge(squared2, n + 1)
                dve.tensor_tensor(mag2[:, :, :], sc_sq[:, :, 0, :], sc_sq[:, :, 1, :], ALU.add).then_inc(mag2_set, 1)

            def less_maximum(n):
                dve.wait_ge(mag_turned, n + 1)
                turned = tp[0:R, 0:P]
                dve.tensor_reduce(top[:, :], turned.rearrange("p (m b) -> p b m", m=N), AX_X, ALU.max).then_inc(top_set, 1)
                dve.wait_ge(top_set, n + 1)
                dve.tensor_tensor(ex[:, :, :], turned.rearrange("p (m b) -> p m b", m=N),
                                  top[:, :].unsqueeze(1).broadcast_to([R, N, GB]), ALU.subtract).then_inc(less_top, 1)

            def normalize(n):
                dve.wait_ge(exp_set, n + 1)
                dve.tensor_reduce(den[:, :], ex[:, :, :].rearrange("p m b -> p b m"), AX_X, ALU.add).then_inc(den_set, 1)
                dve.wait_ge(den_set, n + 1)
                dve.reciprocal(den[:, :], den[:, :]).then_inc(den_inv, 1)
                dve.wait_ge(den_inv, n + 1)
                dve.tensor_tensor(ex[:, :, :], ex[:, :, :], den[:, :].unsqueeze(1).broadcast_to([R, N, GB]),
                                  ALU.mult).then_inc(prob_set, 1)

            def keep_turned(n):
                dve.wait_ge(prob_turned, n + 1)
                dve.wait_ge(pt_set, n)
                dve.tensor_copy(w_t[:, :], tp[:, P:P + R]).then_inc(w_t_set, 1)

            def qk(c, hh, n=None):
                for i in range(8):
                    take_odd(c, hh, i)
                    if n is not None:
                        if i == 1:
                            less_maximum(n)
                        if i == 2:
                            normalize(n)
                        if i == 3:
                            keep_turned(n)

            def body(c, last):
                for i in range(8):
                    take_v(c, i)
                    take_scores(c, 0, i)
                magnitudes(2 * c)
                qk(c, 1, 2 * c)
                for i in range(8):
                    take_scores(c, 1, i)
                magnitudes(2 * c + 1)
                if not last:
                    qk(c + 1, 0, 2 * c + 1)
                else:
                    less_maximum(2 * c + 1)
                    normalize(2 * c + 1)
                    keep_turned(2 * c + 1)

            qk(0, 0)
            with dve.Fori(0, CH - 1) as c:
                body(c, False)
            body(CH - 1, True)

        @block.tensor
        def _(pe):
            pe.wait_ge(set_up, 3)

            def three(out, a_hi, a_lo, b_hi, b_lo, first, last):
                pe.matmul(out, a_hi, b_hi, start=first, stop=False)
                pe.matmul(out, a_hi, b_lo, start=False, stop=False)
                return pe.matmul(out, a_lo, b_hi, start=False, stop=last)

            def bank_free(c, stage, i):
                pe.wait_ge(odd_out, PER * c + stage + i - 1 + CREDIT)
                if stage == V0:
                    pe.wait_ge(even_out, 16 * c + min(7 + i, 8) + CREDIT)
                else:
                    at = 16 * c + (8 if stage == QK1 else 0)
                    pe.wait_ge(even_out, at + (max(i - 1, 0) if stage == QK1 else i - 1) + CREDIT)

            def qk_tile(c, hh, i):
                j, kind = i // 4, i % 4
                e = (2 * hh + j) * P
                r = kind % 2
                bank_free(c, qk_at[hh], i)
                for k in range(DT):
                    last = three(proj[i % 2][:, :], wt_hi[:, kind, k, e:e + P], wt_lo[:, kind, k, e:e + P],
                                 s_hi[:, r, k, :], s_lo[:, r, k, :], k == 0, k == DT - 1)
                last.then_inc(proj_done, 1)

            def v_tile(c, i):
                g, r = i // 2, i % 2
                bank_free(c, V0, i)
                for k in range(DT):
                    last = three(proj[i % 2][:, :], s_hi[:, r, k, g:T:G], s_lo[:, r, k, g:T:G],
                                 wt_hi[:, 4 + r, k, :], wt_lo[:, 4 + r, k, :], k == 0, k == DT - 1)
                last.then_inc(proj_done, 1)

            def scores(c, hh, i):
                g = i // 2
                n = 16 * c + 8 * hh + i
                if i == 0:
                    pe.wait_ge(odd_out, PER * c + qk_at[hh] + 8 + CREDIT)
                    pe.wait_ge(even_out, 16 * c + 8 * hh + 8 + CREDIT)
                pe.wait_ge(score_out, n - 1 + CREDIT)
                for a in range(2):
                    h = 2 * (i % 2) + a
                    last = pe.matmul(scp[i % 2][:, a * 2 * P:(a + 1) * 2 * P], ks[:, h, g * P:(g + 1) * P],
                                     q2[:, h, :, g * P:(g + 1) * P], start=a == 0, stop=a == 1, skip_group_check=True)
                last.then_inc(score_done, 1)

            def turn_magnitudes(n):
                pe.wait_ge(mag_set, n + 1)
                pe.matmul(tp[0:R, 0:P], mag[:, :], ident[:, :], start=True, stop=True).then_inc(mag_turned, 1)

            def turn_probabilities(n):
                pe.wait_ge(set_up, 3)
                pe.wait_ge(prob_set, n + 1)
                pe.transpose(tp[:, P:P + R], ex[:, :, :].rearrange("p m b -> p (m b)"), ident[0:R, 0:R]).then_inc(prob_turned, 1)

            def attend(c, hh, g):
                if g == 0:
                    pe.wait_ge(pt_set, 2 * c + hh + 1)
                    pe.wait_ge(odd_out, PER * c + V0 + 8 + CREDIT)
                n = 8 * c + 4 * hh + g
                pe.wait_ge(o_set, n - 1 + CREDIT)
                for a in range(HH):
                    last = pe.matmul(avp[g % 2][:, a * P:(a + 1) * P],
                                     v[:, g, HH * hh + a].rearrange("p r d -> p (r d)"),
                                     pt[:, g * HH + a, :], start=a == 0, stop=a == HH - 1, skip_group_check=True)
                last.then_inc(av_done, 1)

            def qk(c, hh, n=None):
                if hh == 0:
                    pe.wait_ge(s_in, 64 * (c + 1))
                for i in range(8):
                    qk_tile(c, hh, i)
                    if n is not None:
                        if i == 1:
                            turn_magnitudes(n)
                        if i == 3:
                            turn_probabilities(n)

            def body(c, last):
                for i in range(8):
                    v_tile(c, i)
                    scores(c, 0, i)
                qk(c, 1, 2 * c)
                for i in range(8):
                    scores(c, 1, i)
                    if i % 2:
                        attend(c, 0, i // 2)
                if not last:
                    qk(c + 1, 0, 2 * c + 1)
                else:
                    turn_magnitudes(2 * c + 1)
                    turn_probabilities(2 * c + 1)
                for g in range(G):
                    attend(c, 1, g)

            pe.wait_ge(w_hi_done, 6)
            pe.wait_ge(w_lo_done, 6)
            qk(0, 0)
            with pe.Fori(0, CH - 1) as c:
                body(c, False)
            body(CH - 1, True)


def interact(nc, sems, wo_w, wo_bias, int_w, o_dram, z_dram):
    UNITS = HALVES * N
    MAT = DT * D
    BT = HB // P

    with ExitStack() as ctx:
        def sb(name, shape, dt=F32):
            return ctx.enter_context(nc.sbuf_tensor(name, shape, dt))

        def sem(name):
            return sems.enter_context(nc.semaphore(name))

        wo_hi = sb("wo_hi", [P, 2, MAT], F32R)
        wo_lo = sb("wo_lo", [P, 2, MAT], F32R)
        o_raw = sb("o_raw", [P, DT, HB])
        o_hi = sb("o_hi", [P, 2, DT, HB], F32R)
        o_lo = sb("o_lo", [P, 2, DT, HB], F32R)
        w_raw = sb("w_raw", [P, 2, MAT])
        m_hi = sb("m_hi", [P, 3, MAT], F32R)
        m_lo = sb("m_lo", [P, 3, MAT], F32R)
        a_hi = sb("a_hi", [P, 3, DT, HB], F32R)
        a_lo = sb("a_lo", [P, 3, DT, HB], F32R)
        comb = sb("comb", [P, MAT // 2])
        a_raw = sb("a_raw", [P, 3, HB])
        k1 = sb("k1", [P, 2, D])
        z_out = sb("z_out", [P, 2, 2, D])
        wo_b = sb("wo_b", [P, 2, DT])
        wops = [ctx.enter_context(nc.psum_tensor(f"wops{u}", [P, HB], F32)) for u in range(2)]
        kps = [[ctx.enter_context(nc.psum_tensor(f"kps{u}{x}", [P, D], F32)) for x in range(3)] for u in range(2)]

        wo_in = [sem(f"wo_in{u}") for u in range(2)]
        small_in = sem("small_in3")
        wo_hi_done = sem("wo_hi_done")
        wo_lo_done = sem("wo_lo_done")
        o_in = sem("o_in")
        w_in = sem("w_in3")
        o_hi_done = sem("o_hi_done")
        o_lo_done = sem("o_lo_done")
        comb_set = sem("comb_set")
        m_hi_done = sem("m_hi_done")
        m_lo_done = sem("m_lo_done")
        dve_split = sem("dve_split")
        wo_done = sem("wo_done")
        a_raw_set = sem("a_raw_set")
        a_sum_set = sem("a_sum_set")
        a_hi_done = sem("a_hi_done")
        a_lo_done = sem("a_lo_done")
        k_done = sem("k_done")
        k1_out = sem("k1_out")
        z_set = sem("z_set")
        z_stored = [sem(f"z_stored{u}") for u in range(2)]

        block = ctx.enter_context(nc.Block())

        @block.sync
        def _(sp):
            sp.dma_start(wo_b[:, :, :], wo_bias).then_inc(small_in, 16)
            for u in range(2):
                sp.dma_start(w_raw[:, u, :], wo_w[u]).then_inc(wo_in[u], 16)
                sp.sem_inc(z_stored[u], 32)

            def load_o(h, n, r):
                for hh in range(2):
                    for d in range(2):
                        sp.dma_start(o_raw[:, 2 * hh + d, :].rearrange("p (c b) -> p c b", b=P),
                                     o_dram[r, hh, bass.ds(h * BT, BT), :, d, bass.ds(n * P, P)]
                                     .rearrange("c p b -> p c b")).then_inc(o_in, 16)

            def load_w(n):
                for r in range(2):
                    sp.dma_start(w_raw[:, r, :], int_w[r, bass.ds(n, 1)].rearrange("n p m -> p (n m)")).then_inc(w_in, 16)

            def store(h, n, k):
                for m in range(BT):
                    sp.wait_ge(z_set, 2 * BT * k + 2 * m + 2)
                    sp.dma_start(z_dram[bass.ds(h * BT + m, 1), :, :, bass.ds(n, 1), :].rearrange("c b r n d -> b (c r) (n d)"),
                                 z_out[:, m % 2, :, :]).then_inc(z_stored[m % 2], 32)

            load_o(0, 0, 0)
            sp.wait_ge(o_hi_done, 1)
            sp.wait_ge(o_lo_done, 1)
            load_o(0, 0, 1)
            for u in range(2):
                sp.wait_ge(wo_hi_done, 2)
                sp.wait_ge(wo_lo_done, 2)
            load_w(0)

            def unit(h, n, h1, n1, last):
                k = h * N + n
                if not last:
                    for r in range(2):
                        sp.wait_ge(o_hi_done, 2 * k + r + 2)
                        sp.wait_ge(o_lo_done, 2 * k + r + 2)
                        load_o(h1, n1, r)
                        if r == 0:
                            sp.wait_ge(m_lo_done, k + 1)
                            sp.wait_ge(dve_split, 4 * k + 4)
                            load_w(n1)
                store(h, n, k)

            for h in range(HALVES):
                with sp.Fori(0, N - 1) as n:
                    unit(h, n, h, n + 1, False)
                unit(h, N - 1, h + 1, 0, h == HALVES - 1)
            for u in range(2):
                sp.wait_ge(z_stored[u], 32 * (UNITS * BT // 2 + 1))

        @block.gpsimd
        def _(pool):
            for u in range(2):
                pool.wait_ge(wo_hi_done, u + 1)
                pool.tensor_tensor(wo_lo[:, u, :], w_raw[:, u, :], wo_hi[:, u, :].bitcast(F32), ALU.subtract).then_inc(wo_lo_done, 1)

            def unit(k):
                pool.wait_ge(m_hi_done, 5 * k + 1)
                pool.tensor_tensor(m_lo[:, 0, :], w_raw[:, 0, :], m_hi[:, 0, :].bitcast(F32), ALU.subtract).then_inc(m_lo_done, 1)

            def split_o(k):
                for r in range(2):
                    pool.wait_ge(o_hi_done, 2 * k + r + 1)
                    pool.tensor_tensor(o_lo[:, r].rearrange("p a b -> p (a b)"), o_raw[:, :, :].rearrange("p a b -> p (a b)"),
                                       o_hi[:, r].rearrange("p a b -> p (a b)").bitcast(F32), ALU.subtract).then_inc(o_lo_done, 1)

            split_o(0)
            with pool.Fori(0, UNITS - 1) as k:
                unit(k)
                split_o(k + 1)
            unit(UNITS - 1)

        @block.scalar
        def _(act):
            act.wait_ge(small_in, 16)
            for u in range(2):
                act.wait_ge(wo_in[u], 16)
                act.activation(wo_hi[:, u, :], w_raw[:, u, :], ACT.Copy).then_inc(wo_hi_done, 1)

            def split_o(k):
                act.wait_ge(wo_done, 2 * DT * k)
                for r in range(2):
                    act.wait_ge(o_in, 64 * (2 * k + r + 1))
                    act.activation(o_hi[:, r].rearrange("p a b -> p (a b)"), o_raw[:, :, :].rearrange("p a b -> p (a b)"),
                                   ACT.Copy).then_inc(o_hi_done, 1)

            def split_m(k):
                act.wait_ge(w_in, 32 * (k + 1))
                act.wait_ge(k_done, BT * k)
                act.activation(m_hi[:, 0, :], w_raw[:, 0, :], ACT.Copy).then_inc(m_hi_done, 1)
                for x in range(1, 3):
                    for c in range(2):
                        act.wait_ge(comb_set, 4 * k + 2 * (x - 1) + c + 1)
                        act.activation(m_hi[:, x, c * MAT // 2:(c + 1) * MAT // 2], comb[:, :], ACT.Copy).then_inc(m_hi_done, 1)

            def project(k, j):
                for r in range(2):
                    act.wait_ge(wo_done, 2 * DT * k + 2 * j + r + 1)
                    if r == 0:
                        act.wait_ge(a_lo_done, 3 * DT * k + 3 * j)
                    act.activation(a_raw[:, 1 + r, :], wops[r][:, :], ACT.Identity,
                                   bias=wo_b[:, r, j:j + 1]).then_inc(a_raw_set, 1)
                at = 3 * DT * k + 3 * j
                act.wait_ge(a_raw_set, 2 * DT * k + 2 * j + 2)
                act.activation(a_hi[:, 1, j, :], a_raw[:, 1, :], ACT.Copy).then_inc(a_hi_done, 1)
                act.activation(a_hi[:, 2, j, :], a_raw[:, 2, :], ACT.Copy).then_inc(a_hi_done, 1)
                act.wait_ge(a_sum_set, DT * k + j + 1)
                act.activation(a_hi[:, 0, j, :], a_raw[:, 0, :], ACT.Copy).then_inc(a_hi_done, 1)

            def take_k1(k, m):
                act.wait_ge(k_done, BT * k + m + 1)
                if m >= 2:
                    act.wait_ge(z_set, 2 * BT * k + 2 * m - 2)
                act.activation(k1[:, m % 2, :], kps[m % 2][0][:, :], ACT.Copy).then_inc(k1_out, 1)

            def unit(k, last):
                split_m(k)
                for j in range(DT):
                    project(k, j)
                if not last:
                    split_o(k + 1)
                for m in range(BT):
                    take_k1(k, m)

            split_o(0)
            with act.Fori(0, UNITS - 1) as k:
                unit(k, False)
            unit(UNITS - 1, True)

        @block.vector
        def _(dve):
            def unit(k):
                dve.wait_ge(w_in, 32 * (k + 1))
                for x, (i0, i1, op) in ((1, (1, 0, ALU.subtract)), (2, (0, 1, ALU.add))):
                    for c in range(2):
                        cols = slice(c * MAT // 2, (c + 1) * MAT // 2)
                        done = 2 * (x - 1) + c
                        dve.wait_ge(dve_split, 4 * k + done)
                        dve.tensor_tensor(comb[:, :], w_raw[:, i0, cols], w_raw[:, i1, cols], op).then_inc(comb_set, 1)
                        dve.wait_ge(m_hi_done, 5 * k + done + 2)
                        dve.tensor_tensor(m_lo[:, x, cols], comb[:, :], m_hi[:, x, cols].bitcast(F32), ALU.subtract).then_inc(dve_split, 1)
                for j in range(DT):
                    dve.wait_ge(a_raw_set, 2 * DT * k + 2 * j + 2)
                    dve.tensor_tensor(a_raw[:, 0, :], a_raw[:, 1, :], a_raw[:, 2, :], ALU.add).then_inc(a_sum_set, 1)
                    for n, x in enumerate((1, 2, 0)):
                        dve.wait_ge(a_hi_done, 3 * DT * k + 3 * j + n + 1)
                        dve.tensor_tensor(a_lo[:, x, j, :], a_raw[:, x, :], a_hi[:, x, j, :].bitcast(F32),
                                          ALU.subtract).then_inc(a_lo_done, 1)
                for m in range(BT):
                    u = m % 2
                    dve.wait_ge(k1_out, BT * k + m + 1)
                    dve.wait_ge(z_stored[u], 32 * (BT // 2 * k + m // 2 + 1))
                    dve.tensor_tensor(z_out[:, u, 0, :], k1[:, u, :], kps[u][2][:, :], ALU.subtract).then_inc(z_set, 1)
                    dve.tensor_tensor(z_out[:, u, 1, :], k1[:, u, :], kps[u][1][:, :], ALU.add).then_inc(z_set, 1)

            with dve.Fori(0, UNITS) as k:
                unit(k)

        @block.tensor
        def _(pe):
            def three(out, a_h, a_l, b_h, b_l, first, last):
                pe.matmul(out, a_h, b_h, start=first, stop=False)
                pe.matmul(out, a_h, b_l, start=False, stop=False)
                return pe.matmul(out, a_l, b_h, start=False, stop=last)

            def unit(k):
                pe.wait_ge(o_lo_done, 2 * k + 2)
                for j in range(DT):
                    for r in range(2):
                        pe.wait_ge(a_raw_set, 2 * DT * k + 2 * j + r - 1 if j else 2 * DT * k)
                        for d in range(DT):
                            w = slice(d * D + j * P, d * D + (j + 1) * P)
                            last = three(wops[r][:, :], wo_hi[:, r, w], wo_lo[:, r, w], o_hi[:, r, d, :], o_lo[:, r, d, :],
                                         d == 0, d == DT - 1)
                        last.then_inc(wo_done, 1)
                pe.wait_ge(m_lo_done, k + 1)
                pe.wait_ge(dve_split, 4 * k + 4)
                pe.wait_ge(a_lo_done, 3 * DT * (k + 1))
                for m in range(BT):
                    pe.wait_ge(z_set, 2 * BT * k + 2 * m - 2 if m >= 2 else 2 * BT * k)
                    for x in range(3):
                        for d in range(DT):
                            b = slice(m * P, (m + 1) * P)
                            w = slice(d * D, (d + 1) * D)
                            last = three(kps[m % 2][x][:, :], a_hi[:, x, d, b], a_lo[:, x, d, b], m_hi[:, x, w], m_lo[:, x, w],
                                         d == 0, d == DT - 1)
                    last.then_inc(k_done, 1)

            pe.wait_ge(wo_lo_done, 2)
            with pe.Fori(0, UNITS) as k:
                unit(k)


I32 = mybir.dt.int32
LEAST = 1e-34


def finish(nc, sems, ids, tables, meas_w, post_w, post_rows, top1_w, top2_w, top3_w, top2_b, z_dram, hx_dram, out):
    PAIRS = [(0, 1), (1, 2), (2, 3), (0, 2), (1, 3), (0, 3)]
    SHIFTS = [(1, 0, 3), (2, 3, 5), (3, 5, 6)]
    pair_of = {frozenset(p): n for n, p in enumerate(PAIRS)}
    MAT = DT * D
    T1 = 512 // P
    T2 = 256 // P

    with ExitStack() as ctx:
        def sb(name, shape, dt=F32):
            return ctx.enter_context(nc.sbuf_tensor(name, shape, dt))

        def sem(name):
            return sems.enter_context(nc.semaphore(name))

        def ps(name):
            return ctx.enter_context(nc.psum_tensor(name, [P, 512], F32))

        z = sb("z", [P, 2, 2, N, D])
        ids_sb = sb("ids_sb", [P, CH, N], I32)
        st = sb("st", [P, CH, N, N])
        p2 = sb("p2", [P, N, D])
        prod = sb("prod", [P, 2, N, D])
        flag = sb("flag", [P, N, D])
        cos = sb("cos", [P, 6, D])
        part = sb("part", [P, 6, D])
        flags = sb("flags", [P, 6, D])
        coef = sb("coef", [P, N, D])
        sup = sb("sup", [P, 2, D])
        supn = sb("supn", [P, 2, D])
        sup_t = sb("sup_t", [P, 3, D])
        ss = sb("ss", [P, 1])
        root = sb("root", [P, 1])
        m_sq = sb("m_sq", [P, 2, D])
        amp = sb("amp", [P, D])
        amp_t = sb("amp_t", [P, D])
        y = sb("y", [P, D])
        stats = sb("stats", [P, 6])
        mv = sb("mv", [P, 2])
        rs = sb("rs", [P, 1])
        z_t = sb("z_t", [P, DT, B])
        ident = sb("ident4", [P, P])
        eps = sb("eps4", [P, 1])
        tiny = sb("tiny4", [P, 1])
        mw = sb("mw", [P, 2, MAT])
        pw = sb("pw", [P, MAT])
        rows = sb("rows", [P, 3, D])
        w1 = sb("w1", [P, MAT])
        w2 = sb("w2", [P, DT, 256])
        w3 = sb("w3", [P, T2])
        b2 = sb("b2", [P, T2])
        turn = [ps("turn_r"), ps("turn_i")]
        mea = [ps("mea_r"), ps("mea_i")]
        ampp, postp, zp = ps("ampp"), ps("postp"), ps("zp")
        hx = prod[:, :, :, :].rearrange("p a n d -> p (a n d)").rearrange("p (h t b) -> p h t b", h=HALVES, t=T1)
        h1 = z[:, 0].rearrange("p a n d -> p (a n d)").rearrange("p (h t b) -> p h t b", h=HALVES, t=T1)
        h2 = z[:, 1].rearrange("p a n d -> p (a n d)")[:, 0:HALVES * T2 * HB].rearrange("p (h t b) -> p h t b", h=HALVES, t=T2)
        y_out = sup[0:1, :, :]

        z_in = [sem(f"z_in{u}") for u in range(2)]
        ids_in, hx_in = sem("ids_in"), sem("hx_in")
        gathered = sem("gathered")
        made = sem("made")
        names = ("z_sq p2_set flag_set p2_max p_root p_inv unit_r unit_i cos1 part1 flags1 part2 cos_set coef_step "
                 "prod_set sup_set ss_set root_set root_inv supn_set sup_turned sup_t_set meas_done m_sq_set amp2_set "
                 "amp_set amp_turned amp_t_set post_done y_set stat_set mv_set var_root rs_set y_norm y_g y_gb y_gelu "
                 "y_turned z_t_set h1_done h1_sum h1_set h2_done h2_set y_done y_copied y_stored").split()
        S = {n: sem("f_" + n) for n in names}
        const_in = sem("const_in")
        block = ctx.enter_context(nc.Block())

        def flat(x):
            return x.rearrange("p n d -> p (n d)")

        @block.sync
        def _(sp):
            sp.dma_start(ids_sb[:, :, :], ids).then_inc(ids_in, 16)
            sp.dma_start(z[:, 0], z_dram[0]).then_inc(z_in[0], 16)
            sp.dma_start(z[:, 1], z_dram[1]).then_inc(z_in[1], 16)
            for r in range(2):
                sp.dma_start(mw[:, r, :], meas_w[r]).then_inc(const_in, 16)
            sp.dma_start(pw[:, :], post_w).then_inc(const_in, 16)
            sp.dma_start(rows[:, :, :], post_rows.partition_broadcast(P)).then_inc(const_in, 16)
            sp.dma_start(w1[:, :], top1_w).then_inc(const_in, 16)
            sp.dma_start(w2[:, :, :], top2_w).then_inc(const_in, 16)
            sp.dma_start(w3[:, :], top3_w).then_inc(const_in, 16)
            sp.dma_start(b2[:, :], top2_b).then_inc(const_in, 16)
            with sp.Fori(1, CH // 2) as i:
                for u in range(2):
                    sp.wait_ge(S["prod_set"], 2 * (2 * i + u) - 2)
                    sp.dma_start(z[:, u], z_dram[bass.ds(2 * i + u, 1)].rearrange("c p r n d -> p (c r) n d")).then_inc(z_in[u], 16)
            sp.wait_ge(S["sup_set"], CH)
            for h in range(HALVES):
                sp.dma_start(hx[:, h], hx_dram[h]).then_inc(hx_in, 16)
            sp.wait_ge(S["y_copied"], 2)
            sp.dma_start(out.rearrange("(h b) o -> o h b", h=HALVES), y_out).then_inc(S["y_stored"], 16)
            sp.wait_ge(S["y_stored"], 16)

        @block.gpsimd
        def _(pool):
            pool.memset(ident[:, :], 0.0).then_inc(made, 1)
            pool.wait_ge(made, 1)
            pool.affine_select(out=ident[:, :], in_=ident[:, :], compare_op=ALU.not_equal, fill=1.0,
                               base=0, pattern=[[-1, P]], channel_multiplier=1).then_inc(made, 1)
            pool.memset(eps[:, :], EPS).then_inc(made, 1)
            pool.memset(tiny[:, :], 1e-8).then_inc(made, 1)
            pool.wait_ge(ids_in, 16)
            for c in range(CH):
                for n in range(N):
                    pool.indirect_dma_start(out=st[:, c, n, :], out_offset=None, in_=tables[n],
                                            in_offset=bass.IndirectOffsetOnAxis(ap=ids_sb[:, c, n:n + 1], axis=0)
                                            ).then_inc(gathered, 16)

            def head(c, u):
                pool.wait_ge(S["flag_set"], c + 1)
                for s, a, b in SHIFTS:
                    last = pool.tensor_tensor(flags[:, a:b], flag[:, 0:N - s], flag[:, s:N], ALU.add)
                last.then_inc(S["flags1"], 1)
                pool.wait_ge(S["unit_i"], c + 1)
                pool.wait_ge(S["cos_set"], c)
                for s, a, b in SHIFTS:
                    last = pool.tensor_tensor(part[:, a:b], prod[:, 1, 0:N - s], prod[:, 1, s:N], ALU.mult)
                last.then_inc(S["part1"], 1)
                pool.wait_ge(S["flags1"], c + 1)
                pool.wait_ge(S["part1"], c + 1)
                pool.tensor_tensor(flat(part[:, :, :]), flat(part[:, :, :]), flat(flags[:, :, :]), ALU.add).then_inc(S["part2"], 1)
                pool.wait_ge(S["part2"], c + 1)

            head(0, 0)
            with pool.Fori(1, CH) as c:
                head(c, 0)

        @block.scalar
        def _(act):
            act.wait_ge(made, 4)

            def head_squares(c, u):
                act.wait_ge(z_in[u], 16 * (c // 2 + 1))
                act.wait_ge(S["sup_set"], c)
                for r in range(2):
                    act.activation(prod[:, r].rearrange("p n d -> p (n d)"), z[:, u, r].rearrange("p n d -> p (n d)"),
                                   ACT.Square).then_inc(S["z_sq"], 1)

            def head_root(c):
                act.wait_ge(S["p2_max"], c + 1)
                act.activation(flat(p2[:, :, :]), flat(p2[:, :, :]), ACT.Sqrt).then_inc(S["p_root"], 1)

            def head_norm(c):
                act.wait_ge(S["sup_set"], c + 1)
                act.activation(supn[:, :, :], sup[:, :, :], ACT.Square, accum_out=ss[:, 0:1]).then_inc(S["ss_set"], 1)
                act.wait_ge(S["ss_set"], c + 1)
                act.activation(root[:, :], ss[:, :], ACT.Sqrt, bias=tiny[:, 0:1]).then_inc(S["root_set"], 1)

            def tail_turned(c):
                act.wait_ge(S["sup_turned"], c + 1)
                act.activation(sup_t[:, 0, :], turn[0][:, :], ACT.Copy)
                act.activation(sup_t[:, 1, :], turn[1][:, :], ACT.Copy)
                act.activation(sup_t[:, 2, :], turn[1][:, :], ACT.Copy, scale=-1.0).then_inc(S["sup_t_set"], 1)

            def tail_amp(c):
                act.wait_ge(S["meas_done"], c + 1)
                for r in range(2):
                    act.activation(m_sq[:, r, :], mea[r][:, :], ACT.Square).then_inc(S["m_sq_set"], 1)
                act.wait_ge(S["amp2_set"], c + 1)
                act.activation(amp[:, :], amp[:, :], ACT.Sqrt).then_inc(S["amp_set"], 1)
                act.wait_ge(S["amp_turned"], c + 1)
                act.activation(amp_t[:, :], ampp[:, :], ACT.Copy).then_inc(S["amp_t_set"], 1)

            def tail_post(c):
                act.wait_ge(S["mv_set"], c + 1)
                act.activation(rs[:, :], mv[:, 1:2], ACT.Sqrt, bias=eps[:, 0:1]).then_inc(S["var_root"], 1)
                act.wait_ge(S["y_gb"], c + 1)
                act.activation(y[:, :], y[:, :], ACT.Gelu).then_inc(S["y_gelu"], 1)

            def tail_keep(c):
                act.wait_ge(S["y_turned"], c + 1)
                act.activation(z_t[:, :, bass.ds(c * P, P)], zp[:, :].rearrange("p (k b) -> p k b", k=DT),
                               ACT.Copy).then_inc(S["z_t_set"], 1)

            def both(c, u):
                tail_turned(c - 1)
                head_squares(c, u)
                head_root(c)
                tail_amp(c - 1)
                head_norm(c)
                tail_post(c - 1)
                tail_keep(c - 1)

            head_squares(0, 0)
            head_root(0)
            head_norm(0)
            with act.Fori(0, CH // 2 - 1) as i:
                both(2 * i + 1, 1)
                both(2 * i + 2, 0)
            both(CH - 1, 1)
            tail_turned(CH - 1)
            tail_amp(CH - 1)
            tail_post(CH - 1)
            tail_keep(CH - 1)
            for h in range(HALVES):
                for t in range(T2):
                    act.wait_ge(S["h2_done"], h * T2 + t + 1)
                    act.activation(h2[:, h, t, :], turn[t][:, :], ACT.Relu, bias=b2[:, t:t + 1]).then_inc(S["h2_set"], 1)
            for h in range(HALVES):
                act.wait_ge(S["y_done"], h + 1)
                act.activation(y_out[:, h, :], (ampp, postp)[h][0:1, :], ACT.Copy).then_inc(S["y_copied"], 1)

        @block.vector
        def _(dve):
            def head_one(c):
                dve.wait_ge(S["z_sq"], 2 * c + 2)
                dve.tensor_tensor(flat(p2[:, :, :]), prod[:, 0].rearrange("p n d -> p (n d)"),
                                  prod[:, 1].rearrange("p n d -> p (n d)"), ALU.add).then_inc(S["p2_set"], 1)
                dve.wait_ge(S["p2_set"], c + 1)
                dve.wait_ge(S["flags1"], c)
                dve.tensor_scalar(flat(flag[:, :, :]), flat(p2[:, :, :]), LEAST, None, ALU.is_lt).then_inc(S["flag_set"], 1)
                dve.wait_ge(S["flag_set"], c + 1)
                dve.tensor_scalar(flat(p2[:, :, :]), flat(p2[:, :, :]), LEAST, None, ALU.max).then_inc(S["p2_max"], 1)

            def head_two(c, u):
                dve.wait_ge(S["p_root"], c + 1)
                dve.reciprocal(flat(p2[:, :, :]), flat(p2[:, :, :])).then_inc(S["p_inv"], 1)
                dve.wait_ge(S["p_inv"], c + 1)
                for r, name in ((1, "unit_i"), (0, "unit_r")):
                    dve.tensor_tensor(prod[:, r].rearrange("p n d -> p (n d)"), z[:, u, r].rearrange("p n d -> p (n d)"),
                                      flat(p2[:, :, :]), ALU.mult).then_inc(S[name], 1)
                dve.wait_ge(S["unit_r"], c + 1)
                for s, a, b in SHIFTS:
                    last = dve.tensor_tensor(cos[:, a:b], prod[:, 0, 0:N - s], prod[:, 0, s:N], ALU.mult)
                last.then_inc(S["cos1"], 1)

            def head_three(c, u):
                dve.wait_ge(S["part2"], c + 1)
                dve.wait_ge(S["cos1"], c + 1)
                dve.tensor_tensor(flat(cos[:, :, :]), flat(cos[:, :, :]), flat(part[:, :, :]), ALU.add).then_inc(S["cos_set"], 1)
                dve.wait_ge(S["cos_set"], c + 1)

                def strength(i, j):
                    return st[:, bass.ds(c, 1), i, j:j + 1].rearrange("p a b -> p (a b)")

                for k in range(3):
                    for j in range(N):
                        i = [x for x in range(N) if x != j][k]
                        pair = cos[:, pair_of[frozenset((i, j))], :]
                        if k == 0:
                            dve.tensor_scalar(coef[:, j, :], pair, strength(i, j), strength(j, j),
                                              ALU.mult, ALU.add).then_inc(S["coef_step"], 1)
                        else:
                            dve.wait_ge(S["coef_step"], 12 * c + 4 * (k - 1) + j + 1)
                            dve.scalar_tensor_tensor(out=coef[:, j, :], in0=pair, scalar=strength(i, j), in1=coef[:, j, :],
                                                     op0=ALU.mult, op1=ALU.add).then_inc(S["coef_step"], 1)
                dve.wait_ge(S["coef_step"], 12 * c + 12)
                for r in range(2):
                    dve.tensor_tensor(prod[:, r].rearrange("p n d -> p (n d)"), z[:, u, r].rearrange("p n d -> p (n d)"),
                                      flat(coef[:, :, :]), ALU.mult).then_inc(S["prod_set"], 1)
                dve.wait_ge(S["prod_set"], 2 * c + 2)
                dve.wait_ge(S["supn_set"], c)
                dve.tensor_reduce(sup[:, :, :], prod[:, :, :, :].rearrange("p r n d -> p r d n"), AX_X, ALU.add).then_inc(S["sup_set"], 1)

            def head_four(c):
                dve.wait_ge(S["root_set"], c + 1)
                dve.reciprocal(root[:, :], root[:, :]).then_inc(S["root_inv"], 1)
                dve.wait_ge(S["root_inv"], c + 1)
                dve.wait_ge(S["sup_turned"], c)
                dve.tensor_scalar(supn[:, :, :], sup[:, :, :], root[:, 0:1], None, ALU.mult).then_inc(S["supn_set"], 1)

            def tail_amp(c):
                dve.wait_ge(S["m_sq_set"], 2 * c + 2)
                dve.wait_ge(S["amp_turned"], c)
                dve.tensor_tensor(amp[:, :], m_sq[:, 0, :], m_sq[:, 1, :], ALU.add).then_inc(S["amp2_set"], 1)

            def tail_post(c):
                dve.wait_ge(S["post_done"], c + 1)
                dve.wait_ge(S["y_turned"], c)
                dve.tensor_tensor(y[:, :], postp[:, :], rows[:, 0, :], ALU.add).then_inc(S["y_set"], 1)
                dve.wait_ge(S["y_set"], c + 1)
                dve.bn_stats(stats[:, :], y[:, :]).then_inc(S["stat_set"], 1)
                dve.wait_ge(const_in, 16 * 8)
                dve.wait_ge(S["stat_set"], c + 1)
                dve.bn_aggr(mv[:, :], stats[:, :]).then_inc(S["mv_set"], 1)
                dve.wait_ge(S["var_root"], c + 1)
                dve.reciprocal(rs[:, :], rs[:, :]).then_inc(S["rs_set"], 1)
                dve.wait_ge(S["rs_set"], c + 1)
                dve.tensor_scalar(y[:, :], y[:, :], mv[:, 0:1], rs[:, 0:1], ALU.subtract, ALU.mult).then_inc(S["y_norm"], 1)
                dve.wait_ge(S["y_norm"], c + 1)
                dve.tensor_tensor(y[:, :], y[:, :], rows[:, 1, :], ALU.mult).then_inc(S["y_g"], 1)
                dve.wait_ge(S["y_g"], c + 1)
                dve.tensor_tensor(y[:, :], y[:, :], rows[:, 2, :], ALU.add).then_inc(S["y_gb"], 1)

            def both(c, u):
                head_one(c)
                head_two(c, u)
                tail_amp(c - 1)
                head_three(c, u)
                head_four(c)
                tail_post(c - 1)

            dve.wait_ge(gathered, 16 * CH * N)
            dve.wait_ge(const_in, 16 * 8)
            head_one(0)
            head_two(0, 0)
            head_three(0, 0)
            head_four(0)
            with dve.Fori(0, CH // 2 - 1) as i:
                both(2 * i + 1, 1)
                both(2 * i + 2, 0)
            both(CH - 1, 1)
            tail_amp(CH - 1)
            tail_post(CH - 1)
            dve.wait_ge(hx_in, 16 * HALVES)
            for h in range(HALVES):
                for t in range(T1):
                    n = h * T1 + t
                    dve.wait_ge(S["h1_done"], n + 1)
                    dve.tensor_tensor(h1[:, h, t, :], mea[n % 2][:, :], hx[:, h, t, :], ALU.add).then_inc(S["h1_sum"], 1)
                    dve.wait_ge(S["h1_sum"], n + 1)
                    dve.tensor_scalar(h1[:, h, t, :], h1[:, h, t, :], 0.0, None, ALU.max).then_inc(S["h1_set"], 1)

        @block.tensor
        def _(pe):
            pe.wait_ge(made, 4)
            pe.wait_ge(const_in, 16 * 8)

            def tail(c):
                pe.wait_ge(S["supn_set"], c + 1)
                for r in range(2):
                    for k in range(DT):
                        last = pe.transpose(turn[r][:, k * P:(k + 1) * P], supn[:, r, k * P:(k + 1) * P], ident[:, :])
                last.then_inc(S["sup_turned"], 1)
                pe.wait_ge(S["sup_t_set"], c + 1)
                pe.wait_ge(S["m_sq_set"], 2 * c)
                for r in range(2):
                    for x, (a, w) in enumerate(((0, r), (2 - r, 1 - r))):
                        for k in range(DT):
                            last = pe.matmul(mea[r][:, :], sup_t[:, a, k * P:(k + 1) * P], mw[:, w, k * D:(k + 1) * D],
                                             start=x == 0 and k == 0, stop=x == 1 and k == DT - 1)
                last.then_inc(S["meas_done"], 1)
                pe.wait_ge(S["amp_set"], c + 1)
                pe.wait_ge(S["amp_t_set"], c)
                for k in range(DT):
                    last = pe.transpose(ampp[:, k * P:(k + 1) * P], amp[:, k * P:(k + 1) * P], ident[:, :])
                last.then_inc(S["amp_turned"], 1)
                pe.wait_ge(S["amp_t_set"], c + 1)
                pe.wait_ge(S["y_set"], c)
                for k in range(DT):
                    last = pe.matmul(postp[:, :], amp_t[:, k * P:(k + 1) * P], pw[:, k * D:(k + 1) * D],
                                     start=k == 0, stop=k == DT - 1)
                last.then_inc(S["post_done"], 1)
                pe.wait_ge(S["y_gelu"], c + 1)
                pe.wait_ge(S["z_t_set"], c)
                for k in range(DT):
                    last = pe.transpose(zp[:, k * P:(k + 1) * P], y[:, k * P:(k + 1) * P], ident[:, :])
                last.then_inc(S["y_turned"], 1)

            with pe.Fori(0, CH) as c:
                tail(c)
            pe.wait_ge(S["z_t_set"], CH)
            for h in range(HALVES):
                for t in range(T1):
                    n = h * T1 + t
                    if n >= 2:
                        pe.wait_ge(S["h1_sum"], n - 1)
                    for k in range(DT):
                        last = pe.matmul(mea[n % 2][:, :], w1[:, k * D + t * P:k * D + (t + 1) * P],
                                         z_t[:, k, h * HB:(h + 1) * HB], start=k == 0, stop=k == DT - 1)
                    last.then_inc(S["h1_done"], 1)
                pe.wait_ge(S["h1_set"], (h + 1) * T1)
                for t in range(T2):
                    if h:
                        pe.wait_ge(S["h2_set"], t + 1)
                    for k in range(T1):
                        last = pe.matmul(turn[t][:, :], w2[:, k, t * P:(t + 1) * P], h1[:, h, k, :],
                                         start=k == 0, stop=k == T1 - 1)
                    last.then_inc(S["h2_done"], 1)
                pe.wait_ge(S["h2_set"], (h + 1) * T2)
                for k in range(T2):
                    last = pe.matmul((ampp, postp)[h][0:1, :], w3[:, k:k + 1], h2[:, h, k, :], start=k == 0, stop=k == T2 - 1)
                last.then_inc(S["y_done"], 1)


def program(nc, t, out):
    s_dram = nc.dram_tensor("s_scratch", [2, 2, CH, P, DT * N, P], F32).ap()
    hx_dram = nc.dram_tensor("hx_scratch", [HALVES, P, 512 // P, HB], F32).ap()
    o_dram = nc.dram_tensor("o_scratch", [2, 2, CH, P, 2, N * P], F32).ap()
    z_dram = nc.dram_tensor("z_scratch", [CH, P, 2, N, D], F32).ap()
    with ExitStack() as sems:
        encoders(nc, sems, t["x_t"], t["enc_w"], t["enc_bias"], t["ln_gb"], s_dram, hx_dram)
        attention(nc, sems, t["qkv_w"], t["qk_bias"], t["v_bias"], s_dram, o_dram)
        interact(nc, sems, t["wo_w"], t["wo_bias"], t["int_w"], o_dram, z_dram)
        finish(nc, sems, t["row_ids"], [t[f"table_{n}"] for n in range(N)], t["meas_w"], t["post_w"], t["post_rows"],
               t["top1_w"], t["top2_w"], t["top3_w"], t["top2_b"], z_dram, hx_dram, out)



def lay_out(inp, np):
    def g(name):
        return np.asarray(inp[name])

    def rec(name):
        return g("L0_rec_" + name)

    def pieces(w):
        o, i = w.shape
        return w.reshape(o // P, P, 2, i // P // 2, P).transpose(0, 2, 4, 3, 1).reshape(o // P * 2, P, i // 2)

    def tokens_inner(w):
        return w.reshape((N, DT, P) + w.shape[1:]).swapaxes(0, 1).reshape(w.shape)

    def by_row(w):
        return w.reshape(DT, P, w.shape[1]).transpose(1, 0, 2).reshape(P, DT * w.shape[1])

    def columns(v):
        return v.reshape(-1, P).T

    out = {
        "x_t": g("r_x").reshape(HALVES, HB, KT // 2, 2, P).transpose(0, 2, 4, 3, 1).reshape(HALVES, KT // 2, P, 2 * HB),
        "enc_w": np.concatenate([pieces(w) for w in (
            rec("er_W1"), rec("ei_W1"), g("W_top1")[OUT:].T, tokens_inner(rec("er_W2")), tokens_inner(rec("ei_W2")))]),
        "enc_bias": columns(np.concatenate([rec("er_b1"), rec("ei_b1"), g("b_top1"),
                                            tokens_inner(rec("er_b2")), tokens_inner(rec("ei_b2"))])),
        "ln_gb": np.stack([rec(n) for n in ("er_g1", "er_be1", "ei_g1", "ei_be1")]).reshape(2, 2, KT, P).transpose(3, 0, 1, 2),
        "qkv_w": np.stack([by_row(rec("W" + n).T) for n in ("q_r", "q_i", "k_r", "k_i", "v_r", "v_i")]),
        "qk_bias": np.stack([rec("b" + n) for n in ("q_r", "q_i", "k_r", "k_i")]).reshape(4, DT, P).transpose(2, 0, 1),
        "v_bias": np.stack([rec("bv_r"), rec("bv_i")]),
        "wo_w": np.stack([by_row(rec("Wo_r").T), by_row(rec("Wo_i").T)]),
        "wo_bias": np.stack([rec("bo_r"), rec("bo_i")]).reshape(2, DT, P).transpose(2, 0, 1),
        "int_w": np.stack([np.stack([by_row(w.T) for w in rec(n)]) for n in ("int_Wr", "int_Wi")]),
        "row_ids": g("ids").reshape(CH, P, N).transpose(1, 0, 2),
        "meas_w": np.stack([by_row(rec("meas_Mr").T), by_row(rec("meas_Mi").T)]),
        "post_w": by_row(rec("post_W").T),
        "post_rows": np.stack([rec("post_b"), rec("post_g"), rec("post_be")]),
        "top1_w": by_row(g("W_top1")[:OUT]),
        "top2_w": g("W_top2").reshape(DT, P, 256).transpose(1, 0, 2),
        "top3_w": columns(g("W_top3")),
        "top2_b": columns(g("b_top2")),
    }
    out.update({f"table_{n}": g(f"tbl_{n}") for n in range(N)})
    return {k: np.ascontiguousarray(v) for k, v in out.items()}


def kernel(**inputs):
    import numpy as np
    import concourse.bacc as bacc
    from concourse.bass_utils import run_bass_kernel_spmd

    nc = bacc.Bacc("TRN2", target_bir_lowering=False, num_devices=1)
    arrays = {f"in_{k}": v for k, v in lay_out(inputs, np).items()}
    t = {k[3:]: nc.dram_tensor(k, v.shape, mybir.dt.from_np(v.dtype), kind="ExternalInput").ap() for k, v in arrays.items()}
    out = nc.dram_tensor("out_0_dram", (B, 1), F32, kind="ExternalOutput").ap()
    program(nc, t, out)
    r = run_bass_kernel_spmd(nc, [arrays], core_ids=[0])
    return r.results[0]["out_0_dram"]
```

```python
from contextlib import ExitStack

import concourse.bass as bass
from concourse import mybir

F32 = mybir.dt.float32
F32R = mybir.dt.float32r
ALU = mybir.AluOpType
ACT = mybir.ActivationFunctionType
AX_X = mybir.AxisListType.X

P = 128
B, IN, HID, D, N, H, OUT = 1024, 2048, 2048, 512, 4, 8, 512
HD = D // H
HB = 512
HALVES = B // HB
KT = IN // P
CH = B // P
DT = D // P
EPS = 1e-5
CREDIT = 2


def encoders(nc, sems, x_t, enc_w, enc_bias, ln_gb, s_dram, hx_dram):
    L1 = HID // P
    XP = 512 // P
    L2 = N * D // P
    TILES = 2 * L1 + XP + 2 * L2
    XPIECES = KT // 2
    PIECE = KT // 2 * P
    PIECES = XPIECES + 2 * TILES
    STORES = (XP + 2 * L2) // 2

    with ExitStack() as ctx:
        def sb(name, shape, dt=F32):
            return ctx.enter_context(nc.sbuf_tensor(name, shape, dt))

        def sem(name):
            return sems.enter_context(nc.semaphore(name))

        act_hi = sb("act_hi", [P, KT, HB], F32R)
        act_lo = sb("act_lo", [P, KT, HB], F32R)
        y_r_at = nc.sbuf_base
        y_r = sb("y_r", [P, KT, HB])
        hid_hi = nc.alloc_sbuf_tensor_at("hid_hi", [P, KT, HB], F32R, offset=y_r_at)
        hid_lo = sb("hid_lo", [P, KT, HB], F32R)
        y_i = sb("y_i", [P, KT, HB])
        raw = sb("raw", [P, 2, PIECE])
        w_hi = sb("w_hi", [P, 2, PIECE], F32R)
        w_lo = sb("w_lo", [P, 2, PIECE], F32R)
        total = sb("total", [P, HB])
        sq_total = sb("sq_total", [P, HB])
        mean = sb("mean", [P, HB])
        rstd = sb("rstd", [P, HB])
        ln_tmp = sb("ln_tmp", [P, 2, HB])
        stage = sb("stage", [P, 2, 2, HB])
        bias = sb("bias", [P, TILES])
        gb = sb("gb", [P, 2, 2, KT])
        over_n = sb("over_n", [P, P])
        eps = sb("eps", [P, 1])
        acc = [ctx.enter_context(nc.psum_tensor(f"acc{u}", [P, HB], F32)) for u in range(2)]
        stat = ctx.enter_context(nc.psum_tensor("stat", [P, HB], F32))

        loaded = [sem(f"loaded{u}") for u in range(2)]
        hi_done = sem("hi_done")
        lo_done = sem("lo_done")
        half_done = sem("half_done")
        tile_done = sem("tile_done")
        evacuated = sem("evacuated")
        added = sem("added")
        cleared = sem("cleared")
        stat_done = sem("stat_done")
        mean_ready = sem("mean_ready")
        centered = sem("centered")
        squared = sem("squared")
        sq_added = sem("sq_added")
        root_done = sem("root_done")
        rstd_ready = sem("rstd_ready")
        scaled = sem("scaled")
        gelu_done = sem("gelu_done")
        h_hi = sem("h_hi")
        h_lo = sem("h_lo")
        hi_staged = sem("hi_staged")
        stored = [sem(f"stored{u}") for u in range(2)]
        consts_in = sem("consts_in")
        consts_set = sem("consts_set")

        block = ctx.enter_context(nc.Block())

        R1, I1, TX, R2, I2 = (0, L1), (L1, L1), (2 * L1, XP), (2 * L1 + XP, L2), (2 * L1 + XP + L2, L2)

        @block.sync
        def _(sp):
            sp.dma_start(bias[:, :], enc_bias).then_inc(consts_in, 16)
            sp.dma_start(gb[:, :, :, :], ln_gb).then_inc(consts_in, 16)
            for u in range(2):
                sp.sem_inc(stored[u], 32)

            def load(h, piece, u, src):
                sp.wait_ge(hi_done, h * PIECES + piece + 1)
                sp.wait_ge(lo_done, h * PIECES + piece + 1)
                sp.dma_start(raw[:, u, :], src).then_inc(loaded[u], 16)

            def load_tile(h, t):
                for u in range(2):
                    load(h, XPIECES + 2 * t + u, u, enc_w[bass.ds(2 * t + u, 1)].rearrange("a p n -> p (a n)"))

            def store(h, stage_, t, u):
                first, _ = stage_
                sp.wait_ge(evacuated, h * TILES + first + t + 1 + CREDIT)
                if stage_ is TX:
                    for v in range(2):
                        sp.dma_start(hx_dram[bass.ds(h, 1), :, bass.ds(t, 1), v * 256:(v + 1) * 256]
                                     .rearrange("a p t n -> p (a t n)"),
                                     stage[:, u, 0, v * 256:(v + 1) * 256]).then_inc(stored[u], 16)
                else:
                    ri = 0 if stage_ is R2 else 1
                    for v in range(2):
                        sp.dma_start(s_dram[ri, v, bass.ds(h * 4, 4), :, bass.ds(t, 1), :]
                                     .rearrange("c p t b -> p c (t b)"),
                                     stage[:, u, v, :].rearrange("p (c b) -> p c b", c=4)).then_inc(stored[u], 16)

            with sp.Fori(0, HALVES) as h:
                with sp.Fori(0, XPIECES // 2) as q:
                    for u in range(2):
                        load(h, 2 * q + u, u, x_t[bass.ds(h, 1), bass.ds(2 * q + u, 1)].rearrange("a b p n -> p (a b n)"))
                with sp.Fori(0, L1) as i:
                    load_tile(h, 2 * i)
                    load_tile(h, 2 * i + 1)
                before = None
                for st in (TX, R2, I2):
                    first, tiles = st
                    load_tile(h, first)
                    load_tile(h, first + 1)
                    if before:
                        for u in range(2):
                            store(h, before, before[1] - 2 + u, u)
                    with sp.Fori(1, tiles // 2) as i:
                        load_tile(h, first + 2 * i)
                        load_tile(h, first + 2 * i + 1)
                        for u in range(2):
                            store(h, st, 2 * i - 2 + u, u)
                    before = st
                for u in range(2):
                    store(h, I2, L2 - 2 + u, u)
            for u in range(2):
                sp.wait_ge(stored[u], 32 * (HALVES * STORES + 1))

        @block.gpsimd
        def _(pool):
            pool.sem_inc(lo_done, CREDIT)
            pool.memset(over_n[:, :], 1.0 / HID).then_inc(consts_set, 1)
            pool.memset(eps[:, :], EPS).then_inc(consts_set, 1)

            def low(h, piece, n, u, dst, hi):
                pool.wait_ge(loaded[u], 16 * (h * (PIECES // 2) + n + 1))
                pool.wait_ge(hi_done, h * PIECES + piece + 1 + CREDIT)
                pool.tensor_tensor(dst, raw[:, u, :], hi.bitcast(F32), ALU.subtract).then_inc(lo_done, 1)

            with pool.Fori(0, HALVES) as h:
                with pool.Fori(0, XPIECES // 2) as q:
                    for u in range(2):
                        low(h, 2 * q + u, q, u,
                            act_lo[:, bass.ds(2 * (2 * q + u), 2), :].rearrange("p a b -> p (a b)"),
                            act_hi[:, bass.ds(2 * (2 * q + u), 2), :].rearrange("p a b -> p (a b)"))
                with pool.Fori(0, TILES) as t:
                    for u in range(2):
                        pool.wait_ge((half_done, tile_done)[u], h * TILES + t + CREDIT)
                        low(h, XPIECES + 2 * t + u, XPIECES // 2 + t, u, w_lo[:, u, :], w_hi[:, u, :])

        @block.scalar
        def _(act):
            act.sem_inc(hi_done, CREDIT)

            def high(h, n, u, dst):
                act.wait_ge(consts_in, 32)
                act.wait_ge(loaded[u], 16 * (h * (PIECES // 2) + n + 1))
                act.activation(dst, raw[:, u, :], ACT.Copy).then_inc(hi_done, 1)

            def high_tile(h, t):
                for u in range(2):
                    act.wait_ge((half_done, tile_done)[u], h * TILES + t + CREDIT)
                    high(h, XPIECES // 2 + t, u, w_hi[:, u, :])

            def square(h, ln, y, j, u):
                at = h * 2 * KT + ln * KT + j
                act.wait_ge(centered, at + 1)
                act.wait_ge(sq_added, at + 1)
                act.wait_ge(consts_in, 32)
                act.activation(ln_tmp[:, u, :], y[:, bass.ds(j, 1), :].rearrange("p a b -> p (a b)"),
                               ACT.Square).then_inc(squared, 1)

            def gelu(h, ln, y, hi, j, u):
                at = h * 2 * KT + ln * KT + j
                act.wait_ge(scaled, at + 1)
                act.wait_ge(h_lo, at + 1)
                act.wait_ge(consts_in, 32)
                act.activation(ln_tmp[:, u, :], y[:, bass.ds(j, 1), :].rearrange("p a b -> p (a b)"), ACT.Gelu,
                               scale=gb[:, ln, 0, bass.ds(j, 1)], bias=gb[:, ln, 1, bass.ds(j, 1)]).then_inc(gelu_done, 1)
                act.wait_ge(consts_in, 32)
                act.wait_ge(gelu_done, at + 1)
                act.activation(hi[:, bass.ds(j, 1), :].rearrange("p a b -> p (a b)"), ln_tmp[:, u, :],
                               ACT.Copy).then_inc(h_hi, 1)

            def with_norm(h, ln, first, y, hi):
                for u in range(2):
                    high_tile(h, first + u)
                with act.Fori(0, 4) as i:
                    for v in range(2):
                        high_tile(h, first + 2 + 2 * i + v)
                        for u in range(2):
                            square(h, ln, y, 4 * i + 2 * v + u, u)
                for u in range(2):
                    high_tile(h, first + 10 + u)
                act.wait_ge(stat_done, 4 * h + 2 * ln + 2)
                act.activation(rstd[:, :], stat[:, :], ACT.Sqrt, bias=eps[:, 0:1]).then_inc(root_done, 1)
                with act.Fori(0, 2) as i:
                    for v in range(2):
                        high_tile(h, first + 12 + 2 * i + v)
                        for u in range(4):
                            gelu(h, ln, y, hi, 8 * i + 4 * v + u, u % 2)

            act.wait_ge(consts_in, 32)
            act.wait_ge(consts_set, 2)
            with act.Fori(0, HALVES) as h:
                act.wait_ge(consts_in, 32)
                act.wait_ge(tile_done, h * TILES + CREDIT)
                with act.Fori(0, XPIECES // 2) as q:
                    for u in range(2):
                        high(h, q, u, act_hi[:, bass.ds(2 * (2 * q + u), 2), :].rearrange("p a b -> p (a b)"))
                with act.Fori(0, L1) as t:
                    high_tile(h, t)
                with_norm(h, 0, I1[0], y_r, hid_hi)
                with act.Fori(0, XP) as t:
                    high_tile(h, TX[0] + t)
                with_norm(h, 1, R2[0], y_i, act_hi)
                with act.Fori(0, L2) as t:
                    high_tile(h, I2[0] + t)

        @block.vector
        def _(dve):
            dve.sem_inc(evacuated, CREDIT)
            dve.sem_inc(sq_added, CREDIT)
            dve.sem_inc(h_lo, CREDIT)
            dve.sem_inc(added, 1)

            def tile2(x, j):
                return x[:, bass.ds(j, 1), :].rearrange("p a b -> p (a b)")

            def evacuate_first(h, st, t, u, ln, y):
                first, _ = st
                dve.wait_ge(cleared, 3 * h + ln + 1)
                dve.wait_ge(tile_done, h * TILES + first + t + 1 + CREDIT)
                dve.tensor_scalar(tile2(y, t), acc[u][:, :], bias[:, bass.ds(first + t, 1)], None,
                                  ALU.add).then_inc(evacuated, 1)
                dve.wait_ge(evacuated, h * TILES + first + t + 1 + CREDIT)
                dve.wait_ge(added, h * 2 * KT + ln * KT + t + 1)
                dve.tensor_tensor(total[:, :], total[:, :], tile2(y, t), ALU.add).then_inc(added, 1)

            def evacuate_second(h, st, t, half_t, u, n0):
                first, _ = st
                dve.wait_ge(tile_done, h * TILES + first + t + 1 + CREDIT)
                dve.wait_ge(stored[u], 32 * (h * STORES + n0 + half_t + 1))
                hi = stage[:, u, 0, :]
                b = bias[:, bass.ds(first + t, 1)]
                dve.tensor_scalar(hi.bitcast(F32R), acc[u][:, :], b, None, ALU.add).then_inc(hi_staged, 1)
                dve.wait_ge(hi_staged, h * 2 * L2 + (first - R2[0]) + t + 1)
                dve.scalar_tensor_tensor(out=stage[:, u, 1, :].bitcast(F32R), in0=acc[u][:, :], scalar=b, in1=hi,
                                         op0=ALU.add, op1=ALU.subtract).then_inc(evacuated, 1)

            def with_norm(h, ln, y, hi, lo, evac):
                s = 4 * h + 2 * ln
                dve.wait_ge(stat_done, s + 1)
                dve.tensor_copy(mean[:, :], stat[:, :]).then_inc(mean_ready, 1)
                dve.memset(total[:, :], 0.0)
                dve.memset(sq_total[:, :], 0.0).then_inc(cleared, 1)
                dve.wait_ge(mean_ready, 2 * h + ln + 1)
                dve.wait_ge(cleared, 3 * h + ln + 2)
                evac(0, 0)
                evac(0, 1)
                at = h * 2 * KT + ln * KT
                with dve.Fori(0, 4) as i:
                    for u in range(4):
                        j = 4 * i + u
                        dve.tensor_tensor(tile2(y, j), tile2(y, j), mean[:, :], ALU.subtract).then_inc(centered, 1)
                    for u in range(4):
                        j = 4 * i + u
                        dve.wait_ge(squared, at + j + 1)
                        dve.wait_ge(sq_added, at + j + CREDIT)
                        dve.tensor_tensor(sq_total[:, :], sq_total[:, :], ln_tmp[:, u % 2, :], ALU.add).then_inc(sq_added, 1)
                    evac(i + 1, 0)
                    evac(i + 1, 1)
                dve.wait_ge(root_done, 2 * h + ln + 1)
                dve.reciprocal(rstd[:, :], rstd[:, :]).then_inc(rstd_ready, 1)
                evac(5, 0)
                evac(5, 1)
                dve.wait_ge(consts_in, 32)
                dve.wait_ge(rstd_ready, 2 * h + ln + 1)
                with dve.Fori(0, 2) as i:
                    for u in range(8):
                        j = 8 * i + u
                        dve.tensor_tensor(tile2(y, j), tile2(y, j), rstd[:, :], ALU.mult).then_inc(scaled, 1)
                    for v in range(2):
                        for u in range(4):
                            j = 8 * i + 4 * v + u
                            dve.wait_ge(h_hi, at + j + 1)
                            dve.tensor_tensor(tile2(lo, j), ln_tmp[:, u % 2, :], tile2(hi, j).bitcast(F32),
                                              ALU.subtract).then_inc(h_lo, 1)
                        evac(i + 6, v)

            dve.wait_ge(consts_in, 32)
            with dve.Fori(0, HALVES) as h:
                dve.memset(total[:, :], 0.0).then_inc(cleared, 1)
                with dve.Fori(0, L1 // 2) as i:
                    for u in range(2):
                        evacuate_first(h, R1, 2 * i + u, u, 0, y_r)
                with_norm(h, 0, y_r, hid_hi, hid_lo, lambda i, u: evacuate_first(h, I1, 2 * i + u, u, 1, y_i))
                with dve.Fori(0, XP // 2) as i:
                    for u in range(2):
                        dve.wait_ge(tile_done, h * TILES + TX[0] + 2 * i + u + 1 + CREDIT)
                        dve.wait_ge(stored[u], 32 * (h * STORES + i + 1))
                        dve.tensor_scalar(stage[:, u, 0, :], acc[u][:, :], bias[:, bass.ds(TX[0] + 2 * i + u, 1)], None,
                                          ALU.add).then_inc(evacuated, 1)
                with_norm(h, 1, y_i, act_hi, act_lo,
                          lambda i, u: evacuate_second(h, R2, 2 * i + u, i, u, XP // 2))
                with dve.Fori(0, L2 // 2) as i:
                    for u in range(2):
                        evacuate_second(h, I2, 2 * i + u, i, u, XP // 2 + L2 // 2)

        @block.tensor
        def _(pe):
            pe.sem_inc(half_done, CREDIT)
            pe.sem_inc(tile_done, CREDIT)

            def multiply(h, t, u, hi, lo):
                pe.wait_ge(evacuated, h * TILES + t + 1)
                for q in range(2):
                    piece = h * PIECES + XPIECES + 2 * t + q
                    pe.wait_ge(hi_done, piece + 1 + CREDIT)
                    pe.wait_ge(lo_done, piece + 1 + CREDIT)
                    for k in range(KT // 2):
                        kk = q * (KT // 2) + k
                        wh, wl = w_hi[:, q, k * P:(k + 1) * P], w_lo[:, q, k * P:(k + 1) * P]
                        pe.matmul(acc[u][:, :], wh, hi[:, kk, :], start=kk == 0, stop=False)
                        pe.matmul(acc[u][:, :], wh, lo[:, kk, :], start=False, stop=False)
                        last = pe.matmul(acc[u][:, :], wl, hi[:, kk, :], start=False, stop=kk == KT - 1)
                    last.then_inc((half_done, tile_done)[q], 1)

            def statistic(src):
                return pe.matmul(stat[:, :], over_n[:, :], src[:, :], start=True, stop=True)

            def with_norm(h, ln, first, hi, lo):
                at = h * 2 * KT + ln * KT
                multiply(h, first, 0, hi, lo)
                pe.wait_ge(added, at + KT + 1)
                statistic(total).then_inc(stat_done, 1)
                multiply(h, first + 1, 1, hi, lo)
                with pe.Fori(1, 5) as i:
                    for u in range(2):
                        multiply(h, first + 2 * i + u, u, hi, lo)
                pe.wait_ge(sq_added, at + KT + CREDIT)
                statistic(sq_total).then_inc(stat_done, 1)
                with pe.Fori(5, 8) as i:
                    for u in range(2):
                        multiply(h, first + 2 * i + u, u, hi, lo)

            pe.wait_ge(consts_set, 2)
            with pe.Fori(0, HALVES) as h:
                with pe.Fori(0, L1 // 2) as i:
                    for u in range(2):
                        multiply(h, 2 * i + u, u, act_hi, act_lo)
                with_norm(h, 0, I1[0], act_hi, act_lo)
                with pe.Fori(0, XP // 2) as i:
                    for u in range(2):
                        multiply(h, TX[0] + 2 * i + u, u, act_hi, act_lo)
                pe.wait_ge(h_lo, h * 2 * KT + KT + CREDIT)
                with_norm(h, 1, R2[0], hid_hi, hid_lo)
                pe.wait_ge(consts_set, 2)
                pe.wait_ge(h_lo, h * 2 * KT + 2 * KT + CREDIT)
                with pe.Fori(0, L2 // 2) as i:
                    for u in range(2):
                        multiply(h, I2[0] + 2 * i + u, u, act_hi, act_lo)


G = 4
GB = P // G
T = N * P
HH = H // 2


def attention(nc, sems, qkv_w, qk_bias, v_bias, ids, tables, st, s_dram, o_dram):
    with ExitStack() as ctx:
        def sb(name, shape, dt=F32):
            return ctx.enter_context(nc.sbuf_tensor(name, shape, dt))

        def sem(name):
            return sems.enter_context(nc.semaphore(name))

        def ps(name, shape):
            return ctx.enter_context(nc.psum_tensor(name, shape, F32))

        wt_hi = sb("wt_hi", [P, 6, DT, D], F32R)
        wt_lo = sb("wt_lo", [P, 6, DT, D], F32R)
        s_hi = sb("s_hi", [P, 2, DT, T], F32R)
        s_lo = sb("s_lo", [P, 2, DT, T], F32R)
        q2 = sb("q2", [P, HH, 2, T])
        ks = sb("ks", [P, HH, T])
        v = sb("v", [P, G, H, 2, HD])
        pt = sb("pt", [P, G * HH, P])
        o_out = sb("o_out", [P, 2, HH, T])
        masked = sb("masked", [P, 2, 16, GB])
        vb = sb("vb", [P, 2, D])
        ids_sb = sb("ids_sb", [P, CH, N], mybir.dt.int32)
        qkb = sb("qkb", [P, 4, DT])
        neg_b = sb("neg_b", [P, DT])
        ident = sb("ident", [P, P])
        mask = sb("mask", [P, GB])
        sc = sb("sc", [P, G, 2, 2, 2, N])
        sc_sq = sb("sc_sq", [P, G * HH, 2, N])
        mag2 = sb("mag2", [P, G * HH, N])
        mag = sb("mag", [P, G * HH * N])
        top = sb("top", [G * HH * N, GB])
        ex = sb("ex", [G * HH * N, N, GB])
        den = sb("den", [G * HH * N, GB])
        w_t = sb("w_t", [P, G * HH * N])
        tiny = sb("tiny", [P, 1])
        proj = [ps(f"proj{u}", [P, T]) for u in range(2)]
        scp = [ps(f"scp{u}", [P, T]) for u in range(2)]
        avp = [ps(f"avp{u}", [P, T]) for u in range(2)]
        tp = ps("tp", [P, T])
        R = G * HH * N
        raw = v[:, :, :, :, :].rearrange("p g h r d -> p (g h r d)").rearrange("p (u n) -> p u n", u=2)

        w_in = [sem(f"w_in{u}") for u in range(2)]
        w_hi_done = sem("w_hi_done")
        w_lo_done = sem("w_lo_done")
        small_in = sem("small_in")
        ids_in = sem("ids_in")
        gathered = sem("gathered")
        neg_set = sem("neg_set")
        s_in = sem("s_in")
        proj_done = sem("proj_done")
        even_out = sem("even_out")
        odd_out = sem("odd_out")
        score_done = sem("score_done")
        score_masked = sem("score_masked")
        score_out = sem("score_out")
        squared2 = sem("squared2")
        mag2_set = sem("mag2_set")
        mag_set = sem("mag_set")
        mag_turned = sem("mag_turned")
        top_set = sem("top_set")
        less_top = sem("less_top")
        exp_set = sem("exp_set")
        den_set = sem("den_set")
        den_inv = sem("den_inv")
        prob_set = sem("prob_set")
        prob_turned = sem("prob_turned")
        w_t_set = sem("w_t_set")
        pt_set = sem("pt_set")
        av_done = sem("av_done")
        o_set = sem("o_set")
        o_stored = [sem(f"o_stored{u}") for u in range(2)]
        set_up = sem("set_up")

        block = ctx.enter_context(nc.Block())
        QK0, V0, QK1, PER = 0, 8, 16, 24
        qk_at = (QK0, QK1)

        @block.sync
        def _(sp):
            sp.dma_start(qkb[:, :, :], qk_bias).then_inc(small_in, 16)
            sp.dma_start(ids_sb[:, :, :], ids).then_inc(ids_in, 16)
            sp.dma_start(vb[:, :, :], v_bias.partition_broadcast(P)).then_inc(small_in, 16)
            for u in range(2):
                sp.sem_inc(o_stored[u], 64)
            for m in range(6):
                if m >= 2:
                    sp.wait_ge(w_hi_done, m - 1)
                    sp.wait_ge(w_lo_done, m - 1)
                sp.dma_start(raw[:, m % 2, :], qkv_w[m]).then_inc(w_in[m % 2], 16)

            def load_s(c):
                for r in range(2):
                    for x, t in ((0, s_hi), (1, s_lo)):
                        sp.dma_start(t[:, r].rearrange("p d t -> p (d t)").bitcast(F32),
                                     s_dram[r, x, bass.ds(c, 1)].rearrange("c p t b -> p (c t b)")).then_inc(s_in, 16)

            def store_o(c, hh):
                sp.wait_ge(o_set, 8 * c + 4 * hh + 4 + CREDIT)
                for r in range(2):
                    for par in range(2):
                        sp.dma_start(o_dram[r, hh, bass.ds(c, 1), par * HD:(par + 1) * HD].rearrange("c p d t -> p (c d) t"),
                                     o_out[r * HD:(r + 1) * HD, hh].rearrange("p (d a) t -> p a d t", a=2)[:, par]
                                     ).then_inc(o_stored[hh], 16)

            load_s(0)
            with sp.Fori(1, CH) as c:
                sp.wait_ge(proj_done, PER * c)
                load_s(c)
                store_o(c - 1, 0)
                store_o(c - 1, 1)
            store_o(CH - 1, 0)
            store_o(CH - 1, 1)
            for u in range(2):
                sp.wait_ge(o_stored[u], 64 * (CH + 1))

        @block.gpsimd
        def _(pool):
            pool.memset(tiny[:, :], 1e-8)
            pool.memset(ident[:, :], 0.0).then_inc(set_up, 1)
            pool.wait_ge(set_up, 1)
            pool.affine_select(out=ident[:, :], in_=ident[:, :], compare_op=ALU.not_equal, fill=1.0,
                               base=0, pattern=[[-1, P]], channel_multiplier=1).then_inc(set_up, 1)
            for m in range(6):
                pool.wait_ge(w_in[m % 2], 16 * (m // 2 + 1))
                pool.wait_ge(w_hi_done, m + 1)
                pool.tensor_tensor(wt_lo[:, m].rearrange("p k n -> p (k n)"), raw[:, m % 2, :],
                                   wt_hi[:, m].rearrange("p k n -> p (k n)").bitcast(F32), ALU.subtract).then_inc(w_lo_done, 1)

            def expand(c, hh):
                pool.wait_ge(av_done, 8 * c + 4 * hh)
                pool.wait_ge(w_t_set, 2 * c + hh + 1)
                pool.tensor_tensor(pt[:, :, :].rearrange("p a (n b) -> p (a n) b", b=GB),
                                   w_t[:, :].unsqueeze(2).broadcast_to([P, R, GB]),
                                   mask[:, :].unsqueeze(1).broadcast_to([P, R, GB]), ALU.mult).then_inc(pt_set, 1)

            pool.wait_ge(ids_in, 16)
            for c in range(CH):
                for n in range(N):
                    pool.indirect_dma_start(out=st[:, c, n, :], out_offset=None, in_=tables[n],
                                            in_offset=bass.IndirectOffsetOnAxis(ap=ids_sb[:, c, n:n + 1], axis=0)
                                            ).then_inc(gathered, 16)
            pool.wait_ge(set_up, 3)
            expand(0, 0)
            expand(0, 1)
            with pool.Fori(1, CH) as c:
                expand(c, 0)
                expand(c, 1)
            pool.wait_ge(gathered, 16 * CH * N)

        @block.scalar
        def _(act):
            act.sem_inc(even_out, CREDIT)
            act.sem_inc(o_set, CREDIT)
            for m in range(6):
                act.wait_ge(w_in[m % 2], 16 * (m // 2 + 1))
                act.activation(wt_hi[:, m].rearrange("p k n -> p (k n)"), raw[:, m % 2, :], ACT.Copy).then_inc(w_hi_done, 1)
            act.wait_ge(small_in, 32)
            act.activation(neg_b[:, :], qkb[:, 0, :], ACT.Copy, scale=-1.0).then_inc(neg_set, 1)
            act.wait_ge(neg_set, 1)
            act.wait_ge(set_up, 3)

            def take_even(c, hh, i):
                j, kind = i // 4, i % 4
                act.wait_ge(proj_done, PER * c + qk_at[hh] + i + 1)
                src = proj[i % 2][0:HD, :].rearrange("p (t g) -> p g t", g=G)
                b = qkb[0:HD, kind, 2 * hh + j:2 * hh + j + 1]

                def to(x):
                    return x.rearrange("p (g t) -> p g t", g=G)

                h = 2 * j
                if kind == 0:
                    act.activation(to(q2[0:HD, h, 0]), src, ACT.Identity, bias=b)
                    act.activation(to(q2[HD:P, h, 1]), src, ACT.Identity, scale=-1.0,
                                   bias=neg_b[0:HD, 2 * hh + j:2 * hh + j + 1]).then_inc(even_out, 1)
                elif kind == 1:
                    act.activation(to(q2[HD:P, h, 0]), src, ACT.Identity, bias=b)
                    act.activation(to(q2[0:HD, h, 1]), src, ACT.Identity, bias=b).then_inc(even_out, 1)
                else:
                    row = (kind - 2) * HD
                    act.activation(to(ks[row:row + HD, h]), src, ACT.Identity, bias=b).then_inc(even_out, 1)

            def qk(c, hh, n=None):
                if n is not None:
                    act.wait_ge(mag2_set, n + 1)
                    act.activation(mag[:, :], mag2[:, :, :].rearrange("p a n -> p (a n)"), ACT.Sqrt,
                                   bias=tiny[:, 0:1]).then_inc(mag_set, 1)
                for i in range(8):
                    take_even(c, hh, i)
                    if i == 1 and n is not None:
                        exponent(n)

            def exponent(n):
                act.wait_ge(less_top, n + 1)
                act.activation(ex[:, :, :], ex[:, :, :], ACT.Exp, scale=HD ** -0.5).then_inc(exp_set, 1)

            def take_o(c, hh, g):
                act.wait_ge(av_done, 8 * c + 4 * hh + g + 1)
                if g == 0:
                    act.wait_ge(o_stored[hh], 64 * (c + 1))
                act.activation(o_out[:, hh, :, g:T:G], avp[g % 2][:, :].rearrange("p (h t) -> p h t", h=HH), ACT.Copy).then_inc(o_set, 1)

            def body(c, last):
                qk(c, 1, 2 * c)
                for g in range(G):
                    take_o(c, 0, g)
                if not last:
                    qk(c + 1, 0, 2 * c + 1)
                else:
                    act.wait_ge(mag2_set, 2 * c + 2)
                    act.activation(mag[:, :], mag2[:, :, :].rearrange("p a n -> p (a n)"), ACT.Sqrt,
                                   bias=tiny[:, 0:1]).then_inc(mag_set, 1)
                    exponent(2 * c + 1)
                for g in range(G):
                    take_o(c, 1, g)

            qk(0, 0)
            with act.Fori(0, CH - 1) as c:
                body(c, False)
            body(CH - 1, True)

        @block.vector
        def _(dve):
            dve.sem_inc(odd_out, CREDIT)
            dve.sem_inc(score_out, CREDIT)
            dve.wait_ge(set_up, 2)
            dve.tensor_reduce(mask[:, :], ident[:, :].rearrange("p (m b) -> p b m", m=N), AX_X, ALU.add).then_inc(set_up, 1)
            dve.wait_ge(small_in, 32)
            dve.wait_ge(set_up, 3)

            def take_odd(c, hh, i):
                j, kind = i // 4, i % 4
                dve.wait_ge(proj_done, PER * c + qk_at[hh] + i + 1)
                src = proj[i % 2][HD:P, :].rearrange("p (t g) -> p g t", g=G)
                b = qkb[HD:P, kind, 2 * hh + j:2 * hh + j + 1]

                def to(x):
                    return x.rearrange("p (g t) -> p g t", g=G)

                h = 2 * j + 1
                if kind == 0:
                    dve.tensor_scalar(to(q2[0:HD, h, 0]), src, b, None, ALU.add)
                    dve.tensor_scalar(to(q2[HD:P, h, 1]), src, b, -1.0, ALU.add, ALU.mult).then_inc(odd_out, 1)
                elif kind == 1:
                    dve.tensor_scalar(to(q2[HD:P, h, 0]), src, b, None, ALU.add)
                    dve.tensor_scalar(to(q2[0:HD, h, 1]), src, b, None, ALU.add).then_inc(odd_out, 1)
                else:
                    row = (kind - 2) * HD
                    dve.tensor_scalar(to(ks[row:row + HD, h]), src, b, None, ALU.add).then_inc(odd_out, 1)

            def take_v(c, i):
                g, r = i // 2, i % 2
                dve.wait_ge(proj_done, PER * c + V0 + i + 1)
                dve.tensor_tensor(v[:, g, :, r, :], proj[i % 2][:, :].rearrange("p (h d) -> p h d", h=H),
                                  vb[:, r].rearrange("p (h d) -> p h d", h=H), ALU.add).then_inc(odd_out, 1)

            def take_scores(c, hh, i):
                n = 16 * c + 8 * hh + i
                dve.wait_ge(score_done, n + 1)
                dve.tensor_tensor(masked[:, i % 2], scp[i % 2][:, :].rearrange("p (a b) -> p a b", b=GB),
                                  mask[:, :].unsqueeze(1).broadcast_to([P, 16, GB]), ALU.mult).then_inc(score_masked, 1)
                dve.wait_ge(score_masked, n + 1)
                dve.tensor_reduce(sc[:, i // 2, i % 2].rearrange("p h x n -> p (h x n)"), masked[:, i % 2],
                                  AX_X, ALU.add).then_inc(score_out, 1)

            def magnitudes(n):
                dve.wait_ge(score_out, 8 * n + 8 + CREDIT)
                s = sc[:, :, :, :, :, :].rearrange("p g a h x n -> p (g a h) x n")
                dve.tensor_tensor(sc_sq[:, :, :, :], s, s, ALU.mult).then_inc(squared2, 1)
                dve.wait_ge(squared2, n + 1)
                dve.tensor_tensor(mag2[:, :, :], sc_sq[:, :, 0, :], sc_sq[:, :, 1, :], ALU.add).then_inc(mag2_set, 1)

            def less_maximum(n):
                dve.wait_ge(mag_turned, n + 1)
                turned = tp[0:R, 0:P]
                dve.tensor_reduce(top[:, :], turned.rearrange("p (m b) -> p b m", m=N), AX_X, ALU.max).then_inc(top_set, 1)
                dve.wait_ge(top_set, n + 1)
                dve.tensor_tensor(ex[:, :, :], turned.rearrange("p (m b) -> p m b", m=N),
                                  top[:, :].unsqueeze(1).broadcast_to([R, N, GB]), ALU.subtract).then_inc(less_top, 1)

            def normalize(n):
                dve.wait_ge(exp_set, n + 1)
                dve.tensor_reduce(den[:, :], ex[:, :, :].rearrange("p m b -> p b m"), AX_X, ALU.add).then_inc(den_set, 1)
                dve.wait_ge(den_set, n + 1)
                dve.reciprocal(den[:, :], den[:, :]).then_inc(den_inv, 1)
                dve.wait_ge(den_inv, n + 1)
                dve.tensor_tensor(ex[:, :, :], ex[:, :, :], den[:, :].unsqueeze(1).broadcast_to([R, N, GB]),
                                  ALU.mult).then_inc(prob_set, 1)

            def keep_turned(n):
                dve.wait_ge(prob_turned, n + 1)
                dve.wait_ge(pt_set, n)
                dve.tensor_copy(w_t[:, :], tp[:, P:P + R]).then_inc(w_t_set, 1)

            def qk(c, hh, n=None):
                for i in range(8):
                    take_odd(c, hh, i)
                    if n is not None:
                        if i == 1:
                            less_maximum(n)
                        if i == 2:
                            normalize(n)
                        if i == 3:
                            keep_turned(n)

            def body(c, last):
                for i in range(8):
                    take_v(c, i)
                    take_scores(c, 0, i)
                magnitudes(2 * c)
                qk(c, 1, 2 * c)
                for i in range(8):
                    take_scores(c, 1, i)
                magnitudes(2 * c + 1)
                if not last:
                    qk(c + 1, 0, 2 * c + 1)
                else:
                    less_maximum(2 * c + 1)
                    normalize(2 * c + 1)
                    keep_turned(2 * c + 1)

            qk(0, 0)
            with dve.Fori(0, CH - 1) as c:
                body(c, False)
            body(CH - 1, True)

        @block.tensor
        def _(pe):
            pe.wait_ge(set_up, 3)

            def three(out, a_hi, a_lo, b_hi, b_lo, first, last):
                pe.matmul(out, a_hi, b_hi, start=first, stop=False)
                pe.matmul(out, a_hi, b_lo, start=False, stop=False)
                return pe.matmul(out, a_lo, b_hi, start=False, stop=last)

            def bank_free(c, stage, i):
                pe.wait_ge(odd_out, PER * c + stage + i - 1 + CREDIT)
                if stage == V0:
                    pe.wait_ge(even_out, 16 * c + min(7 + i, 8) + CREDIT)
                else:
                    at = 16 * c + (8 if stage == QK1 else 0)
                    pe.wait_ge(even_out, at + (max(i - 1, 0) if stage == QK1 else i - 1) + CREDIT)

            def qk_tile(c, hh, i):
                j, kind = i // 4, i % 4
                e = (2 * hh + j) * P
                r = kind % 2
                bank_free(c, qk_at[hh], i)
                for k in range(DT):
                    last = three(proj[i % 2][:, :], wt_hi[:, kind, k, e:e + P], wt_lo[:, kind, k, e:e + P],
                                 s_hi[:, r, k, :], s_lo[:, r, k, :], k == 0, k == DT - 1)
                last.then_inc(proj_done, 1)

            def v_tile(c, i):
                g, r = i // 2, i % 2
                bank_free(c, V0, i)
                for k in range(DT):
                    last = three(proj[i % 2][:, :], s_hi[:, r, k, g:T:G], s_lo[:, r, k, g:T:G],
                                 wt_hi[:, 4 + r, k, :], wt_lo[:, 4 + r, k, :], k == 0, k == DT - 1)
                last.then_inc(proj_done, 1)

            def scores(c, hh, i):
                g = i // 2
                n = 16 * c + 8 * hh + i
                if i == 0:
                    pe.wait_ge(odd_out, PER * c + qk_at[hh] + 8 + CREDIT)
                    pe.wait_ge(even_out, 16 * c + 8 * hh + 8 + CREDIT)
                pe.wait_ge(score_out, n - 1 + CREDIT)
                for a in range(2):
                    h = 2 * (i % 2) + a
                    last = pe.matmul(scp[i % 2][:, a * 2 * P:(a + 1) * 2 * P], ks[:, h, g * P:(g + 1) * P],
                                     q2[:, h, :, g * P:(g + 1) * P], start=a == 0, stop=a == 1, skip_group_check=True)
                last.then_inc(score_done, 1)

            def turn_magnitudes(n):
                pe.wait_ge(mag_set, n + 1)
                pe.matmul(tp[0:R, 0:P], mag[:, :], ident[:, :], start=True, stop=True).then_inc(mag_turned, 1)

            def turn_probabilities(n):
                pe.wait_ge(set_up, 3)
                pe.wait_ge(prob_set, n + 1)
                pe.transpose(tp[:, P:P + R], ex[:, :, :].rearrange("p m b -> p (m b)"), ident[0:R, 0:R]).then_inc(prob_turned, 1)

            def attend(c, hh, g):
                if g == 0:
                    pe.wait_ge(pt_set, 2 * c + hh + 1)
                    pe.wait_ge(odd_out, PER * c + V0 + 8 + CREDIT)
                n = 8 * c + 4 * hh + g
                pe.wait_ge(o_set, n - 1 + CREDIT)
                for a in range(HH):
                    last = pe.matmul(avp[g % 2][:, a * P:(a + 1) * P],
                                     v[:, g, HH * hh + a].rearrange("p r d -> p (r d)"),
                                     pt[:, g * HH + a, :], start=a == 0, stop=a == HH - 1, skip_group_check=True)
                last.then_inc(av_done, 1)

            def qk(c, hh, n=None):
                if hh == 0:
                    pe.wait_ge(s_in, 64 * (c + 1))
                for i in range(8):
                    qk_tile(c, hh, i)
                    if n is not None:
                        if i == 1:
                            turn_magnitudes(n)
                        if i == 3:
                            turn_probabilities(n)

            def body(c, last):
                for i in range(8):
                    v_tile(c, i)
                    scores(c, 0, i)
                qk(c, 1, 2 * c)
                for i in range(8):
                    scores(c, 1, i)
                    if i % 2:
                        attend(c, 0, i // 2)
                if not last:
                    qk(c + 1, 0, 2 * c + 1)
                else:
                    turn_magnitudes(2 * c + 1)
                    turn_probabilities(2 * c + 1)
                for g in range(G):
                    attend(c, 1, g)

            pe.wait_ge(w_hi_done, 6)
            pe.wait_ge(w_lo_done, 6)
            qk(0, 0)
            with pe.Fori(0, CH - 1) as c:
                body(c, False)
            body(CH - 1, True)


def interact(nc, sems, wo_w, wo_bias, int_w, o_dram, z_dram):
    UNITS = HALVES * N
    MAT = DT * D
    BT = HB // P

    with ExitStack() as ctx:
        def sb(name, shape, dt=F32):
            return ctx.enter_context(nc.sbuf_tensor(name, shape, dt))

        def sem(name):
            return sems.enter_context(nc.semaphore(name))

        wo_hi = sb("wo_hi", [P, 2, MAT], F32R)
        wo_lo = sb("wo_lo", [P, 2, MAT], F32R)
        o_raw = sb("o_raw", [P, DT, HB])
        o_hi = sb("o_hi", [P, 2, DT, HB], F32R)
        o_lo = sb("o_lo", [P, 2, DT, HB], F32R)
        w_raw = sb("w_raw", [P, 2, MAT])
        m_hi = sb("m_hi", [P, 3, MAT], F32R)
        m_lo = sb("m_lo", [P, 3, MAT], F32R)
        a_hi = sb("a_hi", [P, 3, DT, HB], F32R)
        a_lo = sb("a_lo", [P, 3, DT, HB], F32R)
        comb = sb("comb", [P, MAT // 2])
        a_raw = sb("a_raw", [P, 3, HB])
        k1 = sb("k1", [P, 2, D])
        z_out = sb("z_out", [P, 2, 2, D])
        wo_b = sb("wo_b", [P, 2, DT])
        wops = [ctx.enter_context(nc.psum_tensor(f"wops{u}", [P, HB], F32)) for u in range(2)]
        kps = [[ctx.enter_context(nc.psum_tensor(f"kps{u}{x}", [P, D], F32)) for x in range(3)] for u in range(2)]

        wo_in = [sem(f"wo_in{u}") for u in range(2)]
        small_in = sem("small_in3")
        wo_hi_done = sem("wo_hi_done")
        wo_lo_done = sem("wo_lo_done")
        o_in = sem("o_in")
        w_in = sem("w_in3")
        o_hi_done = sem("o_hi_done")
        o_lo_done = sem("o_lo_done")
        comb_set = sem("comb_set")
        m_hi_done = sem("m_hi_done")
        m_lo_done = sem("m_lo_done")
        dve_split = sem("dve_split")
        wo_done = sem("wo_done")
        a_raw_set = sem("a_raw_set")
        a_sum_set = sem("a_sum_set")
        a_hi_done = sem("a_hi_done")
        a_lo_done = sem("a_lo_done")
        k_done = sem("k_done")
        k1_out = sem("k1_out")
        z_set = sem("z_set")
        z_stored = [sem(f"z_stored{u}") for u in range(2)]

        block = ctx.enter_context(nc.Block())

        @block.sync
        def _(sp):
            sp.dma_start(wo_b[:, :, :], wo_bias).then_inc(small_in, 16)
            for u in range(2):
                sp.dma_start(w_raw[:, u, :], wo_w[u]).then_inc(wo_in[u], 16)
                sp.sem_inc(z_stored[u], 32)

            def load_o(h, n, r):
                for hh in range(2):
                    for d in range(2):
                        sp.dma_start(o_raw[:, 2 * hh + d, :].rearrange("p (c b) -> p c b", b=P),
                                     o_dram[r, hh, bass.ds(h * BT, BT), :, d, bass.ds(n * P, P)]
                                     .rearrange("c p b -> p c b")).then_inc(o_in, 16)

            def load_w(n):
                for r in range(2):
                    sp.dma_start(w_raw[:, r, :], int_w[r, bass.ds(n, 1)].rearrange("n p m -> p (n m)")).then_inc(w_in, 16)

            def store(h, n, k):
                for m in range(BT):
                    sp.wait_ge(z_set, 2 * BT * k + 2 * m + 2)
                    sp.dma_start(z_dram[bass.ds(h * BT + m, 1), :, :, bass.ds(n, 1), :].rearrange("c b r n d -> b (c r) (n d)"),
                                 z_out[:, m % 2, :, :]).then_inc(z_stored[m % 2], 32)

            load_o(0, 0, 0)
            sp.wait_ge(o_hi_done, 1)
            sp.wait_ge(o_lo_done, 1)
            load_o(0, 0, 1)
            for u in range(2):
                sp.wait_ge(wo_hi_done, 2)
                sp.wait_ge(wo_lo_done, 2)
            load_w(0)

            def unit(h, n, h1, n1, last):
                k = h * N + n
                if not last:
                    for r in range(2):
                        sp.wait_ge(o_hi_done, 2 * k + r + 2)
                        sp.wait_ge(o_lo_done, 2 * k + r + 2)
                        load_o(h1, n1, r)
                        if r == 0:
                            sp.wait_ge(m_lo_done, k + 1)
                            sp.wait_ge(dve_split, 4 * k + 4)
                            load_w(n1)
                store(h, n, k)

            for h in range(HALVES):
                with sp.Fori(0, N - 1) as n:
                    unit(h, n, h, n + 1, False)
                unit(h, N - 1, h + 1, 0, h == HALVES - 1)
            for u in range(2):
                sp.wait_ge(z_stored[u], 32 * (UNITS * BT // 2 + 1))

        @block.gpsimd
        def _(pool):
            for u in range(2):
                pool.wait_ge(wo_hi_done, u + 1)
                pool.tensor_tensor(wo_lo[:, u, :], w_raw[:, u, :], wo_hi[:, u, :].bitcast(F32), ALU.subtract).then_inc(wo_lo_done, 1)

            def unit(k):
                pool.wait_ge(m_hi_done, 5 * k + 1)
                pool.tensor_tensor(m_lo[:, 0, :], w_raw[:, 0, :], m_hi[:, 0, :].bitcast(F32), ALU.subtract).then_inc(m_lo_done, 1)

            def split_o(k):
                for r in range(2):
                    pool.wait_ge(o_hi_done, 2 * k + r + 1)
                    pool.tensor_tensor(o_lo[:, r].rearrange("p a b -> p (a b)"), o_raw[:, :, :].rearrange("p a b -> p (a b)"),
                                       o_hi[:, r].rearrange("p a b -> p (a b)").bitcast(F32), ALU.subtract).then_inc(o_lo_done, 1)

            split_o(0)
            with pool.Fori(0, UNITS - 1) as k:
                unit(k)
                split_o(k + 1)
            unit(UNITS - 1)

        @block.scalar
        def _(act):
            act.wait_ge(small_in, 16)
            for u in range(2):
                act.wait_ge(wo_in[u], 16)
                act.activation(wo_hi[:, u, :], w_raw[:, u, :], ACT.Copy).then_inc(wo_hi_done, 1)

            def split_o(k):
                act.wait_ge(wo_done, 2 * DT * k)
                for r in range(2):
                    act.wait_ge(o_in, 64 * (2 * k + r + 1))
                    act.activation(o_hi[:, r].rearrange("p a b -> p (a b)"), o_raw[:, :, :].rearrange("p a b -> p (a b)"),
                                   ACT.Copy).then_inc(o_hi_done, 1)

            def split_m(k):
                act.wait_ge(w_in, 32 * (k + 1))
                act.wait_ge(k_done, BT * k)
                act.activation(m_hi[:, 0, :], w_raw[:, 0, :], ACT.Copy).then_inc(m_hi_done, 1)
                for x in range(1, 3):
                    for c in range(2):
                        act.wait_ge(comb_set, 4 * k + 2 * (x - 1) + c + 1)
                        act.activation(m_hi[:, x, c * MAT // 2:(c + 1) * MAT // 2], comb[:, :], ACT.Copy).then_inc(m_hi_done, 1)

            def project(k, j):
                for r in range(2):
                    act.wait_ge(wo_done, 2 * DT * k + 2 * j + r + 1)
                    if r == 0:
                        act.wait_ge(a_lo_done, 3 * DT * k + 3 * j)
                    act.activation(a_raw[:, 1 + r, :], wops[r][:, :], ACT.Identity,
                                   bias=wo_b[:, r, j:j + 1]).then_inc(a_raw_set, 1)
                at = 3 * DT * k + 3 * j
                act.wait_ge(a_raw_set, 2 * DT * k + 2 * j + 2)
                act.activation(a_hi[:, 1, j, :], a_raw[:, 1, :], ACT.Copy).then_inc(a_hi_done, 1)
                act.activation(a_hi[:, 2, j, :], a_raw[:, 2, :], ACT.Copy).then_inc(a_hi_done, 1)
                act.wait_ge(a_sum_set, DT * k + j + 1)
                act.activation(a_hi[:, 0, j, :], a_raw[:, 0, :], ACT.Copy).then_inc(a_hi_done, 1)

            def take_k1(k, m):
                act.wait_ge(k_done, BT * k + m + 1)
                if m >= 2:
                    act.wait_ge(z_set, 2 * BT * k + 2 * m - 2)
                act.activation(k1[:, m % 2, :], kps[m % 2][0][:, :], ACT.Copy).then_inc(k1_out, 1)

            def unit(k, last):
                split_m(k)
                for j in range(DT):
                    project(k, j)
                if not last:
                    split_o(k + 1)
                for m in range(BT):
                    take_k1(k, m)

            split_o(0)
            with act.Fori(0, UNITS - 1) as k:
                unit(k, False)
            unit(UNITS - 1, True)

        @block.vector
        def _(dve):
            def unit(k):
                dve.wait_ge(w_in, 32 * (k + 1))
                for x, (i0, i1, op) in ((1, (1, 0, ALU.subtract)), (2, (0, 1, ALU.add))):
                    for c in range(2):
                        cols = slice(c * MAT // 2, (c + 1) * MAT // 2)
                        done = 2 * (x - 1) + c
                        dve.wait_ge(dve_split, 4 * k + done)
                        dve.tensor_tensor(comb[:, :], w_raw[:, i0, cols], w_raw[:, i1, cols], op).then_inc(comb_set, 1)
                        dve.wait_ge(m_hi_done, 5 * k + done + 2)
                        dve.tensor_tensor(m_lo[:, x, cols], comb[:, :], m_hi[:, x, cols].bitcast(F32), ALU.subtract).then_inc(dve_split, 1)
                for j in range(DT):
                    dve.wait_ge(a_raw_set, 2 * DT * k + 2 * j + 2)
                    dve.tensor_tensor(a_raw[:, 0, :], a_raw[:, 1, :], a_raw[:, 2, :], ALU.add).then_inc(a_sum_set, 1)
                    for n, x in enumerate((1, 2, 0)):
                        dve.wait_ge(a_hi_done, 3 * DT * k + 3 * j + n + 1)
                        dve.tensor_tensor(a_lo[:, x, j, :], a_raw[:, x, :], a_hi[:, x, j, :].bitcast(F32),
                                          ALU.subtract).then_inc(a_lo_done, 1)
                for m in range(BT):
                    u = m % 2
                    dve.wait_ge(k1_out, BT * k + m + 1)
                    dve.wait_ge(z_stored[u], 32 * (BT // 2 * k + m // 2 + 1))
                    dve.tensor_tensor(z_out[:, u, 0, :], k1[:, u, :], kps[u][2][:, :], ALU.subtract).then_inc(z_set, 1)
                    dve.tensor_tensor(z_out[:, u, 1, :], k1[:, u, :], kps[u][1][:, :], ALU.add).then_inc(z_set, 1)

            with dve.Fori(0, UNITS) as k:
                unit(k)

        @block.tensor
        def _(pe):
            def three(out, a_h, a_l, b_h, b_l, first, last):
                pe.matmul(out, a_h, b_h, start=first, stop=False)
                pe.matmul(out, a_h, b_l, start=False, stop=False)
                return pe.matmul(out, a_l, b_h, start=False, stop=last)

            def unit(k):
                pe.wait_ge(o_lo_done, 2 * k + 2)
                for j in range(DT):
                    for r in range(2):
                        pe.wait_ge(a_raw_set, 2 * DT * k + 2 * j + r - 1 if j else 2 * DT * k)
                        for d in range(DT):
                            w = slice(d * D + j * P, d * D + (j + 1) * P)
                            last = three(wops[r][:, :], wo_hi[:, r, w], wo_lo[:, r, w], o_hi[:, r, d, :], o_lo[:, r, d, :],
                                         d == 0, d == DT - 1)
                        last.then_inc(wo_done, 1)
                pe.wait_ge(m_lo_done, k + 1)
                pe.wait_ge(dve_split, 4 * k + 4)
                pe.wait_ge(a_lo_done, 3 * DT * (k + 1))
                for m in range(BT):
                    pe.wait_ge(z_set, 2 * BT * k + 2 * m - 2 if m >= 2 else 2 * BT * k)
                    for x in range(3):
                        for d in range(DT):
                            b = slice(m * P, (m + 1) * P)
                            w = slice(d * D, (d + 1) * D)
                            last = three(kps[m % 2][x][:, :], a_hi[:, x, d, b], a_lo[:, x, d, b], m_hi[:, x, w], m_lo[:, x, w],
                                         d == 0, d == DT - 1)
                    last.then_inc(k_done, 1)

            pe.wait_ge(wo_lo_done, 2)
            with pe.Fori(0, UNITS) as k:
                unit(k)


LEAST = 1e-34


def finish(nc, sems, st, meas_w, post_w, post_rows, top1_w, top2_w, top3_w, top2_b, z_dram, hx_dram, out):
    PAIRS = [(0, 1), (1, 2), (2, 3), (0, 2), (1, 3), (0, 3)]
    SHIFTS = [(1, 0, 3), (2, 3, 5), (3, 5, 6)]
    pair_of = {frozenset(p): n for n, p in enumerate(PAIRS)}
    MAT = DT * D
    T1 = 512 // P
    T2 = 256 // P
    DH = D // 2
    BASE = 2

    with ExitStack() as ctx:
        def sb(name, shape, dt=F32):
            return ctx.enter_context(nc.sbuf_tensor(name, shape, dt))

        def sem(name):
            return sems.enter_context(nc.semaphore(name))

        def ps(name):
            return ctx.enter_context(nc.psum_tensor(name, [P, 512], F32))

        z = sb("z", [P, 2, 2, 2, N, DH])
        unit = sb("unit", [P, 2, 2, N, DH])
        p2 = sb("p2", [P, N, DH])
        root = sb("root", [P, N, DH])
        both = sb("both", [P, N // 2, DH])
        flag = sb("flag", [P, 2, N, DH])
        cos = sb("cos", [P, 2, 6, DH])
        part = sb("part", [P, 6, DH])
        coef = sb("coef", [P, 2, N, DH])
        sup_t = sb("sup_t", [P, 3, D])
        sup_sq = sb("sup_sq", [P, 2, D])
        inv = sb("inv", [P, 1])
        m_sq = sb("m_sq", [P, 2, D])
        amp = sb("amp", [P, D])
        amp_t = sb("amp_t", [P, D])
        y = sb("y", [P, D])
        stats = sb("stats", [P, 6])
        mv = sb("mv", [P, 2])
        rs = sb("rs", [P, 1])
        z_t = sb("z_t", [P, DT, B])
        ident = sb("ident4", [P, P])
        ones = sb("ones4", [P, 1])
        eps = sb("eps4", [P, 1])
        least = sb("least4", [P, 1])
        mw = sb("mw", [P, 2, MAT])
        pw = sb("pw", [P, MAT])
        rows = sb("rows", [P, 3, D])
        w1 = sb("w1", [P, MAT])
        w2 = sb("w2", [P, DT, 256])
        w3 = sb("w3", [P, T2])
        b2 = sb("b2", [P, T2])
        hx = sb("hx", [P, HALVES, T1, HB])
        h1 = sb("h1", [P, T1, HB])
        h2 = sb("h2", [P, T2, HB])
        y_out = sb("y_out", [1, HALVES, HB])
        turn = [ps("turn_r"), ps("turn_i")]
        mea = [ps("mea_r"), ps("mea_i")]
        ampp, postp, zp = ps("ampp"), ps("postp"), ps("zp")
        ssp = ps("ssp")

        z_in = [[sem(f"z_in{v}{h}") for h in range(2)] for v in range(2)]
        made = sem("made")
        names = ("z_sq p2_set flag_set p_root both_set both_inv p_inv unit_set cos1 part1 part2 part3 cos_set coef0 coef1 coef2 "
                 "prod_set sup_turned sup_t_set sup_sq_set ss_set ss_more inv_set meas_done m_sq_set amp2_set amp_set "
                 "amp_turned amp_t_set post_done y_set stat_set mv_set var_root rs_set y_norm y_g y_gb y_gelu y_turned z_t_set "
                 "h1_done h1_sum h1_set h2_done h2_set y_done y_copied").split()
        S = {n: sem("f_" + n) for n in names}
        meas_in, post_in, top_in, y_stored = sem("meas_in"), sem("post_in"), sem("top_in"), sem("y_stored")
        block = ctx.enter_context(nc.Block())

        def flat(x):
            return x.rearrange("p n d -> p (n d)")

        def strength(c, i, j):
            return st[:, bass.ds(c, 1), i, j:j + 1].rearrange("p a b -> p (a b)")

        @block.sync
        def _(sp):
            def load_z(c, v, h):
                for r in range(2):
                    sp.dma_start(z[:, v, h, r], z_dram[bass.ds(c, 1), :, r, :, h * DH:(h + 1) * DH]
                                 .rearrange("c p n d -> p (c n) d")).then_inc(z_in[v][h], 16)

            for v in range(2):
                for h in range(2):
                    load_z(v, v, h)
            for r in range(2):
                sp.dma_start(mw[:, r, :], meas_w[r]).then_inc(meas_in, 16)
            sp.dma_start(pw[:, :], post_w).then_inc(post_in, 16)
            sp.dma_start(rows[:, :, :], post_rows.partition_broadcast(P)).then_inc(post_in, 16)
            sp.dma_start(w1[:, :], top1_w).then_inc(top_in, 16)
            sp.dma_start(w2[:, :, :], top2_w).then_inc(top_in, 16)
            sp.dma_start(w3[:, :], top3_w).then_inc(top_in, 16)
            sp.dma_start(b2[:, :], top2_b).then_inc(top_in, 16)
            for h in range(HALVES):
                sp.dma_start(hx[:, h], hx_dram[h]).then_inc(top_in, 16)
            with sp.Fori(1, CH // 2) as i:
                for v in range(2):
                    for h in range(2):
                        sp.wait_ge(S["sup_turned"], 4 * i + 2 * v + h - 3 + BASE)
                        load_z(2 * i + v, v, h)
            sp.wait_ge(S["y_copied"], HALVES + BASE)
            sp.dma_start(out.rearrange("(h b) o -> o h b", h=HALVES), y_out[0:1, :, :]).then_inc(y_stored, 16)
            sp.wait_ge(y_stored, 16)

        @block.gpsimd
        def _(pool):
            for n in names:
                pool.sem_inc(S[n], BASE)
            pool.memset(ident[:, :], 0.0).then_inc(made, 1)
            pool.wait_ge(made, 1)
            pool.affine_select(out=ident[:, :], in_=ident[:, :], compare_op=ALU.not_equal, fill=1.0,
                               base=0, pattern=[[-1, P]], channel_multiplier=1).then_inc(made, 1)
            pool.memset(ones[:, :], 1.0)
            pool.memset(eps[:, :], EPS)
            pool.memset(least[:, :], LEAST * 1e-3).then_inc(made, 1)

            def cosines(m, h):
                pool.wait_ge(S["unit_set"], m + 1 + BASE)
                pool.wait_ge(S["cos_set"], m + BASE)
                for s, a, b in SHIFTS:
                    last = pool.tensor_tensor(part[:, a:b], unit[:, h, 1, 0:N - s], unit[:, h, 1, s:N], ALU.mult)
                last.then_inc(S["part1"], 1)
                pool.wait_ge(S["part1"], m + 1 + BASE)
                pool.wait_ge(S["flag_set"], m + 1 + BASE)
                for s, a, b in SHIFTS:
                    last = pool.tensor_tensor(part[:, a:b], part[:, a:b], flag[:, h, 0:N - s], ALU.add)
                last.then_inc(S["part2"], 1)
                pool.wait_ge(S["part2"], m + 1 + BASE)
                for s, a, b in SHIFTS:
                    last = pool.tensor_tensor(part[:, a:b], part[:, a:b], flag[:, h, s:N], ALU.add)
                last.then_inc(S["part3"], 1)
                pool.wait_ge(S["part3"], m + 1 + BASE)
                pool.wait_ge(S["cos1"], m + 1 + BASE)
                pool.tensor_tensor(flat(cos[:, h]), flat(cos[:, h]), flat(part[:, :, :]), ALU.add).then_inc(S["cos_set"], 1)

            with pool.Fori(0, CH) as c:
                for h in range(2):
                    cosines(2 * c + h, h)

        @block.scalar
        def _(act):
            def squares(m, v, h, n):
                act.wait_ge(z_in[v][h], 32 * (n + 1))
                act.wait_ge(S["part1"], m - 1 + BASE)
                act.wait_ge(S["cos1"], m - 1 + BASE)
                act.activation(unit[:, h].rearrange("p r n d -> p (r n d)"), z[:, v, h].rearrange("p r n d -> p (r n d)"),
                               ACT.Square).then_inc(S["z_sq"], 1)

            def roots(m, h):
                act.wait_ge(S["p2_set"], m + 1 + BASE)
                act.wait_ge(S["p_inv"], m + BASE)
                act.wait_ge(S["part3"], m - 1 + BASE)
                act.activation(flat(root[:, :, :]), flat(p2[:, :, :]), ACT.Sqrt, bias=least[:, 0:1]).then_inc(S["p_root"], 1)
                act.activation(flat(flag[:, h]), flat(p2[:, :, :]), ACT.Relu, scale=-1 / LEAST, bias=ones[:, 0:1]).then_inc(S["flag_set"], 1)

            def first_coefficients(c, h):
                m = 2 * c + h
                act.wait_ge(made, 3)
                act.wait_ge(S["cos_set"], m + 1 + BASE)
                for j in range(N):
                    i = 0 if j else 1
                    last = act.activation(coef[:, h, j, :], cos[:, h, pair_of[frozenset((i, j))], :], ACT.Identity,
                                          scale=strength(c, i, j), bias=strength(c, j, j))
                last.then_inc(S["coef0"], 1)

            def keep_turned(c):
                act.wait_ge(S["sup_turned"], 2 * c + 2 + BASE)
                act.wait_ge(S["meas_done"], c + BASE)
                act.activation(sup_t[:, 0, :], turn[0][:, :], ACT.Copy)
                act.activation(sup_t[:, 1, :], turn[1][:, :], ACT.Copy)
                act.activation(sup_t[:, 2, :], turn[1][:, :], ACT.Copy, scale=-1.0).then_inc(S["sup_t_set"], 1)
                act.wait_ge(S["ss_set"], c + BASE)
                act.activation(sup_sq[:, 0, :], turn[0][:, :], ACT.Square)
                act.activation(sup_sq[:, 1, :], turn[1][:, :], ACT.Square).then_inc(S["sup_sq_set"], 1)

            def measured_squares(c):
                act.wait_ge(S["meas_done"], c + 1 + BASE)
                act.wait_ge(S["amp2_set"], c + BASE)
                act.activation(m_sq[:, 0, :], mea[0][:, :], ACT.Square)
                act.activation(m_sq[:, 1, :], mea[1][:, :], ACT.Square).then_inc(S["m_sq_set"], 1)

            def amp_root(c):
                act.wait_ge(S["amp2_set"], c + 1 + BASE)
                act.activation(amp[:, :], amp[:, :], ACT.Sqrt, scale=inv[:, 0:1]).then_inc(S["amp_set"], 1)

            def var_root(c):
                act.wait_ge(S["mv_set"], c + 1 + BASE)
                act.activation(rs[:, :], mv[:, 1:2], ACT.Sqrt, bias=eps[:, 0:1]).then_inc(S["var_root"], 1)

            def keep_amp(c):
                act.wait_ge(S["amp_turned"], c + 1 + BASE)
                act.wait_ge(S["post_done"], c + BASE)
                act.activation(amp_t[:, :], ampp[:, :], ACT.Copy).then_inc(S["amp_t_set"], 1)

            def gelu(c):
                act.wait_ge(S["y_gb"], c + 1 + BASE)
                act.activation(y[:, :], y[:, :], ACT.Gelu).then_inc(S["y_gelu"], 1)

            def keep_z(c):
                act.wait_ge(S["y_turned"], c + 1 + BASE)
                act.activation(z_t[:, :, bass.ds(c * P, P)], zp[:, :].rearrange("p (k b) -> p k b", k=DT),
                               ACT.Copy).then_inc(S["z_t_set"], 1)

            def beside(c, v, n1, last):
                keep_turned(c - 1)
                if not last:
                    squares(2 * c + 2, 1 - v, 0, n1)
                first_coefficients(c, 0)
                if not last:
                    roots(2 * c + 2, 0)
                measured_squares(c - 1)
                if not last:
                    squares(2 * c + 3, 1 - v, 1, n1)
                first_coefficients(c, 1)
                if not last:
                    roots(2 * c + 3, 1)
                amp_root(c - 1)
                keep_amp(c - 1)
                var_root(c - 1)
                gelu(c - 1)
                keep_z(c - 1)

            def relu1(h, t):
                n = h * T1 + t
                act.wait_ge(S["h1_sum"], n + 1 + BASE)
                act.activation(h1[:, t, :], h1[:, t, :], ACT.Relu).then_inc(S["h1_set"], 1)

            def relu2(h):
                for t in range(T2):
                    act.wait_ge(S["h2_done"], h * T2 + t + 1 + BASE)
                    act.activation(h2[:, t, :], turn[t][:, :], ACT.Relu, bias=b2[:, t:t + 1]).then_inc(S["h2_set"], 1)

            def keep_y(h):
                act.wait_ge(S["y_done"], h + 1 + BASE)
                act.activation(y_out[:, h, :], (ampp, postp)[h][0:1, :], ACT.Copy).then_inc(S["y_copied"], 1)

            act.wait_ge(made, 3)
            squares(0, 0, 0, 0)
            squares(1, 0, 1, 0)
            roots(0, 0)
            roots(1, 1)
            squares(2, 1, 0, 0)
            first_coefficients(0, 0)
            roots(2, 0)
            squares(3, 1, 1, 0)
            first_coefficients(0, 1)
            roots(3, 1)
            with act.Fori(0, CH // 2 - 1) as i:
                beside(2 * i + 1, 1, i + 1, False)
                beside(2 * i + 2, 0, i + 1, False)
            beside(CH - 1, 1, 0, True)
            keep_turned(CH - 1)
            act.wait_ge(top_in, 96)
            relu1(0, 0)
            relu1(0, 1)
            measured_squares(CH - 1)
            amp_root(CH - 1)
            relu1(0, 2)
            keep_amp(CH - 1)
            relu1(0, 3)
            var_root(CH - 1)
            gelu(CH - 1)
            relu2(0)
            keep_z(CH - 1)
            keep_y(0)
            for t in range(T1):
                relu1(1, t)
            relu2(1)
            keep_y(1)

        @block.vector
        def _(dve):
            def absolute(m, h):
                dve.wait_ge(S["z_sq"], m + 1 + BASE)
                dve.wait_ge(S["unit_set"], m + BASE)
                dve.tensor_tensor(flat(p2[:, :, :]), flat(unit[:, h, 0]), flat(unit[:, h, 1]), ALU.add).then_inc(S["p2_set"], 1)

            def units(m, v, h):
                dve.wait_ge(S["p_root"], m + 1 + BASE)
                dve.tensor_tensor(both[:, :, :], root[:, 0:2, :], root[:, 2:4, :], ALU.mult).then_inc(S["both_set"], 1)
                dve.wait_ge(S["both_set"], m + 1 + BASE)
                dve.reciprocal(flat(both[:, :, :]), flat(both[:, :, :])).then_inc(S["both_inv"], 1)
                dve.wait_ge(S["flag_set"], m + 1 + BASE)
                dve.wait_ge(S["both_inv"], m + 1 + BASE)
                dve.tensor_tensor(p2[:, 0:2, :], both[:, :, :], root[:, 2:4, :], ALU.mult)
                dve.tensor_tensor(p2[:, 2:4, :], both[:, :, :], root[:, 0:2, :], ALU.mult).then_inc(S["p_inv"], 1)
                dve.wait_ge(S["p_inv"], m + 1 + BASE)
                dve.tensor_tensor(unit[:, h].rearrange("p r n d -> p r (n d)"), z[:, v, h].rearrange("p r n d -> p r (n d)"),
                                  flat(p2[:, :, :]).unsqueeze(1).broadcast_to([P, 2, N * DH]), ALU.mult).then_inc(S["unit_set"], 1)
                dve.wait_ge(S["unit_set"], m + 1 + BASE)
                dve.wait_ge(S["prod_set"], m - 1 + BASE)
                for s, a, b in SHIFTS:
                    last = dve.tensor_tensor(cos[:, h, a:b], unit[:, h, 0, 0:N - s], unit[:, h, 0, s:N], ALU.mult)
                last.then_inc(S["cos1"], 1)

            def sums(c, v, h):
                m = 2 * c + h
                for k in (1, 2):
                    dve.wait_ge(S[f"coef{k - 1}"], m + 1 + BASE)
                    for j in range(N):
                        i = [x for x in range(N) if x != j][k]
                        last = dve.scalar_tensor_tensor(out=coef[:, h, j, :], in0=cos[:, h, pair_of[frozenset((i, j))], :],
                                                        scalar=strength(c, i, j), in1=coef[:, h, j, :],
                                                        op0=ALU.mult, op1=ALU.add)
                    last.then_inc(S[f"coef{k}"], 1)
                dve.wait_ge(S["coef2"], m + 1 + BASE)
                zz = z[:, v, h].rearrange("p r n d -> p r (n d)")
                dve.tensor_tensor(zz, zz, flat(coef[:, h]).unsqueeze(1).broadcast_to([P, 2, N * DH]), ALU.mult).then_inc(S["prod_set"], 1)

            def amplitude(c):
                dve.wait_ge(S["ss_set"], c + 1 + BASE)
                dve.wait_ge(S["amp_set"], c + BASE)
                dve.tensor_scalar(inv[:, :], ssp[:, 0:1], 1e-8, None, ALU.add).then_inc(S["ss_more"], 1)
                dve.wait_ge(S["ss_more"], c + 1 + BASE)
                dve.reciprocal(inv[:, :], inv[:, :]).then_inc(S["inv_set"], 1)
                dve.wait_ge(S["m_sq_set"], c + 1 + BASE)
                dve.wait_ge(S["inv_set"], c + 1 + BASE)
                dve.wait_ge(S["amp_turned"], c + BASE)
                dve.tensor_tensor(amp[:, :], m_sq[:, 0, :], m_sq[:, 1, :], ALU.add).then_inc(S["amp2_set"], 1)

            def post(c):
                dve.wait_ge(S["post_done"], c + 1 + BASE)
                dve.wait_ge(S["y_turned"], c + BASE)
                dve.tensor_tensor(y[:, :], postp[:, :], rows[:, 0, :], ALU.add).then_inc(S["y_set"], 1)
                dve.wait_ge(S["y_set"], c + 1 + BASE)
                dve.bn_stats(stats[:, :], y[:, :]).then_inc(S["stat_set"], 1)
                dve.wait_ge(post_in, 32)
                dve.wait_ge(S["stat_set"], c + 1 + BASE)
                dve.bn_aggr(mv[:, :], stats[:, :]).then_inc(S["mv_set"], 1)
                dve.wait_ge(S["var_root"], c + 1 + BASE)
                dve.reciprocal(rs[:, :], rs[:, :]).then_inc(S["rs_set"], 1)
                dve.wait_ge(S["rs_set"], c + 1 + BASE)
                dve.tensor_scalar(y[:, :], y[:, :], mv[:, 0:1], rs[:, 0:1], ALU.subtract, ALU.mult).then_inc(S["y_norm"], 1)
                dve.wait_ge(S["y_norm"], c + 1 + BASE)
                dve.tensor_tensor(y[:, :], y[:, :], rows[:, 1, :], ALU.mult).then_inc(S["y_g"], 1)
                dve.wait_ge(S["y_g"], c + 1 + BASE)
                dve.tensor_tensor(y[:, :], y[:, :], rows[:, 2, :], ALU.add).then_inc(S["y_gb"], 1)

            def beside(c, v, last):
                units(2 * c + 1, v, 1)
                if not last:
                    absolute(2 * c + 2, 0)
                sums(c, v, 0)
                if not last:
                    units(2 * c + 2, 1 - v, 0)
                    absolute(2 * c + 3, 1)
                amplitude(c - 1)
                sums(c, v, 1)
                post(c - 1)

            def add_top(h, t):
                n = h * T1 + t
                dve.wait_ge(S["h1_done"], n + 1 + BASE)
                dve.wait_ge(S["h2_done"], h * T2 + BASE)
                dve.tensor_tensor(h1[:, t, :], mea[n % 2][:, :], hx[:, h, t, :], ALU.add).then_inc(S["h1_sum"], 1)

            absolute(0, 0)
            units(0, 0, 0)
            absolute(1, 1)
            units(1, 0, 1)
            absolute(2, 0)
            sums(0, 0, 0)
            units(2, 1, 0)
            absolute(3, 1)
            dve.wait_ge(post_in, 32)
            sums(0, 0, 1)
            with dve.Fori(0, CH // 2 - 1) as i:
                beside(2 * i + 1, 1, False)
                beside(2 * i + 2, 0, False)
            beside(CH - 1, 1, True)
            dve.wait_ge(top_in, 96)
            add_top(0, 0)
            add_top(0, 1)
            amplitude(CH - 1)
            add_top(0, 2)
            add_top(0, 3)
            post(CH - 1)
            for t in range(T1):
                add_top(1, t)

        @block.tensor
        def _(pe):
            def turn_sup(c, v, h):
                pe.wait_ge(S["sup_sq_set"], c + BASE)
                pe.wait_ge(S["prod_set"], 2 * c + h + 1 + BASE)
                for r in range(2):
                    for k in range(DT // 2):
                        at = (h * DT // 2 + k) * P
                        for n in range(N):
                            last = pe.matmul(turn[r][:, at:at + P], z[:, v, h, r, n, k * P:(k + 1) * P], ident[:, :],
                                             start=n == 0, stop=n == N - 1)
                last.then_inc(S["sup_turned"], 1)

            def measure(c):
                pe.wait_ge(S["m_sq_set"], c + BASE)
                pe.wait_ge(S["sup_t_set"], c + 1 + BASE)
                for r in range(2):
                    for x, (a, w) in enumerate(((0, r), (2 - r, 1 - r))):
                        for k in range(DT):
                            last = pe.matmul(mea[r][:, :], sup_t[:, a, k * P:(k + 1) * P], mw[:, w, k * D:(k + 1) * D],
                                             start=x == 0 and k == 0, stop=x == 1 and k == DT - 1)
                last.then_inc(S["meas_done"], 1)
                pe.wait_ge(S["inv_set"], c + BASE)
                pe.wait_ge(S["sup_sq_set"], c + 1 + BASE)
                for k in range(2 * DT):
                    last = pe.matmul(ssp[:, 0:1], sup_sq[:, k // DT, k % DT * P:(k % DT + 1) * P], ones[:, :],
                                     start=k == 0, stop=k == 2 * DT - 1)
                last.then_inc(S["ss_set"], 1)

            def turn_amp(c):
                pe.wait_ge(S["amp_t_set"], c + BASE)
                pe.wait_ge(S["amp_set"], c + 1 + BASE)
                for k in range(DT):
                    last = pe.transpose(ampp[:, k * P:(k + 1) * P], amp[:, k * P:(k + 1) * P], ident[:, :])
                last.then_inc(S["amp_turned"], 1)

            def post(c):
                pe.wait_ge(S["y_set"], c + BASE)
                pe.wait_ge(S["amp_t_set"], c + 1 + BASE)
                for k in range(DT):
                    last = pe.matmul(postp[:, :], amp_t[:, k * P:(k + 1) * P], pw[:, k * D:(k + 1) * D],
                                     start=k == 0, stop=k == DT - 1)
                last.then_inc(S["post_done"], 1)

            def turn_y(c):
                pe.wait_ge(S["z_t_set"], c + BASE)
                pe.wait_ge(S["y_gelu"], c + 1 + BASE)
                for k in range(DT):
                    last = pe.transpose(zp[:, k * P:(k + 1) * P], y[:, k * P:(k + 1) * P], ident[:, :])
                last.then_inc(S["y_turned"], 1)

            def top1(h, t):
                n = h * T1 + t
                pe.wait_ge(S["z_t_set"], (h + 1) * CH // 2 + BASE)
                pe.wait_ge(S["m_sq_set"], CH - 1 + (n >= 2) + BASE)
                pe.wait_ge(S["h1_sum"], n - 1 + BASE)
                for k in range(DT):
                    last = pe.matmul(mea[n % 2][:, :], w1[:, k * D + t * P:k * D + (t + 1) * P],
                                     z_t[:, k, h * HB:(h + 1) * HB], start=k == 0, stop=k == DT - 1)
                last.then_inc(S["h1_done"], 1)

            def top2(h):
                pe.wait_ge(S["h1_set"], (h + 1) * T1 + BASE)
                pe.wait_ge(S["h2_set"], h * T2 + BASE)
                for t in range(T2):
                    for k in range(T1):
                        last = pe.matmul(turn[t][:, :], w2[:, k, t * P:(t + 1) * P], h1[:, k, :],
                                         start=k == 0, stop=k == T1 - 1)
                    last.then_inc(S["h2_done"], 1)

            def top3(h):
                pe.wait_ge(S["h2_set"], (h + 1) * T2 + BASE)
                for k in range(T2):
                    last = pe.matmul((ampp, postp)[h][0:1, :], w3[:, k:k + 1], h2[:, k, :], start=k == 0, stop=k == T2 - 1)
                last.then_inc(S["y_done"], 1)

            pe.wait_ge(made, 3)
            pe.wait_ge(meas_in, 32)
            pe.wait_ge(post_in, 32)
            def beside(c, v):
                measure(c)
                turn_sup(c + 1, 1 - v, 0)
                turn_amp(c)
                post(c)
                turn_sup(c + 1, 1 - v, 1)
                turn_y(c)

            turn_sup(0, 0, 0)
            turn_sup(0, 0, 1)
            with pe.Fori(0, CH // 2 - 1) as i:
                beside(2 * i, 0)
                beside(2 * i + 1, 1)
            measure(CH - 2)
            turn_sup(CH - 1, 1, 0)
            turn_amp(CH - 2)
            post(CH - 2)
            pe.wait_ge(top_in, 96)
            top1(0, 0)
            top1(0, 1)
            turn_sup(CH - 1, 1, 1)
            turn_y(CH - 2)
            pe.wait_ge(S["h1_sum"], 2 + BASE)
            measure(CH - 1)
            top1(0, 2)
            turn_amp(CH - 1)
            top1(0, 3)
            post(CH - 1)
            top2(0)
            turn_y(CH - 1)
            top3(0)
            for t in range(T1):
                top1(1, t)
            top2(1)
            top3(1)


def program(nc, t, out):
    s_dram = nc.dram_tensor("s_scratch", [2, 2, CH, P, DT * N, P], F32).ap()
    hx_dram = nc.dram_tensor("hx_scratch", [HALVES, P, 512 // P, HB], F32).ap()
    o_dram = nc.dram_tensor("o_scratch", [2, 2, CH, P, 2, N * P], F32).ap()
    z_dram = nc.dram_tensor("z_scratch", [CH, P, 2, N, D], F32).ap()
    with ExitStack() as sems:
        st = sems.enter_context(nc.sbuf_tensor("strengths", [P, CH, N, N], F32))
        encoders(nc, sems, t["x_t"], t["enc_w"], t["enc_bias"], t["ln_gb"], s_dram, hx_dram)
        attention(nc, sems, t["qkv_w"], t["qk_bias"], t["v_bias"], t["row_ids"], [t[f"table_{n}"] for n in range(N)], st,
                  s_dram, o_dram)
        interact(nc, sems, t["wo_w"], t["wo_bias"], t["int_w"], o_dram, z_dram)
        finish(nc, sems, st, t["meas_w"], t["post_w"], t["post_rows"],
               t["top1_w"], t["top2_w"], t["top3_w"], t["top2_b"], z_dram, hx_dram, out)



def lay_out(inp, np):
    def g(name):
        return np.asarray(inp[name])

    def rec(name):
        return g("L0_rec_" + name)

    def pieces(w):
        o, i = w.shape
        return w.reshape(o // P, P, 2, i // P // 2, P).transpose(0, 2, 4, 3, 1).reshape(o // P * 2, P, i // 2)

    def tokens_inner(w):
        return w.reshape((N, DT, P) + w.shape[1:]).swapaxes(0, 1).reshape(w.shape)

    def by_row(w):
        return w.reshape(DT, P, w.shape[1]).transpose(1, 0, 2).reshape(P, DT * w.shape[1])

    def columns(v):
        return v.reshape(-1, P).T

    out = {
        "x_t": g("r_x").reshape(HALVES, HB, KT // 2, 2, P).transpose(0, 2, 4, 3, 1).reshape(HALVES, KT // 2, P, 2 * HB),
        "enc_w": np.concatenate([pieces(w) for w in (
            rec("er_W1"), rec("ei_W1"), g("W_top1")[OUT:].T, tokens_inner(rec("er_W2")), tokens_inner(rec("ei_W2")))]),
        "enc_bias": columns(np.concatenate([rec("er_b1"), rec("ei_b1"), g("b_top1"),
                                            tokens_inner(rec("er_b2")), tokens_inner(rec("ei_b2"))])),
        "ln_gb": np.stack([rec(n) for n in ("er_g1", "er_be1", "ei_g1", "ei_be1")]).reshape(2, 2, KT, P).transpose(3, 0, 1, 2),
        "qkv_w": np.stack([by_row(rec("W" + n).T) for n in ("q_r", "q_i", "k_r", "k_i", "v_r", "v_i")]),
        "qk_bias": np.stack([rec("b" + n) for n in ("q_r", "q_i", "k_r", "k_i")]).reshape(4, DT, P).transpose(2, 0, 1),
        "v_bias": np.stack([rec("bv_r"), rec("bv_i")]),
        "wo_w": np.stack([by_row(rec("Wo_r").T), by_row(rec("Wo_i").T)]),
        "wo_bias": np.stack([rec("bo_r"), rec("bo_i")]).reshape(2, DT, P).transpose(2, 0, 1),
        "int_w": np.stack([np.stack([by_row(w.T) for w in rec(n)]) for n in ("int_Wr", "int_Wi")]),
        "row_ids": g("ids").reshape(CH, P, N).transpose(1, 0, 2),
        "meas_w": np.stack([by_row(rec("meas_Mr").T), by_row(rec("meas_Mi").T)]),
        "post_w": by_row(rec("post_W").T),
        "post_rows": np.stack([rec("post_b"), rec("post_g"), rec("post_be")]),
        "top1_w": by_row(g("W_top1")[:OUT]),
        "top2_w": g("W_top2").reshape(DT, P, 256).transpose(1, 0, 2),
        "top3_w": columns(g("W_top3")),
        "top2_b": columns(g("b_top2")),
    }
    out.update({f"table_{n}": g(f"tbl_{n}") for n in range(N)})
    return {k: np.ascontiguousarray(v) for k, v in out.items()}


def kernel(**inputs):
    import numpy as np
    import concourse.bacc as bacc
    from concourse.bass_utils import run_bass_kernel_spmd

    nc = bacc.Bacc("TRN2", target_bir_lowering=False, num_devices=1)
    arrays = {f"in_{k}": v for k, v in lay_out(inputs, np).items()}
    t = {k[3:]: nc.dram_tensor(k, v.shape, mybir.dt.from_np(v.dtype), kind="ExternalInput").ap() for k, v in arrays.items()}
    out = nc.dram_tensor("out_0_dram", (B, 1), F32, kind="ExternalOutput").ap()
    program(nc, t, out)
    r = run_bass_kernel_spmd(nc, [arrays], core_ids=[0])
    return r.results[0]["out_0_dram"]
```

```python
from contextlib import ExitStack

import concourse.bass as bass
from concourse import mybir

F32 = mybir.dt.float32
F32R = mybir.dt.float32r
ALU = mybir.AluOpType
ACT = mybir.ActivationFunctionType
AX_X = mybir.AxisListType.X

P = 128
B, IN, HID, D, N, H, OUT = 1024, 2048, 2048, 512, 4, 8, 512
HD = D // H
HB = 512
HALVES = B // HB
KT = IN // P
CH = B // P
DT = D // P
EPS = 1e-5
CREDIT = 2


def encoders(nc, sems, x_t, enc_w, enc_bias, ln_gb, s_dram, hx_dram):
    L1 = HID // P
    XP = 512 // P
    L2 = N * D // P
    TILES = 2 * L1 + XP + 2 * L2
    XPIECES = KT // 2
    PIECE = KT // 2 * P
    PIECES = 2 * TILES
    STORES = (XP + 2 * L2) // 2

    with ExitStack() as ctx:
        def sb(name, shape, dt=F32):
            return ctx.enter_context(nc.sbuf_tensor(name, shape, dt))

        def sem(name):
            return sems.enter_context(nc.semaphore(name))

        act_hi = sb("act_hi", [P, KT, HB], F32R)
        act_lo = sb("act_lo", [P, KT, HB], F32R)
        y_r_at = nc.sbuf_base
        y_r = sb("y_r", [P, KT, HB])
        hid_hi = nc.alloc_sbuf_tensor_at("hid_hi", [P, KT, HB], F32R, offset=y_r_at)
        hid_lo = sb("hid_lo", [P, KT, HB], F32R)
        y_i = sb("y_i", [P, KT, HB])
        raw = sb("raw", [P, 2, PIECE])
        w_hi = sb("w_hi", [P, 2, PIECE], F32R)
        w_lo = sb("w_lo", [P, 2, PIECE], F32R)
        total = sb("total", [P, HB])
        sq_total = sb("sq_total", [P, HB])
        mean = sb("mean", [P, HB])
        rstd = sb("rstd", [P, HB])
        ln_tmp = sb("ln_tmp", [P, 2, HB])
        stage = sb("stage", [P, 2, 2, HB])
        bias = sb("bias", [P, TILES])
        gb = sb("gb", [P, 2, 2, KT])
        over_n = sb("over_n", [P, P])
        eps = sb("eps", [P, 1])
        acc = [ctx.enter_context(nc.psum_tensor(f"acc{u}", [P, HB], F32)) for u in range(2)]
        stat = ctx.enter_context(nc.psum_tensor("stat", [P, HB], F32))

        loaded = [sem(f"loaded{u}") for u in range(2)]
        hi_done = sem("hi_done")
        lo_done = sem("lo_done")
        half_done = sem("half_done")
        tile_done = sem("tile_done")
        evacuated = sem("evacuated")
        added = sem("added")
        cleared = sem("cleared")
        stat_done = sem("stat_done")
        mean_ready = sem("mean_ready")
        centered = sem("centered")
        squared = sem("squared")
        sq_added = sem("sq_added")
        root_done = sem("root_done")
        rstd_ready = sem("rstd_ready")
        scaled = sem("scaled")
        gelu_done = sem("gelu_done")
        h_hi = sem("h_hi")
        h_lo = sem("h_lo")
        hi_staged = sem("hi_staged")
        stored = [sem(f"stored{u}") for u in range(2)]
        x_in = [sem(f"x_in{q}") for q in range(XPIECES)]
        x_hi = sem("x_hi")
        x_lo = sem("x_lo")
        consts_in = sem("consts_in")
        consts_set = sem("consts_set")

        block = ctx.enter_context(nc.Block())

        R1, I1, TX, R2, I2 = (0, L1), (L1, L1), (2 * L1, XP), (2 * L1 + XP, L2), (2 * L1 + XP + L2, L2)

        @block.sync
        def _(sp):
            sp.dma_start(bias[:, :], enc_bias).then_inc(consts_in, 16)
            sp.dma_start(gb[:, :, :, :], ln_gb).then_inc(consts_in, 16)
            for u in range(2):
                sp.sem_inc(stored[u], 32)

            def load(h, piece, u, src):
                sp.wait_ge(hi_done, h * PIECES + piece + 1)
                sp.wait_ge(lo_done, h * PIECES + piece + 1)
                sp.dma_start(raw[:, u, :], src).then_inc(loaded[u], 16)

            def load_half(h, t, u):
                load(h, 2 * t + u, u, enc_w[bass.ds(2 * t + u, 1)].rearrange("a p n -> p (a n)"))

            def load_tile(h, t):
                for u in range(2):
                    load_half(h, t, u)

            def store(h, stage_, t, u):
                first, _ = stage_
                sp.wait_ge(evacuated, h * TILES + first + t + 1 + CREDIT)
                if stage_ is TX:
                    for v in range(2):
                        sp.dma_start(hx_dram[bass.ds(h, 1), :, bass.ds(t, 1), v * 256:(v + 1) * 256]
                                     .rearrange("a p t n -> p (a t n)"),
                                     stage[:, u, 0, v * 256:(v + 1) * 256]).then_inc(stored[u], 16)
                else:
                    ri = 0 if stage_ is R2 else 1
                    for v in range(2):
                        sp.dma_start(s_dram[ri, v, bass.ds(h * 4, 4), :, bass.ds(t, 1), :]
                                     .rearrange("c p t b -> p c (t b)"),
                                     stage[:, u, v, :].rearrange("p (c b) -> p c b", c=4)).then_inc(stored[u], 16)

            def load_x(h, q):
                sp.dma_start(y_i[:, 2 * q:2 * q + 2, :].rearrange("p a b -> p (a b)"), x_t[h, q]).then_inc(x_in[q], 16)

            load_half(0, 0, 0)
            for q in range(2):
                load_x(0, q)
            load_half(0, 0, 1)
            for q in range(2, XPIECES):
                load_x(0, q)
            load_tile(0, 1)
            for h in range(HALVES):
                with sp.Fori(1, L1) as i:
                    load_tile(h, 2 * i)
                    load_tile(h, 2 * i + 1)
                before = None
                for st in (TX, R2, I2):
                    first, tiles = st
                    load_tile(h, first)
                    load_tile(h, first + 1)
                    if before:
                        for u in range(2):
                            store(h, before, before[1] - 2 + u, u)
                    if st is I2 and h + 1 < HALVES:
                        sp.wait_ge(h_lo, h * 2 * KT + 2 * KT + CREDIT)
                        for q in range(XPIECES):
                            load_x(h + 1, q)
                    with sp.Fori(1, tiles // 2) as i:
                        load_tile(h, first + 2 * i)
                        load_tile(h, first + 2 * i + 1)
                        for u in range(2):
                            store(h, st, 2 * i - 2 + u, u)
                    before = st
                if h + 1 < HALVES:
                    load_tile(h + 1, 0)
                for u in range(2):
                    store(h, I2, L2 - 2 + u, u)
                if h + 1 < HALVES:
                    load_tile(h + 1, 1)
            for u in range(2):
                sp.wait_ge(stored[u], 32 * (HALVES * STORES + 1))

        @block.gpsimd
        def _(pool):
            pool.sem_inc(lo_done, CREDIT)
            pool.memset(over_n[:, :], 1.0 / HID).then_inc(consts_set, 1)
            pool.memset(eps[:, :], EPS).then_inc(consts_set, 1)

            def low(h, piece, n, u, dst, hi):
                pool.wait_ge(loaded[u], 16 * (h * TILES + n + 1))
                pool.wait_ge(hi_done, h * PIECES + piece + 1 + CREDIT)
                pool.tensor_tensor(dst, raw[:, u, :], hi.bitcast(F32), ALU.subtract).then_inc(lo_done, 1)

            with pool.Fori(0, HALVES) as h:
                with pool.Fori(0, TILES) as t:
                    for u in range(2):
                        pool.wait_ge((half_done, tile_done)[u], h * TILES + t + CREDIT)
                        low(h, 2 * t + u, t, u, w_lo[:, u, :], w_hi[:, u, :])

        @block.scalar
        def _(act):
            act.sem_inc(hi_done, CREDIT)

            def high(h, n, u, dst):
                act.wait_ge(consts_in, 32)
                act.wait_ge(loaded[u], 16 * (h * TILES + n + 1))
                act.activation(dst, raw[:, u, :], ACT.Copy).then_inc(hi_done, 1)

            def high_half(h, t, u):
                act.wait_ge((half_done, tile_done)[u], h * TILES + t + CREDIT)
                high(h, t, u, w_hi[:, u, :])

            def high_tile(h, t):
                for u in range(2):
                    high_half(h, t, u)

            def high_x(h, q):
                act.wait_ge(x_in[q], 16 * (h + 1))
                act.activation(act_hi[:, 2 * q:2 * q + 2, :].rearrange("p a b -> p (a b)"),
                               y_i[:, 2 * q:2 * q + 2, :].rearrange("p a b -> p (a b)"), ACT.Copy).then_inc(x_hi, 1)

            def square(h, ln, y, j, u):
                at = h * 2 * KT + ln * KT + j
                act.wait_ge(centered, at + 1)
                act.wait_ge(sq_added, at + 1)
                act.wait_ge(consts_in, 32)
                act.activation(ln_tmp[:, u, :], y[:, bass.ds(j, 1), :].rearrange("p a b -> p (a b)"),
                               ACT.Square).then_inc(squared, 1)

            def gelu(h, ln, y, hi, j, u):
                at = h * 2 * KT + ln * KT + j
                act.wait_ge(scaled, at + 1)
                act.wait_ge(h_lo, at + 1)
                act.wait_ge(consts_in, 32)
                act.activation(ln_tmp[:, u, :], y[:, bass.ds(j, 1), :].rearrange("p a b -> p (a b)"), ACT.Gelu,
                               scale=gb[:, ln, 0, bass.ds(j, 1)], bias=gb[:, ln, 1, bass.ds(j, 1)]).then_inc(gelu_done, 1)
                act.wait_ge(consts_in, 32)
                act.wait_ge(gelu_done, at + 1)
                act.activation(hi[:, bass.ds(j, 1), :].rearrange("p a b -> p (a b)"), ln_tmp[:, u, :],
                               ACT.Copy).then_inc(h_hi, 1)

            def with_norm(h, ln, first, y, hi):
                for u in range(2):
                    high_tile(h, first + u)
                with act.Fori(0, 4) as i:
                    for v in range(2):
                        high_tile(h, first + 2 + 2 * i + v)
                        for u in range(2):
                            square(h, ln, y, 4 * i + 2 * v + u, u)
                for u in range(2):
                    high_tile(h, first + 10 + u)
                act.wait_ge(stat_done, 4 * h + 2 * ln + 2)
                act.activation(rstd[:, :], stat[:, :], ACT.Sqrt, bias=eps[:, 0:1]).then_inc(root_done, 1)
                high_tile(h, first + 12)
                with act.Fori(0, 2) as i:
                    for v in range(2):
                        for w in range(2):
                            for u in range(2):
                                gelu(h, ln, y, hi, 8 * i + 4 * v + 2 * w + u, u)
                            high_half(h, first + 13 + 2 * i + v, w)

            act.wait_ge(consts_in, 32)
            act.wait_ge(consts_set, 2)
            with act.Fori(0, HALVES) as h:
                high_half(h, 0, 0)
                act.wait_ge(tile_done, h * TILES + CREDIT)
                for q in range(XPIECES):
                    high_x(h, q)
                    if q == 1:
                        high_half(h, 0, 1)
                with act.Fori(1, L1) as t:
                    high_tile(h, t)
                with_norm(h, 0, I1[0], y_r, hid_hi)
                with act.Fori(1, XP) as t:
                    high_tile(h, TX[0] + t)
                with_norm(h, 1, R2[0], y_i, act_hi)
                with act.Fori(1, L2) as t:
                    high_tile(h, I2[0] + t)

        @block.vector
        def _(dve):
            dve.sem_inc(evacuated, CREDIT)
            dve.sem_inc(sq_added, CREDIT)
            dve.sem_inc(h_lo, CREDIT)
            dve.sem_inc(added, 1)

            def tile2(x, j):
                return x[:, bass.ds(j, 1), :].rearrange("p a b -> p (a b)")

            def evacuate_first(h, st, t, u, ln, y):
                first, _ = st
                dve.wait_ge(cleared, 3 * h + ln + 1)
                dve.wait_ge(tile_done, h * TILES + first + t + 1 + CREDIT)
                dve.tensor_scalar(tile2(y, t), acc[u][:, :], bias[:, bass.ds(first + t, 1)], None,
                                  ALU.add).then_inc(evacuated, 1)
                dve.wait_ge(evacuated, h * TILES + first + t + 1 + CREDIT)
                dve.wait_ge(added, h * 2 * KT + ln * KT + t + 1)
                dve.tensor_tensor(total[:, :], total[:, :], tile2(y, t), ALU.add).then_inc(added, 1)

            def evacuate_second(h, st, t, half_t, u, n0):
                first, _ = st
                dve.wait_ge(tile_done, h * TILES + first + t + 1 + CREDIT)
                dve.wait_ge(stored[u], 32 * (h * STORES + n0 + half_t + 1))
                hi = stage[:, u, 0, :]
                b = bias[:, bass.ds(first + t, 1)]
                dve.tensor_scalar(hi.bitcast(F32R), acc[u][:, :], b, None, ALU.add).then_inc(hi_staged, 1)
                dve.wait_ge(hi_staged, h * 2 * L2 + (first - R2[0]) + t + 1)
                dve.scalar_tensor_tensor(out=stage[:, u, 1, :].bitcast(F32R), in0=acc[u][:, :], scalar=b, in1=hi,
                                         op0=ALU.add, op1=ALU.subtract).then_inc(evacuated, 1)

            def with_norm(h, ln, y, hi, lo, evac):
                s = 4 * h + 2 * ln
                dve.wait_ge(stat_done, s + 1)
                dve.tensor_copy(mean[:, :], stat[:, :]).then_inc(mean_ready, 1)
                dve.memset(total[:, :], 0.0)
                dve.memset(sq_total[:, :], 0.0).then_inc(cleared, 1)
                dve.wait_ge(mean_ready, 2 * h + ln + 1)
                dve.wait_ge(cleared, 3 * h + ln + 2)
                evac(0, 0)
                evac(0, 1)
                at = h * 2 * KT + ln * KT
                with dve.Fori(0, 4) as i:
                    for u in range(4):
                        j = 4 * i + u
                        dve.tensor_tensor(tile2(y, j), tile2(y, j), mean[:, :], ALU.subtract).then_inc(centered, 1)
                    for u in range(4):
                        j = 4 * i + u
                        dve.wait_ge(squared, at + j + 1)
                        dve.wait_ge(sq_added, at + j + CREDIT)
                        dve.tensor_tensor(sq_total[:, :], sq_total[:, :], ln_tmp[:, u % 2, :], ALU.add).then_inc(sq_added, 1)
                    evac(i + 1, 0)
                    evac(i + 1, 1)
                dve.wait_ge(root_done, 2 * h + ln + 1)
                dve.reciprocal(rstd[:, :], rstd[:, :]).then_inc(rstd_ready, 1)
                evac(5, 0)
                evac(5, 1)
                dve.wait_ge(consts_in, 32)
                dve.wait_ge(rstd_ready, 2 * h + ln + 1)
                with dve.Fori(0, 2) as i:
                    for v in range(2):
                        for u in range(4):
                            j = 8 * i + 4 * v + u
                            dve.tensor_tensor(tile2(y, j), tile2(y, j), rstd[:, :], ALU.mult).then_inc(scaled, 1)
                        for u in range(4):
                            j = 8 * i + 4 * v + u
                            dve.wait_ge(h_hi, at + j + 1)
                            dve.tensor_tensor(tile2(lo, j), ln_tmp[:, u % 2, :], tile2(hi, j).bitcast(F32),
                                              ALU.subtract).then_inc(h_lo, 1)
                        evac(i + 6, v)

            dve.wait_ge(consts_in, 32)
            with dve.Fori(0, HALVES) as h:
                dve.memset(total[:, :], 0.0).then_inc(cleared, 1)
                for q in range(XPIECES):
                    dve.wait_ge(x_hi, h * XPIECES + q + 1)
                    dve.tensor_tensor(act_lo[:, 2 * q:2 * q + 2, :].rearrange("p a b -> p (a b)"),
                                      y_i[:, 2 * q:2 * q + 2, :].rearrange("p a b -> p (a b)"),
                                      act_hi[:, 2 * q:2 * q + 2, :].rearrange("p a b -> p (a b)").bitcast(F32),
                                      ALU.subtract).then_inc(x_lo, 1)
                with dve.Fori(0, L1 // 2) as i:
                    for u in range(2):
                        evacuate_first(h, R1, 2 * i + u, u, 0, y_r)
                with_norm(h, 0, y_r, hid_hi, hid_lo, lambda i, u: evacuate_first(h, I1, 2 * i + u, u, 1, y_i))
                with dve.Fori(0, XP // 2) as i:
                    for u in range(2):
                        dve.wait_ge(tile_done, h * TILES + TX[0] + 2 * i + u + 1 + CREDIT)
                        dve.wait_ge(stored[u], 32 * (h * STORES + i + 1))
                        dve.tensor_scalar(stage[:, u, 0, :], acc[u][:, :], bias[:, bass.ds(TX[0] + 2 * i + u, 1)], None,
                                          ALU.add).then_inc(evacuated, 1)
                with_norm(h, 1, y_i, act_hi, act_lo,
                          lambda i, u: evacuate_second(h, R2, 2 * i + u, i, u, XP // 2))
                with dve.Fori(0, L2 // 2) as i:
                    for u in range(2):
                        evacuate_second(h, I2, 2 * i + u, i, u, XP // 2 + L2 // 2)

        @block.tensor
        def _(pe):
            pe.sem_inc(half_done, CREDIT)
            pe.sem_inc(tile_done, CREDIT)

            def multiply(h, t, u, hi, lo, first=False):
                pe.wait_ge(evacuated, h * TILES + t + 1)
                for q in range(2):
                    piece = h * PIECES + 2 * t + q
                    pe.wait_ge(hi_done, piece + 1 + CREDIT)
                    pe.wait_ge(lo_done, piece + 1 + CREDIT)
                    for k in range(KT // 2):
                        kk = q * (KT // 2) + k
                        if first and kk % 2 == 0:
                            pe.wait_ge(x_lo, h * XPIECES + kk // 2 + 1)
                        wh, wl = w_hi[:, q, k * P:(k + 1) * P], w_lo[:, q, k * P:(k + 1) * P]
                        pe.matmul(acc[u][:, :], wh, hi[:, kk, :], start=kk == 0, stop=False)
                        pe.matmul(acc[u][:, :], wh, lo[:, kk, :], start=False, stop=False)
                        last = pe.matmul(acc[u][:, :], wl, hi[:, kk, :], start=False, stop=kk == KT - 1)
                    last.then_inc((half_done, tile_done)[q], 1)

            def statistic(src):
                return pe.matmul(stat[:, :], over_n[:, :], src[:, :], start=True, stop=True)

            def with_norm(h, ln, first, hi, lo):
                at = h * 2 * KT + ln * KT
                multiply(h, first, 0, hi, lo)
                pe.wait_ge(added, at + KT + 1)
                statistic(total).then_inc(stat_done, 1)
                multiply(h, first + 1, 1, hi, lo)
                with pe.Fori(1, 5) as i:
                    for u in range(2):
                        multiply(h, first + 2 * i + u, u, hi, lo)
                pe.wait_ge(sq_added, at + KT + CREDIT)
                statistic(sq_total).then_inc(stat_done, 1)
                with pe.Fori(5, 8) as i:
                    for u in range(2):
                        multiply(h, first + 2 * i + u, u, hi, lo)

            pe.wait_ge(consts_set, 2)
            with pe.Fori(0, HALVES) as h:
                multiply(h, 0, 0, act_hi, act_lo, first=True)
                multiply(h, 1, 1, act_hi, act_lo)
                with pe.Fori(1, L1 // 2) as i:
                    for u in range(2):
                        multiply(h, 2 * i + u, u, act_hi, act_lo)
                with_norm(h, 0, I1[0], act_hi, act_lo)
                with pe.Fori(0, XP // 2) as i:
                    for u in range(2):
                        multiply(h, TX[0] + 2 * i + u, u, act_hi, act_lo)
                pe.wait_ge(h_lo, h * 2 * KT + KT + CREDIT)
                with_norm(h, 1, R2[0], hid_hi, hid_lo)
                pe.wait_ge(consts_set, 2)
                pe.wait_ge(h_lo, h * 2 * KT + 2 * KT + CREDIT)
                with pe.Fori(0, L2 // 2) as i:
                    for u in range(2):
                        multiply(h, I2[0] + 2 * i + u, u, act_hi, act_lo)


G = 4
GB = P // G
T = N * P
HH = H // 2


def attention(nc, sems, qkv_w, qk_bias, v_bias, ids, tables, st, s_dram, o_dram):
    with ExitStack() as ctx:
        def sb(name, shape, dt=F32):
            return ctx.enter_context(nc.sbuf_tensor(name, shape, dt))

        def sem(name):
            return sems.enter_context(nc.semaphore(name))

        def ps(name, shape):
            return ctx.enter_context(nc.psum_tensor(name, shape, F32))

        wt_hi = sb("wt_hi", [P, 6, DT, D], F32R)
        wt_lo = sb("wt_lo", [P, 6, DT, D], F32R)
        s_hi = sb("s_hi", [P, 2, DT, T], F32R)
        s_lo = sb("s_lo", [P, 2, DT, T], F32R)
        q2 = sb("q2", [P, HH, 2, T])
        ks = sb("ks", [P, HH, T])
        v = sb("v", [P, G, H, 2, HD])
        pt = sb("pt", [P, G * HH, P])
        o_out = sb("o_out", [P, 2, HH, T])
        masked = sb("masked", [P, 2, 16, GB])
        vb = sb("vb", [P, 2, D])
        ids_sb = sb("ids_sb", [P, CH, N], mybir.dt.int32)
        qkb = sb("qkb", [P, 4, DT])
        neg_b = sb("neg_b", [P, DT])
        ident = sb("ident", [P, P])
        mask = sb("mask", [P, GB])
        sc = sb("sc", [P, G, 2, 2, 2, N])
        sc_sq = sb("sc_sq", [P, G * HH, 2, N])
        mag2 = sb("mag2", [P, G * HH, N])
        mag = sb("mag", [P, G * HH * N])
        top = sb("top", [G * HH * N, GB])
        ex = sb("ex", [G * HH * N, N, GB])
        den = sb("den", [G * HH * N, GB])
        w_t = sb("w_t", [P, G * HH * N])
        tiny = sb("tiny", [P, 1])
        proj = [ps(f"proj{u}", [P, T]) for u in range(2)]
        scp = [ps(f"scp{u}", [P, T]) for u in range(2)]
        avp = [ps(f"avp{u}", [P, T]) for u in range(2)]
        tp = ps("tp", [P, T])
        R = G * HH * N
        halves = [x for t in (v[:, :, :, :, :].rearrange("p g h r d -> p (g h r d)"),
                              o_out[:, :, :, :].rearrange("p u h t -> p (u h t)")) for x in (t[:, 0:DT * D], t[:, DT * D:])]
        raw = halves + [pt[:, :, :].rearrange("p a b -> p (a b)"), halves[0]]
        BY_VECTOR, BY_POOL = (0, 1, 4), (2, 3, 5)

        w_in = [sem(f"w_in{m}") for m in range(6)]
        w_hi_done = sem("w_hi_done")
        w_lo_dve = sem("w_lo_dve")
        w_lo_pool = sem("w_lo_pool")
        small_in = sem("small_in")
        ids_in = sem("ids_in")
        gathered = sem("gathered")
        neg_set = sem("neg_set")
        s_in = [sem(f"s_in{r}") for r in range(2)]
        proj_done = sem("proj_done")
        even_out = sem("even_out")
        odd_out = sem("odd_out")
        score_done = sem("score_done")
        score_masked = sem("score_masked")
        score_out = sem("score_out")
        squared2 = sem("squared2")
        mag2_set = sem("mag2_set")
        mag_set = sem("mag_set")
        mag_turned = sem("mag_turned")
        top_set = sem("top_set")
        less_top = sem("less_top")
        exp_set = sem("exp_set")
        den_set = sem("den_set")
        den_inv = sem("den_inv")
        prob_set = sem("prob_set")
        prob_turned = sem("prob_turned")
        w_t_set = sem("w_t_set")
        pt_set = sem("pt_set")
        av_done = sem("av_done")
        o_set = sem("o_set")
        o_stored = [sem(f"o_stored{u}") for u in range(2)]
        set_up = sem("set_up")

        block = ctx.enter_context(nc.Block())
        QK0, V0, QK1, PER = 0, 8, 16, 24
        qk_at = (QK0, QK1)

        def head_pair_and_kind(i):
            return i % 4 // 2, i // 4 * 2 + i % 2

        @block.sync
        def _(sp):

            def load_w(m):
                sp.dma_start(raw[m], qkv_w[m]).then_inc(w_in[m], 16)

            def load_s(c, r):
                for x, t in ((0, s_hi), (1, s_lo)):
                    sp.dma_start(t[:, r].rearrange("p d t -> p (d t)").bitcast(F32),
                                 s_dram[r, x, bass.ds(c, 1)].rearrange("c p t b -> p (c t b)")).then_inc(s_in[r], 16)

            def store_o(c, hh):
                sp.wait_ge(o_set, 8 * c + 4 * hh + 4 + CREDIT)
                for r in range(2):
                    for par in range(2):
                        sp.dma_start(o_dram[r, hh, bass.ds(c, 1), par * HD:(par + 1) * HD].rearrange("c p d t -> p (c d) t"),
                                     o_out[r * HD:(r + 1) * HD, hh].rearrange("p (d a) t -> p a d t", a=2)[:, par]
                                     ).then_inc(o_stored[hh], 16)

            load_w(0)
            load_s(0, 0)
            sp.dma_start(qkb[:, :, :], qk_bias).then_inc(small_in, 16)
            sp.dma_start(vb[:, :, :], v_bias.partition_broadcast(P)).then_inc(small_in, 16)
            for m in range(1, 4):
                load_w(m)
            load_s(0, 1)
            sp.dma_start(ids_sb[:, :, :], ids).then_inc(ids_in, 16)
            load_w(4)
            sp.wait_ge(w_lo_dve, 1)
            load_w(5)
            for u in range(2):
                sp.sem_inc(o_stored[u], 64)
            with sp.Fori(1, CH) as c:
                for r in range(2):
                    sp.wait_ge(proj_done, PER * c - 4 + 4 * r)
                    load_s(c, r)
                store_o(c - 1, 0)
                store_o(c - 1, 1)
            store_o(CH - 1, 0)
            store_o(CH - 1, 1)
            for u in range(2):
                sp.wait_ge(o_stored[u], 64 * (CH + 1))

        @block.gpsimd
        def _(pool):
            pool.memset(tiny[:, :], 1e-8)
            pool.memset(ident[:, :], 0.0).then_inc(set_up, 1)
            pool.wait_ge(set_up, 1)
            pool.affine_select(out=ident[:, :], in_=ident[:, :], compare_op=ALU.not_equal, fill=1.0,
                               base=0, pattern=[[-1, P]], channel_multiplier=1).then_inc(set_up, 1)
            pool.sem_inc(av_done, CREDIT)
            pool.sem_inc(pt_set, CREDIT)
            for m in BY_POOL:
                pool.wait_ge(w_hi_done, m + 1)
                pool.tensor_tensor(wt_lo[:, m].rearrange("p k n -> p (k n)"), raw[m],
                                   wt_hi[:, m].rearrange("p k n -> p (k n)").bitcast(F32), ALU.subtract).then_inc(w_lo_pool, 1)

            def expand(c, hh):
                pool.wait_ge(av_done, 8 * c + 4 * hh + CREDIT)
                pool.wait_ge(w_t_set, 2 * c + hh + 1)
                pool.tensor_tensor(pt[:, :, :].rearrange("p a (n b) -> p (a n) b", b=GB),
                                   w_t[:, :].unsqueeze(2).broadcast_to([P, R, GB]),
                                   mask[:, :].unsqueeze(1).broadcast_to([P, R, GB]), ALU.mult).then_inc(pt_set, 1)

            pool.wait_ge(ids_in, 16)
            for c in range(CH):
                for n in range(N):
                    pool.indirect_dma_start(out=st[:, c, n, :], out_offset=None, in_=tables[n],
                                            in_offset=bass.IndirectOffsetOnAxis(ap=ids_sb[:, c, n:n + 1], axis=0)
                                            ).then_inc(gathered, 16)
            pool.wait_ge(set_up, 3)
            expand(0, 0)
            expand(0, 1)
            with pool.Fori(1, CH) as c:
                expand(c, 0)
                expand(c, 1)
            pool.wait_ge(gathered, 16 * CH * N)

        @block.scalar
        def _(act):
            act.sem_inc(even_out, CREDIT)
            act.sem_inc(o_set, CREDIT)

            def high_w(m):
                act.wait_ge(w_in[m], 16)
                act.activation(wt_hi[:, m].rearrange("p k n -> p (k n)"), raw[m], ACT.Copy).then_inc(w_hi_done, 1)

            for m in range(2):
                high_w(m)
            act.wait_ge(small_in, 32)
            act.activation(neg_b[:, :], qkb[:, 0, :], ACT.Copy, scale=-1.0).then_inc(neg_set, 1)
            act.wait_ge(neg_set, 1)
            act.wait_ge(set_up, 3)

            def take_even(c, hh, i):
                j, kind = head_pair_and_kind(i)
                act.wait_ge(proj_done, PER * c + qk_at[hh] + i + 1)
                src = proj[i % 2][0:HD, :].rearrange("p (t g) -> p g t", g=G)
                b = qkb[0:HD, kind, 2 * hh + j:2 * hh + j + 1]

                def to(x):
                    return x.rearrange("p (g t) -> p g t", g=G)

                h = 2 * j
                if kind == 0:
                    act.activation(to(q2[0:HD, h, 0]), src, ACT.Identity, bias=b)
                    act.activation(to(q2[HD:P, h, 1]), src, ACT.Identity, scale=-1.0,
                                   bias=neg_b[0:HD, 2 * hh + j:2 * hh + j + 1]).then_inc(even_out, 1)
                elif kind == 2:
                    act.activation(to(q2[HD:P, h, 0]), src, ACT.Identity, bias=b)
                    act.activation(to(q2[0:HD, h, 1]), src, ACT.Identity, bias=b).then_inc(even_out, 1)
                else:
                    row = kind // 2 * HD
                    act.activation(to(ks[row:row + HD, h]), src, ACT.Identity, bias=b).then_inc(even_out, 1)

            def qk(c, hh, n=None):
                if n is not None:
                    act.wait_ge(mag2_set, n + 1)
                    act.activation(mag[:, :], mag2[:, :, :].rearrange("p a n -> p (a n)"), ACT.Sqrt,
                                   bias=tiny[:, 0:1]).then_inc(mag_set, 1)
                for i in range(8):
                    take_even(c, hh, i)
                    if i == 1 and n is not None:
                        exponent(n)

            def exponent(n):
                act.wait_ge(less_top, n + 1)
                act.activation(ex[:, :, :], ex[:, :, :], ACT.Exp, scale=HD ** -0.5).then_inc(exp_set, 1)

            def take_o(c, hh, g):
                act.wait_ge(av_done, 8 * c + 4 * hh + g + 1 + CREDIT)
                if g == 0:
                    act.wait_ge(o_stored[hh], 64 * (c + 1))
                act.activation(o_out[:, hh, :, g:T:G], avp[g % 2][:, :].rearrange("p (h t) -> p h t", h=HH),
                               ACT.Copy).then_inc(o_set, 1)

            def body(c, last):
                qk(c, 1, 2 * c)
                for g in range(G):
                    take_o(c, 0, g)
                if not last:
                    qk(c + 1, 0, 2 * c + 1)
                else:
                    act.wait_ge(mag2_set, 2 * c + 2)
                    act.activation(mag[:, :], mag2[:, :, :].rearrange("p a n -> p (a n)"), ACT.Sqrt,
                                   bias=tiny[:, 0:1]).then_inc(mag_set, 1)
                    exponent(2 * c + 1)
                for g in range(G):
                    take_o(c, 1, g)

            for i in range(8):
                take_even(0, 0, i)
                if i in (0, 1, 4, 5):
                    high_w(2 + i // 4 * 2 + i % 4)
            with act.Fori(0, CH - 1) as c:
                body(c, False)
            body(CH - 1, True)

        @block.vector
        def _(dve):
            dve.sem_inc(odd_out, CREDIT)
            dve.sem_inc(score_out, CREDIT)
            dve.wait_ge(set_up, 2)
            dve.tensor_reduce(mask[:, :], ident[:, :].rearrange("p (m b) -> p b m", m=N), AX_X, ALU.add).then_inc(set_up, 1)

            def low_w(m):
                dve.wait_ge(w_hi_done, m + 1)
                dve.tensor_tensor(wt_lo[:, m].rearrange("p k n -> p (k n)"), raw[m],
                                  wt_hi[:, m].rearrange("p k n -> p (k n)").bitcast(F32), ALU.subtract).then_inc(w_lo_dve, 1)

            for m in BY_VECTOR[:2]:
                low_w(m)
            dve.wait_ge(small_in, 32)
            dve.wait_ge(set_up, 3)

            def take_odd(c, hh, i):
                j, kind = head_pair_and_kind(i)
                dve.wait_ge(proj_done, PER * c + qk_at[hh] + i + 1)
                src = proj[i % 2][HD:P, :].rearrange("p (t g) -> p g t", g=G)
                b = qkb[HD:P, kind, 2 * hh + j:2 * hh + j + 1]

                def to(x):
                    return x.rearrange("p (g t) -> p g t", g=G)

                h = 2 * j + 1
                if kind == 0:
                    dve.tensor_scalar(to(q2[0:HD, h, 0]), src, b, None, ALU.add)
                    dve.tensor_scalar(to(q2[HD:P, h, 1]), src, b, -1.0, ALU.add, ALU.mult).then_inc(odd_out, 1)
                elif kind == 2:
                    dve.tensor_scalar(to(q2[HD:P, h, 0]), src, b, None, ALU.add)
                    dve.tensor_scalar(to(q2[0:HD, h, 1]), src, b, None, ALU.add).then_inc(odd_out, 1)
                else:
                    row = kind // 2 * HD
                    dve.tensor_scalar(to(ks[row:row + HD, h]), src, b, None, ALU.add).then_inc(odd_out, 1)

            def take_v(c, i):
                g, r = i // 2, i % 2
                dve.wait_ge(proj_done, PER * c + V0 + i + 1)
                dve.tensor_tensor(v[:, g, :, r, :], proj[i % 2][:, :].rearrange("p (h d) -> p h d", h=H),
                                  vb[:, r].rearrange("p (h d) -> p h d", h=H), ALU.add).then_inc(odd_out, 1)

            def take_scores(c, hh, i):
                n = 16 * c + 8 * hh + i
                dve.wait_ge(score_done, n + 1)
                dve.tensor_tensor(masked[:, i % 2], scp[i % 2][:, :].rearrange("p (a b) -> p a b", b=GB),
                                  mask[:, :].unsqueeze(1).broadcast_to([P, 16, GB]), ALU.mult).then_inc(score_masked, 1)
                dve.wait_ge(score_masked, n + 1)
                dve.tensor_reduce(sc[:, i // 2, i % 2].rearrange("p h x n -> p (h x n)"), masked[:, i % 2],
                                  AX_X, ALU.add).then_inc(score_out, 1)

            def magnitudes(n):
                dve.wait_ge(score_out, 8 * n + 8 + CREDIT)
                s = sc[:, :, :, :, :, :].rearrange("p g a h x n -> p (g a h) x n")
                dve.tensor_tensor(sc_sq[:, :, :, :], s, s, ALU.mult).then_inc(squared2, 1)
                dve.wait_ge(squared2, n + 1)
                dve.tensor_tensor(mag2[:, :, :], sc_sq[:, :, 0, :], sc_sq[:, :, 1, :], ALU.add).then_inc(mag2_set, 1)

            def less_maximum(n):
                dve.wait_ge(mag_turned, n + 1)
                turned = tp[0:R, 0:P]
                dve.tensor_reduce(top[:, :], turned.rearrange("p (m b) -> p b m", m=N), AX_X, ALU.max).then_inc(top_set, 1)
                dve.wait_ge(top_set, n + 1)
                dve.tensor_tensor(ex[:, :, :], turned.rearrange("p (m b) -> p m b", m=N),
                                  top[:, :].unsqueeze(1).broadcast_to([R, N, GB]), ALU.subtract).then_inc(less_top, 1)

            def normalize(n):
                dve.wait_ge(exp_set, n + 1)
                dve.tensor_reduce(den[:, :], ex[:, :, :].rearrange("p m b -> p b m"), AX_X, ALU.add).then_inc(den_set, 1)
                dve.wait_ge(den_set, n + 1)
                dve.reciprocal(den[:, :], den[:, :]).then_inc(den_inv, 1)
                dve.wait_ge(den_inv, n + 1)
                dve.tensor_tensor(ex[:, :, :], ex[:, :, :], den[:, :].unsqueeze(1).broadcast_to([R, N, GB]),
                                  ALU.mult).then_inc(prob_set, 1)

            def keep_turned(n):
                dve.wait_ge(prob_turned, n + 1)
                dve.wait_ge(pt_set, n + CREDIT)
                dve.tensor_copy(w_t[:, :], tp[:, P:P + R]).then_inc(w_t_set, 1)

            def qk(c, hh, n=None):
                for i in range(8):
                    take_odd(c, hh, i)
                    if n is not None:
                        if i == 1:
                            less_maximum(n)
                        if i == 2:
                            normalize(n)
                        if i == 3:
                            keep_turned(n)

            def body(c, last):
                for i in range(8):
                    take_v(c, i)
                    take_scores(c, 0, i)
                magnitudes(2 * c)
                qk(c, 1, 2 * c)
                for i in range(8):
                    take_scores(c, 1, i)
                magnitudes(2 * c + 1)
                if not last:
                    qk(c + 1, 0, 2 * c + 1)
                else:
                    less_maximum(2 * c + 1)
                    normalize(2 * c + 1)
                    keep_turned(2 * c + 1)

            for i in range(8):
                take_odd(0, 0, i)
                if i == 5:
                    low_w(BY_VECTOR[2])
            with dve.Fori(0, CH - 1) as c:
                body(c, False)
            body(CH - 1, True)

        @block.tensor
        def _(pe):
            pe.wait_ge(set_up, 3)

            def three(out, a_hi, a_lo, b_hi, b_lo, first, last):
                pe.matmul(out, a_hi, b_hi, start=first, stop=False)
                pe.matmul(out, a_hi, b_lo, start=False, stop=False)
                return pe.matmul(out, a_lo, b_hi, start=False, stop=last)

            def bank_free(c, stage, i):
                pe.wait_ge(odd_out, PER * c + stage + i - 1 + CREDIT)
                if stage == V0:
                    pe.wait_ge(even_out, 16 * c + min(7 + i, 8) + CREDIT)
                else:
                    at = 16 * c + (8 if stage == QK1 else 0)
                    pe.wait_ge(even_out, at + (max(i - 1, 0) if stage == QK1 else i - 1) + CREDIT)

            def weights_in(m):
                if m in BY_VECTOR:
                    pe.wait_ge(w_lo_dve, BY_VECTOR.index(m) + 1)
                else:
                    pe.wait_ge(w_lo_pool, BY_POOL.index(m) + 1)

            def qk_tile(c, hh, i):
                j, kind = head_pair_and_kind(i)
                e = (2 * hh + j) * P
                r = kind // 2
                bank_free(c, qk_at[hh], i)
                for k in range(DT):
                    last = three(proj[i % 2][:, :], wt_hi[:, kind, k, e:e + P], wt_lo[:, kind, k, e:e + P],
                                 s_hi[:, r, k, :], s_lo[:, r, k, :], k == 0, k == DT - 1)
                last.then_inc(proj_done, 1)

            def v_tile(c, i):
                g, r = i // 2, i % 2
                bank_free(c, V0, i)
                for k in range(DT):
                    last = three(proj[i % 2][:, :], s_hi[:, r, k, g:T:G], s_lo[:, r, k, g:T:G],
                                 wt_hi[:, 4 + r, k, :], wt_lo[:, 4 + r, k, :], k == 0, k == DT - 1)
                last.then_inc(proj_done, 1)

            def scores(c, hh, i):
                g = i // 2
                n = 16 * c + 8 * hh + i
                if i == 0:
                    pe.wait_ge(odd_out, PER * c + qk_at[hh] + 8 + CREDIT)
                    pe.wait_ge(even_out, 16 * c + 8 * hh + 8 + CREDIT)
                pe.wait_ge(score_out, n - 1 + CREDIT)
                for a in range(2):
                    h = 2 * (i % 2) + a
                    last = pe.matmul(scp[i % 2][:, a * 2 * P:(a + 1) * 2 * P], ks[:, h, g * P:(g + 1) * P],
                                     q2[:, h, :, g * P:(g + 1) * P], start=a == 0, stop=a == 1, skip_group_check=True)
                last.then_inc(score_done, 1)

            def turn_magnitudes(n):
                pe.wait_ge(mag_set, n + 1)
                pe.matmul(tp[0:R, 0:P], mag[:, :], ident[:, :], start=True, stop=True).then_inc(mag_turned, 1)

            def turn_probabilities(n):
                pe.wait_ge(set_up, 3)
                pe.wait_ge(prob_set, n + 1)
                pe.transpose(tp[:, P:P + R], ex[:, :, :].rearrange("p m b -> p (m b)"),
                             ident[0:R, 0:R]).then_inc(prob_turned, 1)

            def attend(c, hh, g):
                if g == 0:
                    pe.wait_ge(pt_set, 2 * c + hh + 1 + CREDIT)
                    pe.wait_ge(odd_out, PER * c + V0 + 8 + CREDIT)
                n = 8 * c + 4 * hh + g
                pe.wait_ge(o_set, n - 1 + CREDIT)
                for a in range(HH):
                    last = pe.matmul(avp[g % 2][:, a * P:(a + 1) * P],
                                     v[:, g, HH * hh + a].rearrange("p r d -> p (r d)"),
                                     pt[:, g * HH + a, :], start=a == 0, stop=a == HH - 1, skip_group_check=True)
                last.then_inc(av_done, 1)

            def qk(c, hh, n=None):
                for i in range(8):
                    if hh == 0 and i in (0, 4):
                        pe.wait_ge(s_in[i // 4], 32 * (c + 1))
                    qk_tile(c, hh, i)
                    if n is not None:
                        if i == 1:
                            turn_magnitudes(n)
                        if i == 3:
                            turn_probabilities(n)

            def body(c, last):
                for i in range(8):
                    v_tile(c, i)
                    scores(c, 0, i)
                qk(c, 1, 2 * c)
                for i in range(8):
                    if i % 2 == 0:
                        attend(c, 0, i // 2)
                    scores(c, 1, i)
                if not last:
                    qk(c + 1, 0, 2 * c + 1)
                else:
                    turn_magnitudes(2 * c + 1)
                    turn_probabilities(2 * c + 1)
                for g in range(G):
                    attend(c, 1, g)

            for i in range(8):
                weights_in(head_pair_and_kind(i)[1])
                if i in (0, 4):
                    pe.wait_ge(s_in[i // 4], 32)
                qk_tile(0, 0, i)
            for m in (4, 5):
                weights_in(m)
            with pe.Fori(0, CH - 1) as c:
                body(c, False)
            body(CH - 1, True)


def interact(nc, sems, wo_w, wo_bias, int_w, o_dram, z_dram):
    UNITS = HALVES * N
    MAT = DT * D
    BT = HB // P
    BASE = 4

    with ExitStack() as ctx:
        def sb(name, shape, dt=F32):
            return ctx.enter_context(nc.sbuf_tensor(name, shape, dt))

        def sem(name):
            return sems.enter_context(nc.semaphore(name))

        wo_hi = sb("wo_hi", [P, 2, MAT], F32R)
        wo_lo = sb("wo_lo", [P, 2, MAT], F32R)
        o_raw = sb("o_raw", [P, DT, HB])
        o_hi = sb("o_hi", [P, 2, DT, HB], F32R)
        o_lo = sb("o_lo", [P, 2, DT, HB], F32R)
        maps = sb("maps", [P, 3, MAT])
        m_hi = sb("m_hi", [P, 3, MAT], F32R)
        m_lo = sb("m_lo", [P, 3, MAT], F32R)
        a_hi = sb("a_hi", [P, 3, DT, HB], F32R)
        a_lo = sb("a_lo", [P, 3, DT, HB], F32R)
        a_raw = sb("a_raw", [P, 3, HB])
        z_out = sb("z_out", [P, 2, 2, D])
        wo_b = sb("wo_b", [P, 2, DT])
        wops = [ctx.enter_context(nc.psum_tensor(f"wops{u}", [P, HB], F32)) for u in range(2)]
        kps = [[ctx.enter_context(nc.psum_tensor(f"kps{u}{x}", [P, D], F32)) for x in range(3)] for u in range(2)]
        wo_raw = [maps[:, 2, :], z_out[:, :, :, :].rearrange("p u r d -> p (u r d)")]
        first_o_i = maps[:, 2, :].rearrange("p (k b) -> p k b", k=DT)

        wo_in = [sem(f"wo_in{u}") for u in range(2)]
        small_in = sem("small_in3")
        o_in = sem("o_in")
        first_o_in = sem("first_o_in")
        w_in = [sem(f"w_in3{r}") for r in range(2)]
        wo_hi_done = sem("wo_hi_done")
        wo_lo_done = sem("wo_lo_done")
        names = ("o_hi_done o_lo_done difference summed m_hi_done m_lo_pool m_lo_dve wo_done a_raw_set a_sum_set "
                 "a_hi_done a_lo_done k_done k1_out z_set").split()
        S = {n: sem("i_" + n) for n in names}
        z_stored = [sem(f"z_stored{u}") for u in range(2)]

        block = ctx.enter_context(nc.Block())

        @block.sync
        def _(sp):
            def load_o(h, n, r, into=o_raw):
                for hh in range(2):
                    for d in range(2):
                        sp.dma_start(into[:, 2 * hh + d, :].rearrange("p (c b) -> p c b", b=P),
                                     o_dram[r, hh, bass.ds(h * BT, BT), :, d, bass.ds(n * P, P)]
                                     .rearrange("c p b -> p c b")).then_inc(o_in if into is o_raw else first_o_in, 16)

            def load_w(n, r):
                sp.dma_start(maps[:, r, :], int_w[r, bass.ds(n, 1)].rearrange("n p m -> p (n m)")).then_inc(w_in[r], 16)

            def store(h, n, k, m):
                sp.wait_ge(S["z_set"], 2 * BT * k + 2 * m + 2 + BASE)
                sp.dma_start(z_dram[bass.ds(h * BT + m, 1), :, :, bass.ds(n, 1), :].rearrange("c b r n d -> b (c r) (n d)"),
                             z_out[:, m % 2, :, :]).then_inc(z_stored[m % 2], 32)

            sp.dma_start(wo_raw[0], wo_w[0]).then_inc(wo_in[0], 16)
            load_o(0, 0, 0)
            sp.dma_start(wo_raw[1], wo_w[1]).then_inc(wo_in[1], 16)
            sp.wait_ge(wo_lo_done, 1)
            load_o(0, 0, 1, first_o_i)
            sp.dma_start(wo_b[:, :, :], wo_bias).then_inc(small_in, 16)
            for u in range(2):
                sp.sem_inc(z_stored[u], 32)
            load_w(0, 0)
            load_w(0, 1)

            def unit(h, n, h1, n1, last):
                k = h * N + n
                if not last:
                    sp.wait_ge(S["o_hi_done"], 2 * k + 2 + BASE)
                    sp.wait_ge(S["o_lo_done"], 2 * k + 2 + BASE)
                    load_o(h1, n1, 0)
                    sp.wait_ge(S["m_lo_pool"], 2 * k + 2 + BASE)
                    sp.wait_ge(S["m_lo_dve"], 2 * k + 2 + BASE)
                    for r in range(2):
                        load_w(n1, r)
                    sp.wait_ge(S["o_hi_done"], 2 * k + 3 + BASE)
                    sp.wait_ge(S["o_lo_done"], 2 * k + 3 + BASE)
                    load_o(h1, n1, 1)
                for m in range(BT):
                    store(h, n, k, m)

            for h in range(HALVES):
                with sp.Fori(0, N - 1) as n:
                    unit(h, n, h, n + 1, False)
                unit(h, N - 1, h + 1, 0, h == HALVES - 1)
            for u in range(2):
                sp.wait_ge(z_stored[u], 32 * (UNITS * BT // 2 + 1))

        @block.gpsimd
        def _(pool):
            for n in names:
                pool.sem_inc(S[n], BASE)

            def low_m(k):
                for x in range(2):
                    pool.wait_ge(S["m_hi_done"], 3 * k + x + 1 + BASE)
                    pool.tensor_tensor(m_lo[:, x, :], maps[:, x, :], m_hi[:, x, :].bitcast(F32),
                                       ALU.subtract).then_inc(S["m_lo_pool"], 1)

            def low_o(k, r):
                pool.wait_ge(S["o_hi_done"], 2 * k + r + 1 + BASE)
                pool.tensor_tensor(o_lo[:, r].rearrange("p a b -> p (a b)"), o_raw[:, :, :].rearrange("p a b -> p (a b)"),
                                   o_hi[:, r].rearrange("p a b -> p (a b)").bitcast(F32), ALU.subtract).then_inc(S["o_lo_done"], 1)

            with pool.Fori(0, UNITS - 1) as k:
                low_m(k)
                for r in range(2):
                    low_o(k + 1, r)
            low_m(UNITS - 1)

        @block.scalar
        def _(act):
            def high_wo(u):
                act.wait_ge(wo_in[u], 16)
                act.activation(wo_hi[:, u, :], wo_raw[u], ACT.Copy).then_inc(wo_hi_done, 1)

            def high_o(k, r, loads, src=o_raw):
                act.wait_ge(S["wo_done"], 2 * DT * k + BASE)
                if src is o_raw:
                    act.wait_ge(o_in, 64 * loads)
                else:
                    act.wait_ge(first_o_in, 64)
                act.activation(o_hi[:, r].rearrange("p a b -> p (a b)"), src[:, :, :].rearrange("p a b -> p (a b)"),
                               ACT.Copy).then_inc(S["o_hi_done"], 1)

            def high_m(k, x):
                act.wait_ge(S["k_done"], BT * k + BASE)
                if x == 0:
                    act.wait_ge(w_in[0], 16 * (k + 1))
                else:
                    act.wait_ge(S["difference"], k + 1 + BASE)
                    act.wait_ge(S["summed"], k + 1 + BASE)
                act.activation(m_hi[:, x, :], maps[:, x, :], ACT.Copy).then_inc(S["m_hi_done"], 1)

            def project(k, j):
                act.wait_ge(S["a_lo_done"], 3 * DT * k + 3 * j + BASE)
                for r in range(2):
                    act.wait_ge(S["wo_done"], 2 * DT * k + 2 * j + r + 1 + BASE)
                    act.activation(a_raw[:, 2 - r, :], wops[r][:, :], ACT.Identity,
                                   bias=wo_b[:, r, j:j + 1]).then_inc(S["a_raw_set"], 1)
                act.wait_ge(S["a_raw_set"], 2 * DT * k + 2 * j + 2 + BASE)
                act.activation(a_hi[:, 2, j, :], a_raw[:, 2, :], ACT.Copy).then_inc(S["a_hi_done"], 1)
                act.activation(a_hi[:, 1, j, :], a_raw[:, 1, :], ACT.Copy).then_inc(S["a_hi_done"], 1)
                act.wait_ge(S["a_sum_set"], DT * k + j + 1 + BASE)
                act.activation(a_hi[:, 0, j, :], a_raw[:, 0, :], ACT.Copy).then_inc(S["a_hi_done"], 1)

            def first_term(k, m):
                u = m % 2
                act.wait_ge(S["k_done"], BT * k + m + 1 + BASE)
                act.wait_ge(z_stored[u], 32 * (BT // 2 * k + m // 2 + 1))
                act.activation(z_out[:, u, 0, :], kps[u][0][:, :], ACT.Copy).then_inc(S["k1_out"], 1)

            def unit(k, last):
                high_m(k, 0)
                project(k, 0)
                project(k, 1)
                high_m(k, 1)
                project(k, 2)
                high_m(k, 2)
                project(k, 3)
                for m in range(BT):
                    if not last and m in (0, 2):
                        high_o(k + 1, m // 2, 2 * k + 2 + m // 2)
                    first_term(k, m)

            high_wo(0)
            high_o(0, 0, 1)
            high_wo(1)
            high_o(0, 1, 0, first_o_i)
            act.wait_ge(small_in, 16)
            act.wait_ge(wo_lo_done, 2)
            with act.Fori(0, UNITS - 1) as k:
                unit(k, False)
            unit(UNITS - 1, True)

        @block.vector
        def _(dve):
            def combine(k):
                for r in range(2):
                    dve.wait_ge(w_in[r], 16 * (k + 1))
                dve.wait_ge(S["m_lo_dve"], 2 * k + BASE)
                dve.tensor_tensor(maps[:, 2, :], maps[:, 1, :], maps[:, 0, :], ALU.subtract).then_inc(S["difference"], 1)
                dve.wait_ge(S["difference"], k + 1 + BASE)
                dve.tensor_tensor(maps[:, 1, :], maps[:, 1, :], maps[:, 0, :], ALU.add).then_inc(S["summed"], 1)

            def low_a(k, j):
                dve.wait_ge(S["a_raw_set"], 2 * DT * k + 2 * j + 2 + BASE)
                dve.tensor_tensor(a_raw[:, 0, :], a_raw[:, 1, :], a_raw[:, 2, :], ALU.add).then_inc(S["a_sum_set"], 1)
                for n, x in enumerate((2, 1, 0)):
                    dve.wait_ge(S["a_hi_done"], 3 * DT * k + 3 * j + n + 1 + BASE)
                    dve.tensor_tensor(a_lo[:, x, j, :], a_raw[:, x, :], a_hi[:, x, j, :].bitcast(F32),
                                      ALU.subtract).then_inc(S["a_lo_done"], 1)

            def keep_z(k, m):
                u = m % 2
                dve.wait_ge(S["k1_out"], BT * k + m + 1 + BASE)
                dve.tensor_tensor(z_out[:, u, 1, :], z_out[:, u, 0, :], kps[u][2][:, :], ALU.add).then_inc(S["z_set"], 1)
                dve.wait_ge(S["z_set"], 2 * BT * k + 2 * m + 1 + BASE)
                dve.tensor_tensor(z_out[:, u, 0, :], z_out[:, u, 0, :], kps[u][1][:, :], ALU.subtract).then_inc(S["z_set"], 1)

            def unit(k, last):
                for j in range(DT - 1):
                    low_a(k, j)
                dve.wait_ge(S["m_hi_done"], 3 * k + 3 + BASE)
                for n in range(2):
                    cols = slice(n * MAT // 2, (n + 1) * MAT // 2)
                    dve.tensor_tensor(m_lo[:, 2, cols], maps[:, 2, cols], m_hi[:, 2, cols].bitcast(F32),
                                      ALU.subtract).then_inc(S["m_lo_dve"], 1)
                low_a(k, DT - 1)
                keep_z(k, 0)
                keep_z(k, 1)
                if not last:
                    combine(k + 1)
                keep_z(k, 2)
                keep_z(k, 3)

            def low_wo(u):
                dve.wait_ge(wo_hi_done, u + 1)
                dve.tensor_tensor(wo_lo[:, u, :], wo_raw[u], wo_hi[:, u, :].bitcast(F32), ALU.subtract).then_inc(wo_lo_done, 1)

            def low_first_o(r, src):
                dve.wait_ge(S["o_hi_done"], r + 1 + BASE)
                dve.tensor_tensor(o_lo[:, r].rearrange("p a b -> p (a b)"), src[:, :, :].rearrange("p a b -> p (a b)"),
                                  o_hi[:, r].rearrange("p a b -> p (a b)").bitcast(F32), ALU.subtract).then_inc(S["o_lo_done"], 1)

            low_wo(0)
            low_first_o(0, o_raw)
            low_wo(1)
            low_first_o(1, first_o_i)
            dve.wait_ge(S["o_lo_done"], 2 + BASE)
            combine(0)
            with dve.Fori(0, UNITS - 1) as k:
                unit(k, False)
            unit(UNITS - 1, True)

        @block.tensor
        def _(pe):
            def three(out, a_h, a_l, b_h, b_l, first, last):
                pe.matmul(out, a_h, b_h, start=first, stop=False)
                pe.matmul(out, a_h, b_l, start=False, stop=False)
                return pe.matmul(out, a_l, b_h, start=False, stop=last)

            def product(m, x, features):
                for d in features:
                    b = slice(m * P, (m + 1) * P)
                    w = slice(d * D, (d + 1) * D)
                    last = three(kps[m % 2][x][:, :], a_hi[:, x, d, b], a_lo[:, x, d, b], m_hi[:, x, w], m_lo[:, x, w],
                                 d == 0, d == DT - 1)
                return last

            def unit(k):
                for j in range(DT):
                    for r in range(2):
                        if j == 0:
                            pe.wait_ge(wo_lo_done, r + 1)
                            pe.wait_ge(S["o_lo_done"], 2 * k + r + 1 + BASE)
                        pe.wait_ge(S["a_raw_set"], 2 * DT * k + 2 * j + r - 1 + BASE)
                        for d in range(DT):
                            w = slice(d * D + j * P, d * D + (j + 1) * P)
                            last = three(wops[r][:, :], wo_hi[:, r, w], wo_lo[:, r, w], o_hi[:, r, d, :], o_lo[:, r, d, :],
                                         d == 0, d == DT - 1)
                        last.then_inc(S["wo_done"], 1)
                pe.wait_ge(S["a_lo_done"], 3 * DT * (k + 1) - 3 + BASE)
                for m in range(2):
                    pe.wait_ge(S["z_set"], 2 * BT * k + 2 * m - 2 + BASE)
                    for x in range(3):
                        if m == 0 and x < 2:
                            pe.wait_ge(S["m_lo_pool"], 2 * k + x + 1 + BASE)
                        elif m == 0:
                            pe.wait_ge(S["m_lo_dve"], 2 * k + 2 + BASE)
                        product(m, x, range(DT - 1))
                pe.wait_ge(S["a_lo_done"], 3 * DT * (k + 1) + BASE)
                for m in range(2):
                    for x in range(3):
                        last = product(m, x, (DT - 1,))
                    last.then_inc(S["k_done"], 1)
                for m in range(2, BT):
                    pe.wait_ge(S["z_set"], 2 * BT * k + 2 * m - 2 + BASE)
                    for x in range(3):
                        last = product(m, x, range(DT))
                    last.then_inc(S["k_done"], 1)

            with pe.Fori(0, UNITS) as k:
                unit(k)


LEAST = 1e-34


def finish(nc, sems, st, meas_w, post_w, post_b, post_gb, top1_w, top2_w, top3_w, top2_b, z_dram, hx_dram, out):
    PAIRS = [(0, 1), (1, 2), (2, 3), (0, 2), (1, 3), (0, 3)]
    SHIFTS = [(1, 0, 3), (2, 3, 5), (3, 5, 6)]
    pair_of = {frozenset(p): n for n, p in enumerate(PAIRS)}
    MAT = DT * D
    T1 = 512 // P
    T2 = 256 // P
    DH = D // 2
    BASE = 2

    with ExitStack() as ctx:
        def sb(name, shape, dt=F32):
            return ctx.enter_context(nc.sbuf_tensor(name, shape, dt))

        def sem(name):
            return sems.enter_context(nc.semaphore(name))

        def ps(name):
            return ctx.enter_context(nc.psum_tensor(name, [P, 512], F32))

        z = sb("z", [P, 2, 2, 2, N, DH])
        unit = sb("unit", [P, 2, 2, N, DH])
        p2 = sb("p2", [P, N, DH])
        root = sb("root", [P, N, DH])
        both = sb("both", [P, N // 2, DH])
        flag = sb("flag", [P, 2, N, DH])
        cos = sb("cos", [P, 2, 6, DH])
        part = sb("part", [P, 6, DH])
        coef = sb("coef", [P, 2, N, DH])
        sup_t = sb("sup_t", [P, 3, D])
        sup_sq = sb("sup_sq", [P, 2, D])
        inv = sb("inv", [P, 1])
        m_sq = sb("m_sq", [P, 2, D])
        amp = sb("amp", [P, D])
        amp_t = sb("amp_t", [P, D])
        y = sb("y", [P, D])
        stats = sb("stats", [P, 6])
        mv = sb("mv", [P, 2])
        rs = sb("rs", [P, 1])
        z_t = sb("z_t", [P, DT, P])
        ident = sb("ident4", [P, P])
        ones = sb("ones4", [P, 1])
        eps = sb("eps4", [P, 1])
        least = sb("least4", [P, 1])
        mw = sb("mw", [P, 2, MAT])
        pw = sb("pw", [P, MAT])
        bias = sb("bias4", [P, 1, D])
        gb = sb("gb4", [P, 2, DT])
        w1 = sb("w1", [P, MAT])
        w2 = sb("w2", [P, DT, 256])
        w3 = sb("w3", [P, T2])
        b2 = sb("b2", [P, T2])
        hx = sb("hx", [P, CH + 1, T1, P])
        h1 = sb("h1", [P, T1, P])
        h2 = sb("h2", [P, T2, P])
        y_out = sb("y_out", [1, CH + 1, P])
        turn = [ps("turn_r"), ps("turn_i")]
        mea = [ps("mea_r"), ps("mea_i")]
        ampp, postp, zp = ps("ampp"), ps("postp"), ps("zp")
        ssp = ps("ssp")
        h2p, yp = postp[:, 0:T2 * P], postp[0:1, T2 * P:(T2 + 1) * P]

        z_in = [[sem(f"z_in{v}{h}") for h in range(2)] for v in range(2)]
        made = sem("made")
        names = ("z_sq p2_set flag_set p_root both_set both_inv p_inv unit_set cos1 part1 part2 part3 cos_set coef0 coef1 coef2 "
                 "prod_set sup_turned sup_t_set sup_sq_set ss_set ss_more inv_set meas_done m_sq_set amp2_set amp_set "
                 "amp_turned amp_t_set post_done y_set stat_set mv_set var_root rs_set y_norm y_turned z_t_set "
                 "h1_done h1_set h2_done h2_set y_done y_copied").split()
        S = {n: sem("f_" + n) for n in names}
        TOP_IN = 16 * (4 + HALVES * T1)
        meas_in, post_in, top_in, y_stored = sem("meas_in"), sem("post_in"), sem("top_in"), sem("y_stored")
        block = ctx.enter_context(nc.Block())

        def flat(x):
            return x.rearrange("p n d -> p (n d)")

        def strength(c, i, j):
            return st[:, bass.ds(c, 1), i, j:j + 1].rearrange("p a b -> p (a b)")

        @block.sync
        def _(sp):
            def load_z(c, v, h):
                for r in range(2):
                    sp.dma_start(z[:, v, h, r], z_dram[bass.ds(c, 1), :, r, :, h * DH:(h + 1) * DH]
                                 .rearrange("c p n d -> p (c n) d")).then_inc(z_in[v][h], 16)

            for v in range(2):
                for h in range(2):
                    load_z(v, v, h)
            for r in range(2):
                sp.dma_start(mw[:, r, :], meas_w[r]).then_inc(meas_in, 16)
            sp.dma_start(pw[:, :], post_w).then_inc(post_in, 16)
            sp.dma_start(bias[:, :, :], post_b.partition_broadcast(P)).then_inc(post_in, 16)
            sp.dma_start(gb[:, :, :], post_gb).then_inc(post_in, 16)
            sp.dma_start(w1[:, :], top1_w).then_inc(top_in, 16)
            sp.dma_start(w2[:, :, :], top2_w).then_inc(top_in, 16)
            sp.dma_start(w3[:, :], top3_w).then_inc(top_in, 16)
            sp.dma_start(b2[:, :], top2_b).then_inc(top_in, 16)
            for h in range(HALVES):
                for t in range(T1):
                    chunks = slice(1 + h * HB // P, 1 + (h + 1) * HB // P)
                    sp.dma_start(hx[:, chunks, t, :], hx_dram[h, :, t, :].rearrange("p (c b) -> p c b", b=P)).then_inc(top_in, 16)
            with sp.Fori(1, CH // 2) as i:
                for v in range(2):
                    for h in range(2):
                        sp.wait_ge(S["sup_turned"], 4 * i + 2 * v + h - 3 + BASE)
                        load_z(2 * i + v, v, h)
            sp.wait_ge(S["y_copied"], CH + 1 + BASE)
            sp.dma_start(out.rearrange("(c b) o -> o c b", b=P), y_out[0:1, 1:CH + 1, :]).then_inc(y_stored, 16)
            sp.wait_ge(y_stored, 16)

        @block.gpsimd
        def _(pool):
            for n in names:
                pool.sem_inc(S[n], BASE)
            pool.memset(ident[:, :], 0.0).then_inc(made, 1)
            pool.wait_ge(made, 1)
            pool.affine_select(out=ident[:, :], in_=ident[:, :], compare_op=ALU.not_equal, fill=1.0,
                               base=0, pattern=[[-1, P]], channel_multiplier=1).then_inc(made, 1)
            pool.memset(ones[:, :], 1.0)
            pool.memset(z_t[:, :, :], 0.0)
            pool.memset(hx[:, 0], 0.0)
            pool.memset(eps[:, :], EPS)
            pool.memset(least[:, :], LEAST * 1e-3).then_inc(made, 1)

            def cosines(m, h):
                pool.wait_ge(S["unit_set"], m + 1 + BASE)
                pool.wait_ge(S["cos_set"], m + BASE)
                for s, a, b in SHIFTS:
                    last = pool.tensor_tensor(part[:, a:b], unit[:, h, 1, 0:N - s], unit[:, h, 1, s:N], ALU.mult)
                last.then_inc(S["part1"], 1)
                pool.wait_ge(S["part1"], m + 1 + BASE)
                pool.wait_ge(S["flag_set"], m + 1 + BASE)
                for s, a, b in SHIFTS:
                    last = pool.tensor_tensor(part[:, a:b], part[:, a:b], flag[:, h, 0:N - s], ALU.add)
                last.then_inc(S["part2"], 1)
                pool.wait_ge(S["part2"], m + 1 + BASE)
                for s, a, b in SHIFTS:
                    last = pool.tensor_tensor(part[:, a:b], part[:, a:b], flag[:, h, s:N], ALU.add)
                last.then_inc(S["part3"], 1)
                pool.wait_ge(S["part3"], m + 1 + BASE)
                pool.wait_ge(S["cos1"], m + 1 + BASE)
                pool.tensor_tensor(flat(cos[:, h]), flat(cos[:, h]), flat(part[:, :, :]), ALU.add).then_inc(S["cos_set"], 1)

            with pool.Fori(0, CH) as c:
                for h in range(2):
                    cosines(2 * c + h, h)

        @block.scalar
        def _(act):
            def squares(m, v, h, n):
                act.wait_ge(z_in[v][h], 32 * (n + 1))
                act.wait_ge(S["part1"], m - 1 + BASE)
                act.wait_ge(S["cos1"], m - 1 + BASE)
                act.activation(unit[:, h].rearrange("p r n d -> p (r n d)"), z[:, v, h].rearrange("p r n d -> p (r n d)"),
                               ACT.Square).then_inc(S["z_sq"], 1)

            def roots(m, h):
                act.wait_ge(S["p2_set"], m + 1 + BASE)
                act.wait_ge(S["p_inv"], m + BASE)
                act.wait_ge(S["part3"], m - 1 + BASE)
                act.activation(flat(root[:, :, :]), flat(p2[:, :, :]), ACT.Sqrt, bias=least[:, 0:1]).then_inc(S["p_root"], 1)
                act.activation(flat(flag[:, h]), flat(p2[:, :, :]), ACT.Relu, scale=-1 / LEAST,
                               bias=ones[:, 0:1]).then_inc(S["flag_set"], 1)

            def first_coefficients(c, h):
                m = 2 * c + h
                act.wait_ge(made, 3)
                act.wait_ge(S["cos_set"], m + 1 + BASE)
                for j in range(N):
                    i = 0 if j else 1
                    last = act.activation(coef[:, h, j, :], cos[:, h, pair_of[frozenset((i, j))], :], ACT.Identity,
                                          scale=strength(c, i, j), bias=strength(c, j, j))
                last.then_inc(S["coef0"], 1)

            def keep_turned(c):
                act.wait_ge(S["sup_turned"], 2 * c + 2 + BASE)
                act.wait_ge(S["meas_done"], c + BASE)
                act.activation(sup_t[:, 0, :], turn[0][:, :], ACT.Copy)
                act.activation(sup_t[:, 1, :], turn[1][:, :], ACT.Copy)
                act.activation(sup_t[:, 2, :], turn[1][:, :], ACT.Copy, scale=-1.0).then_inc(S["sup_t_set"], 1)
                act.wait_ge(S["ss_set"], c + BASE)
                act.activation(sup_sq[:, 0, :], turn[0][:, :], ACT.Square)
                act.activation(sup_sq[:, 1, :], turn[1][:, :], ACT.Square).then_inc(S["sup_sq_set"], 1)

            def measured_squares(c):
                act.wait_ge(S["meas_done"], c + 1 + BASE)
                act.wait_ge(S["amp2_set"], c + BASE)
                act.activation(m_sq[:, 0, :], mea[0][:, :], ACT.Square)
                act.activation(m_sq[:, 1, :], mea[1][:, :], ACT.Square).then_inc(S["m_sq_set"], 1)

            def amp_root(c):
                act.wait_ge(S["amp2_set"], c + 1 + BASE)
                act.activation(amp[:, :], amp[:, :], ACT.Sqrt, scale=inv[:, 0:1]).then_inc(S["amp_set"], 1)

            def var_root(c):
                act.wait_ge(S["mv_set"], c + 1 + BASE)
                act.activation(rs[:, :], mv[:, 1:2], ACT.Sqrt, bias=eps[:, 0:1]).then_inc(S["var_root"], 1)

            def keep_amp(c):
                act.wait_ge(S["amp_turned"], c + 1 + BASE)
                act.wait_ge(S["post_done"], c + BASE)
                act.activation(amp_t[:, :], ampp[:, :], ACT.Copy).then_inc(S["amp_t_set"], 1)

            def gelu(c):
                act.wait_ge(S["y_turned"], c + 1 + BASE)
                act.wait_ge(S["h1_done"], c + 1 + BASE)
                for k in range(DT):
                    last = act.activation(z_t[:, k, :], zp[:, k * P:(k + 1) * P], ACT.Gelu,
                                          scale=gb[:, 0, k:k + 1], bias=gb[:, 1, k:k + 1])
                last.then_inc(S["z_t_set"], 1)

            def relu1(c):
                act.wait_ge(S["h1_done"], c + 2 + BASE)
                act.wait_ge(S["h2_done"], c + 1 + BASE)
                act.activation(h1[:, :, :].rearrange("p t b -> p (t b)"), zp[:, :], ACT.Relu).then_inc(S["h1_set"], 1)

            def relu2(c):
                act.wait_ge(S["h2_done"], c + 2 + BASE)
                act.wait_ge(S["y_done"], c + 1 + BASE)
                for t in range(T2):
                    last = act.activation(h2[:, t, :], h2p[:, t * P:(t + 1) * P], ACT.Relu, bias=b2[:, t:t + 1])
                last.then_inc(S["h2_set"], 1)

            def keep_y(c):
                act.wait_ge(top_in, TOP_IN)
                act.wait_ge(S["y_done"], c + 2 + BASE)
                act.activation(y_out[:, bass.ds(c + 1, 1), :].rearrange("p a b -> p (a b)"), yp, ACT.Copy).then_inc(S["y_copied"], 1)

            def beside(c, v, n1, last):
                if not last:
                    squares(2 * c + 2, 1 - v, 0, n1)
                first_coefficients(c, 0)
                if not last:
                    roots(2 * c + 2, 0)
                measured_squares(c - 1)
                if not last:
                    squares(2 * c + 3, 1 - v, 1, n1)
                amp_root(c - 1)
                first_coefficients(c, 1)
                relu1(c - 2)
                keep_amp(c - 1)
                relu2(c - 2)
                if not last:
                    roots(2 * c + 3, 1)
                keep_y(c - 2)
                var_root(c - 1)
                keep_turned(c)
                gelu(c - 1)

            act.wait_ge(made, 3)
            squares(0, 0, 0, 0)
            squares(1, 0, 1, 0)
            roots(0, 0)
            roots(1, 1)
            squares(2, 1, 0, 0)
            first_coefficients(0, 0)
            roots(2, 0)
            squares(3, 1, 1, 0)
            first_coefficients(0, 1)
            roots(3, 1)
            act.wait_ge(post_in, 48)
            keep_turned(0)
            with act.Fori(0, CH // 2 - 1) as i:
                beside(2 * i + 1, 1, i + 1, False)
                beside(2 * i + 2, 0, i + 1, False)
            beside(CH - 1, 1, 0, True)
            measured_squares(CH - 1)
            amp_root(CH - 1)
            relu1(CH - 2)
            keep_amp(CH - 1)
            var_root(CH - 1)
            relu2(CH - 2)
            gelu(CH - 1)
            keep_y(CH - 2)
            relu1(CH - 1)
            relu2(CH - 1)
            keep_y(CH - 1)

        @block.vector
        def _(dve):
            def absolute(m, h):
                dve.wait_ge(S["z_sq"], m + 1 + BASE)
                dve.wait_ge(S["unit_set"], m + BASE)
                dve.tensor_tensor(flat(p2[:, :, :]), flat(unit[:, h, 0]), flat(unit[:, h, 1]), ALU.add).then_inc(S["p2_set"], 1)

            def units(m, v, h, between=None):
                dve.wait_ge(S["p_root"], m + 1 + BASE)
                dve.tensor_tensor(both[:, :, :], root[:, 0:2, :], root[:, 2:4, :], ALU.mult).then_inc(S["both_set"], 1)
                dve.wait_ge(S["both_set"], m + 1 + BASE)
                dve.reciprocal(flat(both[:, :, :]), flat(both[:, :, :])).then_inc(S["both_inv"], 1)
                if between:
                    between()
                dve.wait_ge(S["flag_set"], m + 1 + BASE)
                dve.wait_ge(S["both_inv"], m + 1 + BASE)
                dve.tensor_tensor(p2[:, 0:2, :], both[:, :, :], root[:, 2:4, :], ALU.mult)
                dve.tensor_tensor(p2[:, 2:4, :], both[:, :, :], root[:, 0:2, :], ALU.mult).then_inc(S["p_inv"], 1)
                dve.wait_ge(S["p_inv"], m + 1 + BASE)
                dve.tensor_tensor(unit[:, h].rearrange("p r n d -> p r (n d)"), z[:, v, h].rearrange("p r n d -> p r (n d)"),
                                  flat(p2[:, :, :]).unsqueeze(1).broadcast_to([P, 2, N * DH]), ALU.mult).then_inc(S["unit_set"], 1)
                dve.wait_ge(S["unit_set"], m + 1 + BASE)
                dve.wait_ge(S["prod_set"], m - 1 + BASE)
                for s, a, b in SHIFTS:
                    last = dve.tensor_tensor(cos[:, h, a:b], unit[:, h, 0, 0:N - s], unit[:, h, 0, s:N], ALU.mult)
                last.then_inc(S["cos1"], 1)

            def sums(c, v, h):
                m = 2 * c + h
                for k in (1, 2):
                    dve.wait_ge(S[f"coef{k - 1}"], m + 1 + BASE)
                    for j in range(N):
                        i = [x for x in range(N) if x != j][k]
                        last = dve.scalar_tensor_tensor(out=coef[:, h, j, :], in0=cos[:, h, pair_of[frozenset((i, j))], :],
                                                        scalar=strength(c, i, j), in1=coef[:, h, j, :],
                                                        op0=ALU.mult, op1=ALU.add)
                    last.then_inc(S[f"coef{k}"], 1)
                dve.wait_ge(S["coef2"], m + 1 + BASE)
                zz = z[:, v, h].rearrange("p r n d -> p r (n d)")
                dve.tensor_tensor(zz, zz, flat(coef[:, h]).unsqueeze(1).broadcast_to([P, 2, N * DH]), ALU.mult).then_inc(S["prod_set"], 1)

            def amplitude(c):
                dve.wait_ge(S["ss_set"], c + 1 + BASE)
                dve.wait_ge(S["amp_set"], c + BASE)
                dve.tensor_scalar(inv[:, :], ssp[:, 0:1], 1e-8, None, ALU.add).then_inc(S["ss_more"], 1)
                dve.wait_ge(S["ss_more"], c + 1 + BASE)
                dve.reciprocal(inv[:, :], inv[:, :]).then_inc(S["inv_set"], 1)
                dve.wait_ge(S["m_sq_set"], c + 1 + BASE)
                dve.wait_ge(S["inv_set"], c + 1 + BASE)
                dve.wait_ge(S["amp_turned"], c + BASE)
                dve.tensor_tensor(amp[:, :], m_sq[:, 0, :], m_sq[:, 1, :], ALU.add).then_inc(S["amp2_set"], 1)

            def post(c):
                dve.wait_ge(S["post_done"], c + 1 + BASE)
                dve.wait_ge(S["y_turned"], c + BASE)
                dve.tensor_tensor(y[:, :], postp[:, :], bias[:, 0, :], ALU.add).then_inc(S["y_set"], 1)
                dve.wait_ge(S["y_set"], c + 1 + BASE)
                dve.bn_stats(stats[:, :], y[:, :]).then_inc(S["stat_set"], 1)
                dve.wait_ge(post_in, 48)
                dve.wait_ge(S["stat_set"], c + 1 + BASE)
                dve.bn_aggr(mv[:, :], stats[:, :]).then_inc(S["mv_set"], 1)
                dve.wait_ge(S["var_root"], c + 1 + BASE)
                dve.reciprocal(rs[:, :], rs[:, :]).then_inc(S["rs_set"], 1)
                dve.wait_ge(S["rs_set"], c + 1 + BASE)
                dve.tensor_scalar(y[:, :], y[:, :], mv[:, 0:1], rs[:, 0:1], ALU.subtract, ALU.mult).then_inc(S["y_norm"], 1)

            def beside(c, v, last):
                units(2 * c + 1, v, 1)
                if not last:
                    absolute(2 * c + 2, 0)
                sums(c, v, 0)
                if not last:
                    units(2 * c + 2, 1 - v, 0, lambda: amplitude(c - 1))
                    absolute(2 * c + 3, 1)
                else:
                    amplitude(c - 1)
                sums(c, v, 1)
                post(c - 1)

            absolute(0, 0)
            units(0, 0, 0)
            absolute(1, 1)
            units(1, 0, 1)
            absolute(2, 0)
            sums(0, 0, 0)
            units(2, 1, 0)
            absolute(3, 1)
            dve.wait_ge(post_in, 48)
            sums(0, 0, 1)
            with dve.Fori(0, CH // 2 - 1) as i:
                beside(2 * i + 1, 1, False)
                beside(2 * i + 2, 0, False)
            beside(CH - 1, 1, True)
            amplitude(CH - 1)
            post(CH - 1)

        @block.tensor
        def _(pe):
            def turn_sup(c, v, h):
                pe.wait_ge(S["sup_sq_set"], c + BASE)
                pe.wait_ge(S["prod_set"], 2 * c + h + 1 + BASE)
                for r in range(2):
                    for k in range(DT // 2):
                        at = (h * DT // 2 + k) * P
                        for n in range(N):
                            last = pe.matmul(turn[r][:, at:at + P], z[:, v, h, r, n, k * P:(k + 1) * P], ident[:, :],
                                             start=n == 0, stop=n == N - 1)
                last.then_inc(S["sup_turned"], 1)

            def measure(c):
                pe.wait_ge(S["m_sq_set"], c + BASE)
                pe.wait_ge(S["sup_t_set"], c + 1 + BASE)
                for r in range(2):
                    for x, (a, w) in enumerate(((0, r), (2 - r, 1 - r))):
                        for k in range(DT):
                            last = pe.matmul(mea[r][:, :], sup_t[:, a, k * P:(k + 1) * P], mw[:, w, k * D:(k + 1) * D],
                                             start=x == 0 and k == 0, stop=x == 1 and k == DT - 1)
                last.then_inc(S["meas_done"], 1)
                pe.wait_ge(S["inv_set"], c + BASE)
                pe.wait_ge(S["sup_sq_set"], c + 1 + BASE)
                for k in range(2 * DT):
                    last = pe.matmul(ssp[:, 0:1], sup_sq[:, k // DT, k % DT * P:(k % DT + 1) * P], ones[:, :],
                                     start=k == 0, stop=k == 2 * DT - 1)
                last.then_inc(S["ss_set"], 1)

            def turn_amp(c):
                pe.wait_ge(S["amp_t_set"], c + BASE)
                pe.wait_ge(S["amp_set"], c + 1 + BASE)
                for k in range(DT):
                    last = pe.transpose(ampp[:, k * P:(k + 1) * P], amp[:, k * P:(k + 1) * P], ident[:, :])
                last.then_inc(S["amp_turned"], 1)

            def post(c, before=1):
                pe.wait_ge(S["y_copied"], c + before + BASE)
                pe.wait_ge(S["amp_t_set"], c + 1 + BASE)
                for k in range(DT):
                    last = pe.matmul(postp[:, :], amp_t[:, k * P:(k + 1) * P], pw[:, k * D:(k + 1) * D],
                                     start=k == 0, stop=k == DT - 1)
                last.then_inc(S["post_done"], 1)

            def turn_y(c):
                pe.wait_ge(S["h1_set"], c + 1 + BASE)
                pe.wait_ge(S["y_norm"], c + 1 + BASE)
                for k in range(DT):
                    last = pe.transpose(zp[:, k * P:(k + 1) * P], y[:, k * P:(k + 1) * P], ident[:, :])
                last.then_inc(S["y_turned"], 1)

            def top1(c):
                pe.wait_ge(S["z_t_set"], c + 1 + BASE)
                for t in range(T1):
                    o = zp[:, t * P:(t + 1) * P]
                    for k in range(DT):
                        pe.matmul(o, w1[:, k * D + t * P:k * D + (t + 1) * P], z_t[:, k, :], start=k == 0, stop=False)
                    last = pe.matmul(o, ident[:, :], hx[:, bass.ds(c + 1, 1), t, :].rearrange("p a b -> p (a b)"),
                                     start=False, stop=True)
                last.then_inc(S["h1_done"], 1)

            def top2(c, behind=0):
                pe.wait_ge(S["y_set"], c + behind + 1 + BASE)
                pe.wait_ge(S["h1_set"], c + 2 + BASE)
                for t in range(T2):
                    for k in range(T1):
                        last = pe.matmul(h2p[:, t * P:(t + 1) * P], w2[:, k, t * P:(t + 1) * P], h1[:, k, :],
                                         start=k == 0, stop=k == T1 - 1)
                last.then_inc(S["h2_done"], 1)

            def top3(c):
                pe.wait_ge(S["h2_set"], c + 2 + BASE)
                for k in range(T2):
                    last = pe.matmul(yp, w3[:, k:k + 1], h2[:, k, :], start=k == 0, stop=k == T2 - 1)
                last.then_inc(S["y_done"], 1)

            pe.wait_ge(made, 3)
            pe.wait_ge(meas_in, 32)
            pe.wait_ge(post_in, 48)
            pe.wait_ge(top_in, TOP_IN)
            def beside(c, v):
                measure(c)
                turn_sup(c + 1, 1 - v, 0)
                top1(c - 1)
                turn_amp(c)
                top2(c - 1)
                top3(c - 1)
                post(c)
                turn_sup(c + 1, 1 - v, 1)
                turn_y(c)

            turn_sup(0, 0, 0)
            turn_sup(0, 0, 1)
            with pe.Fori(0, CH // 2 - 1) as i:
                beside(2 * i, 0)
                beside(2 * i + 1, 1)
            beside(CH - 2, 0)
            measure(CH - 1)
            top1(CH - 2)
            turn_amp(CH - 1)
            post(CH - 1, 0)
            top2(CH - 2, 1)
            turn_y(CH - 1)
            top3(CH - 2)
            top1(CH - 1)
            top2(CH - 1)
            top3(CH - 1)


def program(nc, t, out):
    s_dram = nc.dram_tensor("s_scratch", [2, 2, CH, P, DT * N, P], F32).ap()
    hx_dram = nc.dram_tensor("hx_scratch", [HALVES, P, 512 // P, HB], F32).ap()
    o_dram = nc.dram_tensor("o_scratch", [2, 2, CH, P, 2, N * P], F32).ap()
    z_dram = nc.dram_tensor("z_scratch", [CH, P, 2, N, D], F32).ap()
    with ExitStack() as sems:
        st = sems.enter_context(nc.sbuf_tensor("strengths", [P, CH, N, N], F32))
        encoders(nc, sems, t["x_t"], t["enc_w"], t["enc_bias"], t["ln_gb"], s_dram, hx_dram)
        attention(nc, sems, t["qkv_w"], t["qk_bias"], t["v_bias"], t["row_ids"], [t[f"table_{n}"] for n in range(N)], st,
                  s_dram, o_dram)
        interact(nc, sems, t["wo_w"], t["wo_bias"], t["int_w"], o_dram, z_dram)
        finish(nc, sems, st, t["meas_w"], t["post_w"], t["post_b"], t["post_gb"],
               t["top1_w"], t["top2_w"], t["top3_w"], t["top2_b"], z_dram, hx_dram, out)



def lay_out(inp, np):
    def g(name):
        return np.asarray(inp[name])

    def rec(name):
        return g("L0_rec_" + name)

    def pieces(w):
        o, i = w.shape
        return w.reshape(o // P, P, 2, i // P // 2, P).transpose(0, 2, 4, 3, 1).reshape(o // P * 2, P, i // 2)

    def tokens_inner(w):
        return w.reshape((N, DT, P) + w.shape[1:]).swapaxes(0, 1).reshape(w.shape)

    def by_row(w):
        return w.reshape(DT, P, w.shape[1]).transpose(1, 0, 2).reshape(P, DT * w.shape[1])

    def columns(v):
        return v.reshape(-1, P).T

    out = {
        "x_t": g("r_x").reshape(HALVES, HB, KT // 2, 2, P).transpose(0, 2, 4, 3, 1).reshape(HALVES, KT // 2, P, 2 * HB),
        "enc_w": np.concatenate([pieces(w) for w in (
            rec("er_W1"), rec("ei_W1"), g("W_top1")[OUT:].T, tokens_inner(rec("er_W2")), tokens_inner(rec("ei_W2")))]),
        "enc_bias": columns(np.concatenate([rec("er_b1"), rec("ei_b1"), g("b_top1"),
                                            tokens_inner(rec("er_b2")), tokens_inner(rec("ei_b2"))])),
        "ln_gb": np.stack([rec(n) for n in ("er_g1", "er_be1", "ei_g1", "ei_be1")]).reshape(2, 2, KT, P).transpose(3, 0, 1, 2),
        "qkv_w": np.stack([by_row(rec("W" + n).T) for n in ("q_r", "k_r", "q_i", "k_i", "v_r", "v_i")]),
        "qk_bias": np.stack([rec("b" + n) for n in ("q_r", "k_r", "q_i", "k_i")]).reshape(4, DT, P).transpose(2, 0, 1),
        "v_bias": np.stack([rec("bv_r"), rec("bv_i")]),
        "wo_w": np.stack([by_row(rec("Wo_r").T), by_row(rec("Wo_i").T)]),
        "wo_bias": np.stack([rec("bo_r"), rec("bo_i")]).reshape(2, DT, P).transpose(2, 0, 1),
        "int_w": np.stack([np.stack([by_row(w.T) for w in rec(n)]) for n in ("int_Wr", "int_Wi")]),
        "row_ids": g("ids").reshape(CH, P, N).transpose(1, 0, 2),
        "meas_w": np.stack([by_row(rec("meas_Mr").T), by_row(rec("meas_Mi").T)]),
        "post_w": by_row(rec("post_W").T),
        "post_b": rec("post_b")[None],
        "post_gb": np.stack([columns(rec("post_g")), columns(rec("post_be"))], axis=1),
        "top1_w": by_row(g("W_top1")[:OUT]),
        "top2_w": g("W_top2").reshape(DT, P, 256).transpose(1, 0, 2),
        "top3_w": columns(g("W_top3")),
        "top2_b": columns(g("b_top2")),
    }
    out.update({f"table_{n}": g(f"tbl_{n}") for n in range(N)})
    return {k: np.ascontiguousarray(v) for k, v in out.items()}


def kernel(**inputs):
    import numpy as np
    import concourse.bacc as bacc
    from concourse.bass_utils import run_bass_kernel_spmd

    nc = bacc.Bacc("TRN2", target_bir_lowering=False, num_devices=1)
    arrays = {f"in_{k}": v for k, v in lay_out(inputs, np).items()}
    t = {k[3:]: nc.dram_tensor(k, v.shape, mybir.dt.from_np(v.dtype), kind="ExternalInput").ap() for k, v in arrays.items()}
    out = nc.dram_tensor("out_0_dram", (B, 1), F32, kind="ExternalOutput").ap()
    program(nc, t, out)
    r = run_bass_kernel_spmd(nc, [arrays], core_ids=[0])
    return r.results[0]["out_0_dram"]
```
